# Optimizing a Trainium2 kernel written in Bass

```python
import numpy as np
import jax
import jax.numpy as jnp

def _softmax(x, axis=-1):
    return jax.nn.softmax(x, axis=axis)

def _gelu(x):
    return jax.nn.gelu(x, approximate=True)

def _silu(x):
    return jax.nn.silu(x)

def _sigmoid(x):
    return jax.nn.sigmoid(x)

def _layernorm(x, axis=-1, eps=1e-05):
    m = jnp.mean(x, axis=axis, keepdims=True)
    v = jnp.var(x, axis=axis, keepdims=True)
    return (x - m) / jnp.sqrt(v + eps)

def _scatter_add(tgt, idx, src, axis=0):
    return tgt.at[idx].add(src)

def _segment_sum(src, seg, n):
    return jax.ops.segment_sum(src, seg, n)
kernel_name = 'mk_adaln_d1_jaxref_r4_7dadcc'

def setup_inputs(seed: int=0):
    np.random.seed(seed)
    _w = jnp.asarray

    def _L0_attn_setup():
        import jax, jax.numpy as jnp
        import numpy as np
        import math
        B, T, H = (2, 512, 512)
        NH = 16
        HS = H // NH
        ROPE_BASE = 10000.0

        def apply_rope(x):
            hs = x.shape[-1]
            t = jnp.arange(x.shape[2], dtype=jnp.float32)
            inv_freq = 1.0 / ROPE_BASE ** (jnp.arange(0, hs, 2, dtype=jnp.float32) / hs)
            ang = t[:, None] * inv_freq[None, :]
            cos, sin = (jnp.cos(ang), jnp.sin(ang))
            x1, x2 = (x[..., 0::2], x[..., 1::2])
            out_even = x1 * cos - x2 * sin
            out_odd = x1 * sin + x2 * cos
            return jnp.stack([out_even, out_odd], axis=-1).reshape(x.shape)
        key = jax.random.key(seed)
        ks = jax.random.split(key, 9)
        s = 1.0 / math.sqrt(H)
        inp = {'x': jax.random.normal(ks[0], (B, T, H), dtype=jnp.float32)}
        for i, name in enumerate(['q', 'k', 'v', 'o']):
            inp[f'W{name}'] = jax.random.normal(ks[1 + i], (H, H), dtype=jnp.float32) * s
            inp[f'b{name}'] = jax.random.normal(ks[5 + i], (H,), dtype=jnp.float32) * 0.01
        return inp
    _L0_attn_in = _L0_attn_setup()

    def _L0_ffn_setup():
        import jax, jax.numpy as jnp
        import numpy as np
        HIDDEN = 512
        INTER = 2048
        SCALE = 64.0

        def fwht(x):
            orig_shape = x.shape
            n = orig_shape[-1]
            x = x.reshape(-1, n)
            h = 1
            while h < n:
                x = x.reshape(-1, n // (2 * h), 2, h)
                a, b = (x[:, :, 0, :], x[:, :, 1, :])
                x = jnp.stack([a + b, a - b], axis=2).reshape(-1, n)
                h *= 2
            return (x / jnp.sqrt(jnp.asarray(n, x.dtype))).reshape(orig_shape)
        key = jax.random.key(seed)
        ks = jax.random.split(key, 8)
        inp = jax.random.normal(ks[0], (4, 512, HIDDEN), dtype=jnp.float32)
        SU_ug = jnp.where(jax.random.bernoulli(ks[1], 0.5, (HIDDEN,)), 1.0, -1.0).astype(jnp.float32)
        SU_dp = jnp.where(jax.random.bernoulli(ks[2], 0.5, (INTER,)), 1.0, -1.0).astype(jnp.float32)
        Wscale_ug = jax.random.uniform(ks[3], (2 * INTER,), jnp.float32, 0.5, 1.5)
        Wscale_dp = jax.random.uniform(ks[4], (HIDDEN,), jnp.float32, 0.5, 1.5)
        W_up = jax.random.normal(ks[5], (INTER, HIDDEN), dtype=jnp.float32) * 0.02
        W_gate = jax.random.normal(ks[6], (INTER, HIDDEN), dtype=jnp.float32) * 0.02
        W_down = jax.random.normal(ks[7], (HIDDEN, INTER), dtype=jnp.float32) * 0.02
        return {'input': inp, 'SU_ug': SU_ug, 'SU_dp': SU_dp, 'Wscale_ug': Wscale_ug, 'Wscale_dp': Wscale_dp, 'W_up': W_up, 'W_gate': W_gate, 'W_down': W_down}
    _L0_ffn_in = _L0_ffn_setup()
    _L0_c = _w((lambda *s: np.random.randn(*s).astype(np.float32) * 0.05)(4, 512))
    _L0_wmod = _w((lambda *s: np.random.randn(*s).astype(np.float32) * 0.05)(512, 6 * 512) * 512 ** (-0.5))
    _d = {'L0_attn_x': _L0_attn_in['x'], 'L0_attn_Wq': _L0_attn_in['Wq'], 'L0_attn_bq': _L0_attn_in['bq'], 'L0_attn_Wk': _L0_attn_in['Wk'], 'L0_attn_bk': _L0_attn_in['bk'], 'L0_attn_Wv': _L0_attn_in['Wv'], 'L0_attn_bv': _L0_attn_in['bv'], 'L0_attn_Wo': _L0_attn_in['Wo'], 'L0_attn_bo': _L0_attn_in['bo'], 'L0_ffn_SU_ug': _L0_ffn_in['SU_ug'], 'L0_ffn_SU_dp': _L0_ffn_in['SU_dp'], 'L0_ffn_Wscale_ug': _L0_ffn_in['Wscale_ug'], 'L0_ffn_Wscale_dp': _L0_ffn_in['Wscale_dp'], 'L0_ffn_W_up': _L0_ffn_in['W_up'], 'L0_ffn_W_gate': _L0_ffn_in['W_gate'], 'L0_ffn_W_down': _L0_ffn_in['W_down'], 'L0_c': _L0_c, 'L0_wmod': _L0_wmod}
    _x0 = _d['L0_attn_x']
    _d['L0_attn_x'] = jax.random.normal(jax.random.fold_in(jax.random.key(seed), 1), (4, 512, 512), dtype=_x0.dtype)
    del _x0
    return _d

def reference(L0_attn_x, L0_attn_Wq, L0_attn_bq, L0_attn_Wk, L0_attn_bk, L0_attn_Wv, L0_attn_bv, L0_attn_Wo, L0_attn_bo, L0_ffn_SU_ug, L0_ffn_SU_dp, L0_ffn_Wscale_ug, L0_ffn_Wscale_dp, L0_ffn_W_up, L0_ffn_W_gate, L0_ffn_W_down, L0_c, L0_wmod):

    def _L0_attn_ref(x, Wq, bq, Wk, bk, Wv, bv, Wo, bo):
        import jax, jax.numpy as jnp
        import numpy as np
        import math
        B, T, H = (2, 512, 512)
        NH = 16
        HS = H // NH
        ROPE_BASE = 10000.0

        def apply_rope(x):
            hs = x.shape[-1]
            t = jnp.arange(x.shape[2], dtype=jnp.float32)
            inv_freq = 1.0 / ROPE_BASE ** (jnp.arange(0, hs, 2, dtype=jnp.float32) / hs)
            ang = t[:, None] * inv_freq[None, :]
            cos, sin = (jnp.cos(ang), jnp.sin(ang))
            x1, x2 = (x[..., 0::2], x[..., 1::2])
            out_even = x1 * cos - x2 * sin
            out_odd = x1 * sin + x2 * cos
            return jnp.stack([out_even, out_odd], axis=-1).reshape(x.shape)
        Bsz, Tl, h = x.shape
        q = (x @ Wq + bq).reshape(Bsz, Tl, NH, HS).transpose(0, 2, 1, 3)
        k = (x @ Wk + bk).reshape(Bsz, Tl, NH, HS).transpose(0, 2, 1, 3)
        v = (x @ Wv + bv).reshape(Bsz, Tl, NH, HS).transpose(0, 2, 1, 3)
        q = apply_rope(q)
        k = apply_rope(k)
        scale = 1.0 / math.sqrt(HS)
        attn = jnp.einsum('bhqd,bhkd->bhqk', q, k) * scale
        attn = jax.nn.softmax(attn, axis=-1)
        tril = jnp.tril(jnp.ones((Tl, Tl), dtype=attn.dtype))
        attn = attn * tril[None, None, :, :]
        out = jnp.einsum('bhqk,bhkd->bhqd', attn, v)
        o = out.transpose(0, 2, 1, 3).reshape(Bsz, Tl, h)
        return o @ Wo + bo

    def _L0_ffn_ref(input, SU_ug, SU_dp, Wscale_ug, Wscale_dp, W_up, W_gate, W_down):
        import jax, jax.numpy as jnp
        import numpy as np
        HIDDEN = 512
        INTER = 2048
        SCALE = 64.0

        def fwht(x):
            orig_shape = x.shape
            n = orig_shape[-1]
            x = x.reshape(-1, n)
            h = 1
            while h < n:
                x = x.reshape(-1, n // (2 * h), 2, h)
                a, b = (x[:, :, 0, :], x[:, :, 1, :])
                x = jnp.stack([a + b, a - b], axis=2).reshape(-1, n)
                h *= 2
            return (x / jnp.sqrt(jnp.asarray(n, x.dtype))).reshape(orig_shape)
        n = SU_ug.shape[0]
        x = input.reshape(-1, n)
        x = fwht(x * SU_ug) / SCALE
        x_up = x @ W_up.T * (Wscale_ug[:INTER] * SCALE)
        x_gate = x @ W_gate.T * (Wscale_ug[INTER:] * SCALE)
        x = jax.nn.silu(x_gate) * x_up
        x = fwht(x * SU_dp) / SCALE
        x = x @ W_down.T * (Wscale_dp * SCALE)
        return x.reshape(input.shape)
    x = L0_attn_x
    mod = (_silu(L0_c) @ L0_wmod).reshape(L0_c.shape[0], 6, 1, -1)
    sa, ca, ga, sb, cb, gb = (mod[:, 0], mod[:, 1], mod[:, 2], mod[:, 3], mod[:, 4], mod[:, 5])
    ga = (2 * (ga >= 0) - 1) * jnp.maximum(jnp.abs(ga), 0.25)
    gb = (2 * (gb >= 0) - 1) * jnp.maximum(jnp.abs(gb), 0.25)
    h = _layernorm(x, axis=-1) * (1 + ca) + sa
    x = x + ga * _L0_attn_ref(h, L0_attn_Wq, L0_attn_bq, L0_attn_Wk, L0_attn_bk, L0_attn_Wv, L0_attn_bv, L0_attn_Wo, L0_attn_bo)
    h = _layernorm(x, axis=-1) * (1 + cb) + sb
    x = x + gb * _L0_ffn_ref(h, L0_ffn_SU_ug, L0_ffn_SU_dp, L0_ffn_Wscale_ug, L0_ffn_Wscale_dp, L0_ffn_W_up, L0_ffn_W_gate, L0_ffn_W_down)
    return x

_drawn_inputs = setup_inputs


def setup_inputs(seed=0):
    import zlib

    import numpy as np

    out = dict(_drawn_inputs(seed))
    spreads = {}
    factors = {'L0_attn_Wq': 5.162,
     'L0_attn_bq': 8.0,
     'L0_attn_Wk': 5.137,
     'L0_attn_bk': 8.0,
     'L0_attn_Wv': 4.218,
     'L0_attn_bv': 8.0,
     'L0_attn_Wo': 4.186,
     'L0_attn_bo': 39.745,
     'L0_ffn_Wscale_ug': 5.067,
     'L0_ffn_Wscale_dp': 7.46}
    for name, (base, spread) in spreads.items():
        noise = np.random.default_rng([zlib.crc32(name.encode()), seed]).standard_normal(out[name].shape)
        drawn = base * np.exp(spread * noise) if base else spread * noise
        out[name] = jnp.asarray(drawn.astype(out[name].dtype))
    for name, factor in factors.items():
        out[name] = (out[name] * factor).astype(out[name].dtype)
    return out
```

```python
from contextlib import ExitStack

import numpy as np

import concourse.bass as bass
from concourse import mybir

F32 = mybir.dt.float32
F32R = mybir.dt.float32r
ALU = mybir.AluOpType
ACT = mybir.ActivationFunctionType
AX = mybir.AxisListType

P = 128
B = 4
T = 512
H = 512
NT = T // P
KB = H // P
NH = 16
HS = H // NH
HG = P // HS
G = NH // HG
U = HG * NT
INTER = 2048
IB = INTER // P
NQ = 4
QB = IB // NQ
EPS = 1e-5
ROPE_BASE = 10000.0

R_BQ, R_BK, R_WUG, R_SUU, R_SUD, R_C, R_N = 0, 4, 8, 40, 44, 60, 76

PT_STEP = 3
PT_BLOCKS = PT_STEP * (NT - 1) + NT

GM_FIRST = KB + 2
VO_PER_BATCH = NT + G


def gm_use(b, kind, g, kb=0):
    per_batch = 3 * G + KB
    at = 3 * g + (KB if g > G - 2 else 0)
    off = {"q": at, "k": at + 1, "lt": at + 2 + kb, "r": at + 2 + (KB if g == G - 2 else 0)}[kind]
    return b * per_batch + GM_FIRST + off


def gm_use_last(b, kind, g):
    per_batch = 3 * G + KB
    off = {"q": 3 * g, "k": 3 * g + 1, "r": 3 * g + (2 if g < G - 1 else 0)}[kind]
    return b * per_batch + GM_FIRST + off


def wait_apart(engine, passed, *waits):
    for semaphore, value in waits:
        engine.wait_ge(semaphore, value)
    engine.sem_inc(passed, 1)


def rope_tables(scale):
    inv = (np.float32(1.0) / np.float32(ROPE_BASE) ** (np.arange(0, HS, 2, dtype=np.float32) / np.float32(HS)))
    ang = np.arange(T, dtype=np.float32)[None, :] * inv.astype(np.float32)[:, None]
    cos, sin = np.cos(ang), np.sin(ang)
    c = np.repeat(cos, 2, axis=0)
    s = np.stack([-sin, sin], axis=1).reshape(HS, T)
    return [np.ascontiguousarray(np.tile(a, (HG, 1)) * np.float32(scale)).astype(np.float32) for a in (c, s)]


def hadamard(n):
    h = np.ones((1, 1), np.float32)
    while h.shape[0] < n:
        h = np.block([[h, h], [h, -h]])
    return h.astype(np.float32)


def build_program(nc, a, stop=4):
    ctx = ExitStack()

    def sem(name):
        return ctx.enter_context(nc.semaphore(name))

    def dram(name, shape):
        return nc.dram_tensor(name, shape, F32, kind="Internal").ap()

    with ctx:
        mod_rows_d = dram("mod_rows_d", (3, B, H))
        attn_d = dram("attn_d", (B, G, P, T))
        x1_d = dram("x1_d", (B, NT, P, H))
        wd_d = dram("wd_d", (KB, P, INTER))

        def keep(name, shape, dt=F32):
            return ctx.enter_context(nc.sbuf_tensor(name, shape, dt))

        ident = keep("ident", [P, P])
        had = keep("had", [P, P])
        cols = keep("cols", [P, R_N])
        modc = keep("modc", [P, 4, KB, B])
        ffn_scale = keep("ffn_scale", [P, 2, IB])
        neg_half = keep("neg_half", [P, NT])
        bank = [ctx.enter_context(nc.psum_tensor(f"bank{i}", [P, 512], F32)) for i in range(8)]

        stage_setup(nc, a, sem, bank, dict(
            ident=ident, had=had, cols=cols, modc=modc, ffn_scale=ffn_scale, neg_half=neg_half,
            mod_rows_d=mod_rows_d, wd_d=wd_d))
        if stop >= 2:
            stage_attention(nc, a, sem, bank, dict(
                ident=ident, cols=cols, modc=modc, neg_half=neg_half, attn_d=attn_d))
        if stop >= 3:
            with nc.sbuf_tensor("h2_hi", [P, KB, B * T], F32R) as h2_hi, \
                    nc.sbuf_tensor("h2_lo", [P, KB, B * T], F32R) as h2_lo:
                stage_project(nc, a, sem, bank, dict(
                    ident=ident, had=had, cols=cols, modc=modc, neg_half=neg_half, attn_d=attn_d,
                    mod_rows_d=mod_rows_d, x1_d=x1_d, h2_hi=h2_hi, h2_lo=h2_lo))
                if stop >= 4:
                    stage_ffn(nc, a, sem, bank, dict(
                        ident=ident, had=had, ffn_scale=ffn_scale, x1_d=x1_d, wd_d=wd_d,
                        mod_rows_d=mod_rows_d, h2_hi=h2_hi, h2_lo=h2_lo))


def stage_setup(nc, a, sem, bank, t):
    ctx = ExitStack()
    with ctx:
        def sb(name, shape, dt=F32):
            return ctx.enter_context(nc.sbuf_tensor(name, shape, dt))

        rows = sb("rows", [P, P])
        silu_c = sb("silu_c", [P, KB, B])
        wmod = sb("wmod", [P, KB, 6 * H])
        gate_bias = sb("gate_bias", [B, 2, H])
        gate = sb("gate", [B, 2, H])
        gate_sign = sb("gate_sign", [B, 2, H])
        gate_abs = sb("gate_abs", [B, 2, H])
        gate_out = sb("gate_out", [B, 3, H])
        wdn = sb("wdn", [P, 2, INTER])
        wdm = sb("wdm", [P, 2, INTER])

        rows_loaded, consts_loaded, wmod_loaded = sem("rows_loaded"), sem("consts_loaded"), sem("wmod_loaded")
        gbias_loaded = sem("gbias_loaded")
        wd_loaded = [sem(f"wd_loaded{i}") for i in range(2)]
        wd_stored = [sem(f"wd_stored{i}") for i in range(2)]
        cols_psum, cols_ready, silu_ready = sem("cols_psum"), sem("cols_ready"), sem("silu_ready")
        modc_psum, gate_psum = sem("modc_psum"), sem("gate_psum")
        vec_chain, gates_ready, gates_stored = sem("vec_chain"), sem("gates_ready"), sem("gates_stored")
        butterfly = sem("butterfly")
        block = ctx.enter_context(nc.Block())

        @block.sync
        def _(sp):
            sp.dma_start(t["ident"][:], a["ident"]).then_inc(consts_loaded, 16)
            for at, name in ((R_BQ, "L0_attn_bq"), (R_BK, "L0_attn_bk"), (R_WUG, "L0_ffn_Wscale_ug"),
                             (R_SUU, "L0_ffn_SU_ug"), (R_SUD, "L0_ffn_SU_dp")):
                n = a[name].shape[0] // P
                sp.dma_start(rows[at:at + n, :], a[name].rearrange("(r p) -> r p", p=P)).then_inc(rows_loaded, 16)
            for kb in range(KB):
                sp.dma_start(rows[R_C + kb * B:R_C + (kb + 1) * B, :],
                             a["L0_c"][:, kb * P:(kb + 1) * P]).then_inc(rows_loaded, 16)
            for kb in range(KB):
                sp.dma_start(wmod[:, kb, :], a["L0_wmod"][kb * P:(kb + 1) * P, :]).then_inc(wmod_loaded, 16)
            sp.dma_start(t["had"][:], a["had"]).then_inc(consts_loaded, 16)
            sp.dma_start(gate_bias[:, 0, :], a["L0_attn_bo"].partition_broadcast(B)).then_inc(gbias_loaded, 16)
            sp.dma_start(gate_bias[:, 1, :], a["L0_ffn_Wscale_dp"].partition_broadcast(B)).then_inc(gbias_loaded, 16)
            sp.wait_ge(gates_ready, 1)
            for i in range(3):
                sp.dma_start(t["mod_rows_d"][i], gate_out[:, i, :]).then_inc(gates_stored, 16)
            sp.wait_ge(gates_stored, 48)
            sp.wait_ge(consts_loaded, 32)

        @block.scalar
        def _(act):
            for i in range(KB):
                if i >= 2:
                    act.wait_ge(butterfly, 8 * (i - 1))
                act.dma_start(wdn[:, i % 2, :], a["L0_ffn_W_down"][i * P:(i + 1) * P, :]).then_inc(wd_loaded[i % 2], 16)
                if i == 1:
                    act.wait_ge(cols_psum, 1)
                    nc.scalar.activation(silu_c[:, :, :].rearrange("p k b -> p (k b)"),
                                         bank[0][:, R_C:R_N], ACT.Silu).then_inc(silu_ready, 1)
                if i >= 1:
                    act.wait_ge(butterfly, 8 * i)
                    act.dma_start(t["wd_d"][i - 1], wdn[:, (i - 1) % 2, :]).then_inc(wd_stored[(i - 1) % 2], 16)
                    if i < KB - 1:
                        act.wait_ge(wd_stored[(i - 1) % 2], 16 * ((i - 1) // 2 + 1))
            act.wait_ge(butterfly, 8 * KB)
            act.dma_start(t["wd_d"][KB - 1], wdn[:, (KB - 1) % 2, :]).then_inc(wd_stored[(KB - 1) % 2], 16)
            for i in range(2):
                act.wait_ge(wd_stored[i], 16 * (KB // 2))

        @block.tensor
        def _(pe):
            pe.wait_ge(consts_loaded, 16)
            pe.wait_ge(rows_loaded, 16 * (5 + KB))
            nc.tensor.transpose(bank[0][:, 0:R_N], rows[0:R_N, :], t["ident"][0:R_N, 0:R_N]).then_inc(cols_psum, 1)
            pe.wait_ge(silu_ready, 1)
            pe.wait_ge(wmod_loaded, 16 * KB)
            for n, chunk in enumerate((0, 1, 3, 4)):
                for mb in range(KB):
                    for kb in range(KB):
                        last = nc.tensor.matmul(
                            bank[1][:, (n * KB + mb) * B:(n * KB + mb + 1) * B],
                            wmod[:, kb, chunk * H + mb * P:chunk * H + (mb + 1) * P], silu_c[:, kb, :],
                            start=kb == 0, stop=kb == KB - 1)
            last.then_inc(modc_psum, 1)
            for n, chunk in enumerate((2, 5)):
                for kb in range(KB):
                    last = nc.tensor.matmul(bank[2 + n][0:B, :], silu_c[:, kb, :],
                                            wmod[:, kb, chunk * H:(chunk + 1) * H],
                                            start=kb == 0, stop=kb == KB - 1)
                last.then_inc(gate_psum, 1)

        @block.vector
        def _(dve):
            chain = [0]

            def link(ins):
                chain[0] += 1
                ins.then_inc(vec_chain, 1)
                dve.wait_ge(vec_chain, chain[0])

            nc.vector.memset(t["neg_half"][:], -0.5)
            dve.wait_ge(cols_psum, 1)
            dve.wait_ge(silu_ready, 1)
            cols = t["cols"]
            link(nc.vector.tensor_copy(cols[:], bank[0][:, 0:R_N]))
            fs = t["ffn_scale"]
            link(nc.vector.tensor_scalar(fs[:, :, :], cols[:, R_WUG:R_WUG + 2 * IB].rearrange("p (n i) -> p n i", n=2),
                                         float(H) ** -0.5, None, ALU.mult))
            link(nc.vector.tensor_tensor(fs[:, 0, :], fs[:, 0, :], cols[:, R_SUD:R_SUD + IB], ALU.mult))
            dve.wait_ge(modc_psum, 1)
            modc = t["modc"]
            mp = bank[1][:, 0:4 * KB * B].rearrange("p (n k b) -> p n k b", n=4, k=KB)
            link(nc.vector.tensor_copy(modc[:, 0, :, :], mp[:, 0, :, :]))
            link(nc.vector.tensor_scalar(modc[:, 1, :, :], mp[:, 1, :, :], 1.0, None, ALU.add))
            link(nc.vector.tensor_copy(modc[:, 2, :, :], mp[:, 2, :, :]))
            link(nc.vector.tensor_scalar(modc[:, 3, :, :], mp[:, 3, :, :], 1.0, None, ALU.add))
            for n in (2, 3):
                for kb in range(KB):
                    link(nc.vector.tensor_scalar(modc[:, n, kb, :], modc[:, n, kb, :],
                                                 cols[:, R_SUU + kb:R_SUU + kb + 1], None, ALU.mult))
            dve.wait_ge(gate_psum, 2)
            for n in range(2):
                link(nc.vector.tensor_copy(gate[:, n, :], bank[2 + n][0:B, :]))
            link(nc.vector.tensor_scalar(gate_sign[:], gate[:], 0.0, 2.0, ALU.is_ge, ALU.mult))
            link(nc.vector.scalar_tensor_tensor(out=gate_abs[:], in0=gate[:], scalar=-1.0, in1=gate[:],
                                                op0=ALU.mult, op1=ALU.max))
            link(nc.vector.tensor_scalar(gate_abs[:], gate_abs[:], 0.25, None, ALU.max))
            link(nc.vector.scalar_tensor_tensor(out=gate[:], in0=gate_sign[:], scalar=-1.0, in1=gate_abs[:],
                                                op0=ALU.add, op1=ALU.mult))
            dve.wait_ge(gbias_loaded, 32)
            link(nc.vector.tensor_copy(gate_out[:, 0, :], gate[:, 0, :]))
            link(nc.vector.tensor_tensor(gate_out[:, 1, :], gate[:, 0, :], gate_bias[:, 0, :], ALU.mult))
            nc.vector.scalar_tensor_tensor(out=gate_out[:, 2, :], in0=gate[:, 1, :], scalar=float(INTER) ** -0.5,
                                           in1=gate_bias[:, 1, :], op0=ALU.mult, op1=ALU.mult).then_inc(gates_ready, 1)
            for i in range(KB):
                dve.wait_ge(wd_loaded[i % 2], 16 * (i // 2 + 1))
                src, dst = wdn[:, i % 2, :], wdm[:, i % 2, :]
                for s in range(4):
                    if i or s:
                        dve.wait_ge(butterfly, 8 * i + 2 * s)
                    n = P << s
                    v = src.rearrange("p (m a n) -> p m a n", a=2, n=n)
                    w = dst.rearrange("p (m a n) -> p m a n", a=2, n=n)
                    nc.vector.tensor_tensor(w[:, :, 0, :], v[:, :, 0, :], v[:, :, 1, :], ALU.add).then_inc(butterfly, 1)
                    nc.vector.tensor_tensor(w[:, :, 1, :], v[:, :, 0, :], v[:, :, 1, :], ALU.subtract).then_inc(butterfly, 1)
                    src, dst = dst, src


def stage_attention(nc, a, sem, bank, t):
    ctx = ExitStack()
    with ctx:
        def sb(name, shape, dt=F32):
            return ctx.enter_context(nc.sbuf_tensor(name, shape, dt))

        w_hi = [sb(f"w{n}_hi", [P, KB, H], F32R) for n in "qkv"]
        w_lo = [sb(f"w{n}_lo", [P, KB, H], F32R) for n in "qkv"]
        rope = [sb(f"rope_{n}", [P, T]) for n in ("qcos", "qsin", "kcos", "ksin")]
        bv_rows = sb("bv_rows", [P, H])
        xt = sb("xt", [P, NT, H])
        stats = sb("stats", [P, NT, 6])
        mean_var = sb("mean_var", [P, NT, 2])
        var_eps = sb("var_eps", [P, NT])
        rstd = sb("rstd", [P, NT])
        ht_f = sb("ht_f", [P, 2, T])
        ht_hi = sb("ht_hi", [P, KB, T], F32R)
        ht_lo = sb("ht_lo", [P, KB, T], F32R)
        qk_raw = sb("qk_raw", [P, 2, T])
        qk_swap = sb("qk_swap", [P, 2, T])
        qk_rot = sb("qk_rot", [P, 2, T])
        qk_hi = sb("qk_hi", [P, 2, T], F32R)
        qk_lo = sb("qk_lo", [P, 2, T], F32R)
        q_stack = sb("q_stack", [P, 2, HG, T], F32R)
        k_stack = sb("k_stack", [P, 2, HG, T], F32R)
        v_sb = sb("v_sb", [P, NT, H])
        probs = sb("probs", [P, 4, T])
        probs_t = sb("probs_t", [P, HG, PT_BLOCKS, P])
        neg_max = sb("neg_max", [P, 2, U])
        row_sum = sb("row_sum", [P, 2, U])
        row_inv = sb("row_inv", [P, U])
        inv_wide = sb("inv_wide", [P, NT, HG, HS])
        inv_t = sb("inv_t", [P, T])
        attn_out = sb("attn_out", [P, 2, T])

        s_bank, pt_bank, gm, vo = bank[0:4], bank[4:6], bank[6], bank[7]

        names = ("w_loaded0 w_loaded1 w_loaded2 tables_loaded w_split_hi w_split_lo x_loaded stats_done aggr_done "
                 "vareps_done rstd_done normed gm_done gm_free ht_hi_done ht_split vo_done vo_free swapped "
                 "sin_done cos_done rotated qk_hi_done qk_split stacked0 stacked1 sc_done neg_max_done "
                 "exp_done masked pt_psum pt_done inv_done wide_done attn_stored0 attn_stored1 "
                 "act_passed dve_passed pool_passed")
        s = {n: sem("b_" + n) for n in names.split()}
        block = ctx.enter_context(nc.Block())
        swap_pairs = [j ^ 1 for j in range(32)]
        w_raw = (probs[:], v_sb[:], probs_t[:].rearrange("p h m n -> p (h m n)")[:, 0:KB * H].rearrange(
            "p (k n) -> p k n", k=KB))
        last_b = B - 1
        x_by_batch = a["L0_attn_x"].rearrange("b (t p) h -> b p t h", p=P)

        def x_of(b):
            return x_by_batch[b]

        def use(b, kind, g, kb=0):
            return gm_use_last(b, kind, g) if isinstance(b, int) and b == last_b else gm_use(b, kind, g, kb)

        @block.sync
        def _(sp):
            sp.sem_inc(s["attn_stored0"], 1)
            sp.sem_inc(s["attn_stored1"], 1)
            sp.dma_start(xt[:], x_of(0)).then_inc(s["x_loaded"], 16)
            for w, name in enumerate(("L0_attn_Wq", "L0_attn_Wk", "L0_attn_Wv")):
                sp.dma_start(w_raw[w], a[name].rearrange("(k p) n -> p k n", p=P)).then_inc(s[f"w_loaded{w}"], 16)
            for n, r in zip(("qcos", "qsin", "kcos", "ksin"), rope):
                sp.dma_start(r[:], a[n]).then_inc(s["tables_loaded"], 16)
            sp.dma_start(bv_rows[:], a["L0_attn_bv"].partition_broadcast(P)).then_inc(s["tables_loaded"], 16)

            def send(m, after_sc, slot, which):
                sp.wait_ge(s["qk_split"], m + 3)
                if after_sc is not None:
                    sp.wait_ge(s["sc_done"], after_sc)
                dst = (q_stack, k_stack)[which]
                order = ((qk_hi, qk_hi, qk_lo), (qk_hi, qk_lo, qk_hi))[which]
                for r, src in enumerate(order):
                    for h in range(HG):
                        sp.dma_start(dst[r * HS:(r + 1) * HS, slot, h, :].bitcast(F32),
                                     src[h * HS:(h + 1) * HS, which, :].bitcast(F32)).then_inc(s[f"stacked{slot}"], 16)

            send(0, None, 0, 0)
            send(1, None, 0, 1)

            def batch(b, last):
                if not last:
                    sp.wait_ge(s["gm_done"], b * (3 * G + KB) + KB)
                    sp.dma_start(xt[:], x_of(b + 1)).then_inc(s["x_loaded"], 16)
                for g in range(G):
                    if not (last and g == G - 1):
                        n = (b * G) + g + 1
                        for which in range(2):
                            send(n * 2 + which, (n - 1) * U + 1, (g + 1) % 2, which)
                    sp.wait_ge(s["vo_free"], b * VO_PER_BATCH + NT + g + 2)
                    sp.dma_start(t["attn_d"][b, g], attn_out[:, g % 2, :]).then_inc(s[f"attn_stored{g % 2}"], 16)

            with sp.Fori(0, last_b) as b:
                batch(b, False)
            batch(last_b, True)
            for i in range(2):
                sp.wait_ge(s[f"attn_stored{i}"], 16 * B * G // 2 + 1)

        @block.tensor
        def _(pe):
            def project(w, g, kbs):
                cs = slice(g * P, (g + 1) * P)
                for kb in kbs:
                    for wt, ht in ((w_hi[w], ht_hi), (w_hi[w], ht_lo), (w_lo[w], ht_hi)):
                        first = kb == 0 and wt is w_hi[w] and ht is ht_hi
                        end = kb == KB - 1 and wt is w_lo[w]
                        ins = nc.tensor.matmul(gm[:], wt[:, kb, cs], ht[:, kb, :], start=first, stop=end)
                return ins

            def norm_transposes(kb):
                for tt in range(NT):
                    ins = nc.tensor.transpose(gm[:, tt * P:(tt + 1) * P], xt[:, tt, kb * P:(kb + 1) * P], t["ident"][:])
                ins.then_inc(s["gm_done"], 1)

            def v_part(tt, kbs):
                ts = slice(tt * P, (tt + 1) * P)
                for kb in kbs:
                    for n, (ht, wt) in enumerate(((ht_hi, w_hi[2]), (ht_lo, w_hi[2]), (ht_hi, w_lo[2]))):
                        ins = nc.tensor.matmul(vo[:], ht[:, kb, ts], wt[:, kb, :],
                                               start=kb == 0 and n == 0, stop=kb == KB - 1 and n == 2)
                return ins

            def scores(U_, slot, u):
                pe.wait_ge(s["exp_done"], U_ + 1)
                h, q = u // NT, u % NT
                nc.tensor.matmul(s_bank[u % 4][:], q_stack[0:3 * HS, slot, h, q * P:(q + 1) * P],
                                 k_stack[0:3 * HS, slot, h, :], start=True, stop=True).then_inc(s["sc_done"], 1)

            pe.sem_inc(s["pt_psum"], 4)
            pe.wait_ge(s["normed"], 1)
            for kb in range(KB):
                pe.wait_ge(s["gm_free"], kb + 1)
                norm_transposes(kb)
            pe.wait_ge(s["w_split_lo"], 3)
            pe.wait_ge(s["ht_split"], KB + 2)
            for w in range(2):
                pe.wait_ge(s["gm_free"], KB + w + 1)
                project(w, 0, range(KB)).then_inc(s["gm_done"], 1)
            pe.wait_ge(s["stacked0"], 6 * HG * 16)
            scores(0, 0, 0)
            scores(1, 0, 1)

            def batch(b, last):
                for g in range(G):
                    slot = g % 2
                    for u in range(U):
                        uu = b * (G * U) + g * U + u
                        if u < U - 2:
                            scores(uu + 2, slot, u + 2)
                        elif not (last and g == G - 1):
                            if u == U - 2:
                                n = b * G + g + 1
                                pe.wait_ge(s[f"stacked{1 - slot}"], (b * 2 + (g + 1) // 2) * (6 * HG * 16) + 6 * HG * 16)
                            scores(uu + 2, 1 - slot, u + 2 - U)
                        if g == 0 and u % 4 < 3:
                            if u % 4 == 0:
                                pe.wait_ge(s["vo_free"], b * VO_PER_BATCH + u // 4 + 1)
                                if u == 0:
                                    pe.wait_ge(s["ht_split"], (b + 1) * KB + 2)
                            if u % 4 < 2:
                                v_part(u // 4, (u % 4,))
                            else:
                                v_part(u // 4, (2, 3)).then_inc(s["vo_done"], 1)
                        if not (last and g == G - 1):
                            gn = (g + 1) % G
                            if u in (0, 4):
                                kind = "qk"[u // 4]
                                pe.wait_ge(s["gm_free"], use(b, kind, g) + 1)
                                if u == 0 and g == G - 1:
                                    pe.wait_ge(s["ht_split"], (b + 2) * KB + 2)
                            if u in (0, 1, 4, 5):
                                project(u // 4, gn, (u % 4,))
                            if u in (2, 6):
                                project(u // 4, gn, (2, 3)).then_inc(s["gm_done"], 1)
                        if not last and g == G - 2 and u in (8, 10, 12, 14):
                            kb = (u - 8) // 2
                            if kb == 0:
                                pe.wait_ge(s["normed"], b + 2)
                            pe.wait_ge(s["gm_free"], use(b, "lt", g, kb) + 1)
                            norm_transposes(kb)
                        h, q = u // NT, u % NT
                        pe.wait_ge(s["masked"], uu + 1)
                        pe.wait_ge(s["pt_done"], uu + 1)
                        for j in range(q + 1):
                            ins = nc.tensor.transpose(pt_bank[u % 2][:, j * P:(j + 1) * P],
                                                      probs[:, u % 4, j * P:(j + 1) * P], t["ident"][:])
                        ins.then_inc(s["pt_psum"], 1)
                    pe.wait_ge(s["vo_free"], b * VO_PER_BATCH + NT + g + 1)
                    pe.wait_ge(s["pt_done"], b * (G * U) + (g + 1) * U + 2)
                    for j in range(NT):
                        for h in range(HG):
                            col = (g * HG + h) * HS
                            rhs = probs_t[:, h, (PT_STEP + 1) * j:(PT_STEP * j + NT), :].rearrange("p m n -> p (m n)")
                            ins = nc.tensor.matmul(vo[h * HS:(h + 1) * HS, j * P:T], v_sb[:, j, col:col + HS], rhs,
                                                   start=j == 0, stop=j == NT - 1)
                    ins.then_inc(s["vo_done"], 1)
                    pe.wait_ge(s["wide_done"], b * G + g + 1)
                    pe.wait_ge(s["gm_free"], use(b, "r", g) + 1)
                    for q in range(NT):
                        ins = nc.tensor.transpose(gm[:, q * P:(q + 1) * P],
                                                  inv_wide[:, q, :, :].rearrange("p h d -> p (h d)"), t["ident"][:])
                    ins.then_inc(s["gm_done"], 1)

            with pe.Fori(0, last_b) as b:
                batch(b, False)
            batch(last_b, True)

        @block.scalar
        def _(act):
            act.sem_inc(s["exp_done"], 4)
            act.sem_inc(s["pt_done"], 2)
            act.sem_inc(s["gm_free"], 1)
            for w in range(3):
                act.wait_ge(s[f"w_loaded{w}"], 16)
                nc.scalar.activation(w_hi[w][:], w_raw[w], ACT.Copy).then_inc(s["w_split_hi"], 1)

            def evac_norm(b, kb, at):
                wait_apart(act, s["act_passed"], (s["gm_done"], at + 1), (s["ht_split"], b * KB + kb + 1))
                nc.scalar.activation(ht_f[:, kb % 2, :], gm[:], ACT.Identity, bias=t["modc"][:, 0, kb, bass.ds(b, 1)],
                                     scale=t["modc"][:, 1, kb, bass.ds(b, 1)]).then_inc(s["gm_free"], 1)

            def evac_qk(n, which, g, at):
                act.wait_ge(s["gm_done"], at + 1)
                act.wait_ge(s["qk_split"], 2 * n + which + 1)
                col = (R_BQ, R_BK)[which] + g
                nc.scalar.activation(qk_raw[:, which, :], gm[:], ACT.Identity,
                                     bias=t["cols"][:, col:col + 1]).then_inc(s["gm_free"], 1)

            for kb in range(KB):
                evac_norm(0, kb, kb)
            for which in range(2):
                evac_qk(0, which, 0, KB + which)

            def evac_probs(uu, b, g, u):
                h, q = u // NT, u % NT
                act.wait_ge(s["pt_psum"], uu + 5)
                if u == 0:
                    act.wait_ge(s["vo_free"], b * VO_PER_BATCH + (NT + g if g else 0) + 1)
                nc.scalar.activation(probs_t[:, h, q:q + PT_STEP * q + 1:PT_STEP, :],
                                     pt_bank[u % 2][:, 0:(q + 1) * P].rearrange("p (j n) -> p j n", n=P),
                                     ACT.Copy).then_inc(s["pt_done"], 1)

            def batch(b, last):
                for g in range(G):
                    n = b * G + g
                    for u in range(U):
                        uu = b * (G * U) + g * U + u
                        if not (last and g == G - 1) and u in (3, 7):
                            which = u // 4
                            evac_qk(n + 1, which, (g + 1) % G, use(b, "qk"[which], g))
                        if not last and g == G - 2 and u in (9, 11, 13, 15):
                            kb = (u - 9) // 2
                            evac_norm(b + 1, kb, use(b, "lt", g, kb))
                        act.wait_ge(s["neg_max_done"], uu + 1)
                        act.wait_ge(s["pt_psum"], uu + 1)
                        nc.scalar.activation(probs[:, u % 4, :], s_bank[u % 4][:], ACT.Exp,
                                             bias=neg_max[:, g % 2, u:u + 1],
                                             accum_out=row_sum[:, g % 2, u:u + 1]).then_inc(s["exp_done"], 1)
                        if u:
                            evac_probs(uu - 1, b, g, u - 1)
                    evac_probs(uu, b, g, U - 1)
                    act.wait_ge(s["gm_done"], use(b, "r", g) + 1)
                    act.wait_ge(s["vo_free"], b * VO_PER_BATCH + NT + g + 1)
                    nc.scalar.activation(inv_t[:], gm[:], ACT.Copy).then_inc(s["gm_free"], 1)

            with act.Fori(0, last_b) as b:
                batch(b, False)
            batch(last_b, True)

        @block.vector
        def _(dve):
            dve.sem_inc(s["vo_free"], 1)
            dve.sem_inc(s["ht_split"], 2)
            dve.sem_inc(s["qk_split"], 2)
            for w in range(3):
                dve.wait_ge(s["w_split_hi"], w + 1)
                nc.vector.tensor_tensor(w_lo[w][:], w_raw[w], w_hi[w][:].bitcast(F32), ALU.subtract).then_inc(s["w_split_lo"], 1)
            dve.wait_ge(s["tables_loaded"], 16 * 5)

            def norm_stats(b, tt):
                if tt == 0:
                    dve.wait_ge(s["x_loaded"], (b + 1) * 16)
                nc.vector.bn_stats(stats[:, tt, :], xt[:, tt, :]).then_inc(s["stats_done"], 1)

            def norm_aggregate(b):
                wait_apart(dve, s["dve_passed"], (s["stats_done"], (b + 1) * NT))
                for tt in range(NT):
                    nc.vector.bn_aggr(mean_var[:, tt, :], stats[:, tt, :]).then_inc(s["aggr_done"], 1)
                dve.wait_ge(s["aggr_done"], (b + 1) * NT)
                nc.vector.tensor_scalar(var_eps[:], mean_var[:, :, 1], EPS, None, ALU.add).then_inc(s["vareps_done"], 1)

            def normalize(b, tt):
                if tt == 0:
                    dve.wait_ge(s["rstd_done"], b + 1)
                ins = nc.vector.tensor_scalar(xt[:, tt, :], xt[:, tt, :], mean_var[:, tt, 0:1], rstd[:, tt:tt + 1],
                                              ALU.subtract, ALU.mult)
                if tt == NT - 1:
                    ins.then_inc(s["normed"], 1)

            def split_norm(b, kb, at):
                dve.wait_ge(s["gm_free"], at + 2)
                nc.vector.tensor_copy(ht_hi[:, kb, :], ht_f[:, kb % 2, :]).then_inc(s["ht_hi_done"], 1)
                dve.wait_ge(s["ht_hi_done"], b * KB + kb + 1)
                nc.vector.tensor_tensor(ht_lo[:, kb, :], ht_f[:, kb % 2, :], ht_hi[:, kb, :].bitcast(F32),
                                        ALU.subtract).then_inc(s["ht_split"], 1)

            def rope_swap(n, which, at):
                wait_apart(dve, s["dve_passed"], (s["gm_free"], at + 2))
                m = 2 * n + which
                nc.vector.stream_shuffle(qk_swap[:, which, :], qk_raw[:, which, :], swap_pairs).then_inc(s["swapped"], 1)
                dve.wait_ge(s["swapped"], m + 1)
                nc.vector.tensor_tensor(qk_swap[:, which, :], qk_swap[:, which, :], rope[2 * which + 1][:],
                                        ALU.mult).then_inc(s["sin_done"], 1)

            def rope_add(n, which, after):
                m = 2 * n + which
                dve.wait_ge(s["sin_done"], m + 1)
                dve.wait_ge(s["cos_done"], m + 1)
                nc.vector.tensor_tensor(qk_rot[:, which, :], qk_rot[:, which, :], qk_swap[:, which, :],
                                        ALU.add).then_inc(s["rotated"], 1)
                dve.wait_ge(s["rotated"], m + 1)
                if after is not None:
                    dve.wait_ge(s[f"stacked{after[0]}"], after[1])
                nc.vector.tensor_copy(qk_hi[:, which, :], qk_rot[:, which, :]).then_inc(s["qk_hi_done"], 1)

            def rope_lo(n, which):
                m = 2 * n + which
                dve.wait_ge(s["qk_hi_done"], m + 1)
                nc.vector.tensor_tensor(qk_lo[:, which, :], qk_rot[:, which, :], qk_hi[:, which, :].bitcast(F32),
                                        ALU.subtract).then_inc(s["qk_split"], 1)

            def normalize_output(b, g):
                dve.wait_ge(s["gm_free"], use(b, "r", g) + 2)
                dve.wait_ge(s["vo_done"], b * VO_PER_BATCH + NT + g + 1)
                nc.vector.tensor_tensor(attn_out[:, g % 2, :], vo[:], inv_t[:], ALU.mult).then_inc(s["vo_free"], 1)

            for tt in range(NT):
                norm_stats(0, tt)
            norm_aggregate(0)
            for tt in range(NT):
                normalize(0, tt)
            for kb in range(KB):
                split_norm(0, kb, kb)
            for which in range(2):
                rope_swap(0, which, KB + which)
                rope_add(0, which, None)
                rope_lo(0, which)

            def batch(b, last):
                for g in range(G):
                    n = b * G + g
                    for u in range(U):
                        uu = b * (G * U) + g * U + u
                        dve.wait_ge(s["sc_done"], uu + 1)
                        nc.vector.tensor_reduce(neg_max[:, g % 2, u:u + 1], s_bank[u % 4][:], AX.X, ALU.max,
                                                negate=True).then_inc(s["neg_max_done"], 1)
                        if not (last and g == G - 1):
                            if u in (4, 8):
                                rope_swap(n + 1, u // 4 - 1, use(b, "qk"[u // 4 - 1], g))
                            if u in (5, 9):
                                done = (b * 2 + g // 2) * (6 * HG * 16) + 6 * HG * 16
                                rope_add(n + 1, u // 4 - 1, (g % 2, done))
                            if u in (6, 10):
                                rope_lo(n + 1, u // 4 - 1)
                        if g == 0 and u % 4 == 3:
                            tt = u // 4
                            dve.wait_ge(s["vo_done"], b * VO_PER_BATCH + tt + 1)
                            nc.vector.tensor_tensor(v_sb[:, tt, :], vo[:], bv_rows[:], ALU.add).then_inc(s["vo_free"], 1)
                        if not last:
                            if g == G - 3 and u >= 12:
                                norm_stats(b + 1, u - 12)
                            if g == G - 2 and u == 0:
                                norm_aggregate(b + 1)
                            if g == G - 2 and u in (3, 4, 5, 6):
                                normalize(b + 1, u - 3)
                            if g == G - 2 and u in (11, 13, 15):
                                split_norm(b + 1, (u - 11) // 2, use(b, "lt", g, (u - 11) // 2))
                    if not last and g == G - 2:
                        split_norm(b + 1, KB - 1, use(b, "lt", g, KB - 1))
                    dve.wait_ge(s["exp_done"], b * (G * U) + (g + 1) * U + 4)
                    nc.vector.reciprocal(row_inv[:], row_sum[:, g % 2, :]).then_inc(s["inv_done"], 1)
                    dve.wait_ge(s[f"attn_stored{g % 2}"], (b * 2 + g // 2) * 16 + 1)
                    normalize_output(b, g)

            with dve.Fori(0, last_b) as b:
                batch(b, False)
            batch(last_b, True)

        @block.gpsimd
        def _(pool):
            def power(b):
                pool.wait_ge(s["vareps_done"], b + 1)
                nc.gpsimd.tensor_tensor(rstd[:], var_eps[:], t["neg_half"][:], ALU.pow).then_inc(s["rstd_done"], 1)

            def rope_cos(n, which, at):
                pool.wait_ge(s["gm_free"], at + 2)
                nc.gpsimd.tensor_tensor(qk_rot[:, which, :], qk_raw[:, which, :], rope[2 * which][:],
                                        ALU.mult).then_inc(s["cos_done"], 1)

            power(0)
            pool.wait_ge(s["tables_loaded"], 16 * 5)
            for which in range(2):
                rope_cos(0, which, KB + which)

            def batch(b, last):
                for g in range(G):
                    n = b * G + g
                    for u in range(U):
                        uu = b * (G * U) + g * U + u
                        wait_apart(pool, s["pool_passed"], (s["exp_done"], uu + 5))
                        q = u % NT
                        v = probs[:, u % 4, q * P:(q + 1) * P]
                        nc.gpsimd.affine_select(out=v, in_=v, compare_op=ALU.is_ge, fill=0.0, base=0,
                                                pattern=[[-1, P]], channel_multiplier=1).then_inc(s["masked"], 1)
                        if not (last and g == G - 1) and u in (3, 7):
                            rope_cos(n + 1, u // 4, use(b, "qk"[u // 4], g))
                        if not last and g == G - 2 and u == 0:
                            power(b + 1)
                    wait_apart(pool, s["pool_passed"], (s["inv_done"], n + 1))
                    nc.gpsimd.tensor_copy(
                        inv_wide[:], row_inv[:].rearrange("p (h q) -> p q h", h=HG).unsqueeze(3)
                        .to_broadcast([P, NT, HG, HS])).then_inc(s["wide_done"], 1)

            with pool.Fori(0, last_b) as b:
                batch(b, False)
            batch(last_b, True)


def stage_project(nc, a, sem, bank, t):
    ctx = ExitStack()
    with ctx:
        def sb(name, shape, dt=F32):
            return ctx.enter_context(nc.sbuf_tensor(name, shape, dt))

        wo_raw = sb("wo_raw", [P, KB, H])
        wo_hi = sb("wo_hi", [P, KB, H], F32R)
        wo_lo = sb("wo_lo", [P, KB, H], F32R)
        ot = sb("ot", [P, KB, T])
        ot_hi = sb("ot_hi", [P, KB, T], F32R)
        ot_lo = sb("ot_lo", [P, KB, T], F32R)
        gates = sb("gates", [P, 2, H])
        xr = sb("xr", [P, NT, H])
        gated = sb("gated", [P, 2, H])
        x1 = sb("x1", [P, NT, H])
        xn = sb("xn", [P, NT, H])
        stats = sb("stats2", [P, NT, 6])
        mean_var = sb("mean_var2", [P, NT, 2])
        var_eps = sb("var_eps2", [P, NT])
        rstd = sb("rstd2", [P, NT])
        z = sb("z", [P, KB, T])
        z2 = sb("z2", [P, KB, T])
        y_bank, tr_bank, h_bank = bank[0:NT], bank[4:6], bank[6:8]

        names = ("wo_loaded wo_hi_done wo_split ot_loaded gates_loaded x_loaded ot_hi_done ot_split y_psum "
                 "gated_done x1_done x_biased stats_done vareps_done rstd_done normed x1_stored tr_psum tr_free "
                 "fly1 fly2 h_psum hi_done h_free aggr_done act_passed dve_passed")
        s = {n: sem("c_" + n) for n in names.split()}
        block = ctx.enter_context(nc.Block())
        x_by_batch = a["L0_attn_x"].rearrange("b (t p) h -> b p t h", p=P)
        attn_by_batch = t["attn_d"].rearrange("b g p t -> b p g t")
        x1_by_batch = t["x1_d"].rearrange("b t p h -> b p t h")
        rows_by_batch = t["mod_rows_d"].rearrange("i b h -> b i h")

        @block.sync
        def _(sp):
            sp.dma_start(wo_raw[:], a["L0_attn_Wo"].rearrange("(k p) n -> p k n", p=P)).then_inc(s["wo_loaded"], 16)

            def load(b):
                sp.dma_start(ot[:], attn_by_batch[b]).then_inc(s["ot_loaded"], 16)
                sp.dma_start(xr[:], x_by_batch[b]).then_inc(s["x_loaded"], 16)
                sp.dma_start(gates[:], rows_by_batch[b, 0:2].partition_broadcast(P)).then_inc(s["gates_loaded"], 16)

            sp.sem_inc(s["x1_stored"], 1)
            load(0)
            with sp.Fori(0, B - 1) as b:
                sp.wait_ge(s["x1_done"], (b + 1) * NT)
                sp.dma_start(x1_by_batch[b], x1[:]).then_inc(s["x1_stored"], 16)
                load(b + 1)
            sp.wait_ge(s["x1_done"], B * NT)
            sp.dma_start(x1_by_batch[B - 1], x1[:]).then_inc(s["x1_stored"], 16)
            sp.wait_ge(s["x1_stored"], B * 16 + 1)

        @block.tensor
        def _(pe):
            pe.wait_ge(s["wo_split"], 1)

            def output(b):
                pe.wait_ge(s["ot_split"], b + 1)
                for tt in range(NT):
                    ts = slice(tt * P, (tt + 1) * P)
                    pe.wait_ge(s["gated_done"], b * NT + tt + 1)
                    for kb in range(KB):
                        for n, (ot_, wo_) in enumerate(((ot_hi, wo_hi), (ot_lo, wo_hi), (ot_hi, wo_lo))):
                            ins = nc.tensor.matmul(y_bank[tt][:], ot_[:, kb, ts], wo_[:, kb, :],
                                                   start=kb == 0 and n == 0, stop=kb == KB - 1 and n == 2)
                    ins.then_inc(s["y_psum"], 1)

            def transposes(b):
                pe.wait_ge(s["normed"], b + 1)
                for kb in range(KB):
                    pe.wait_ge(s["tr_free"], b * KB + kb + 1)
                    for tt in range(NT):
                        ins = nc.tensor.transpose(tr_bank[kb % 2][:, tt * P:(tt + 1) * P],
                                                  xn[:, tt, kb * P:(kb + 1) * P], t["ident"][:])
                    ins.then_inc(s["tr_psum"], 1)

            def hadamard_128(b):
                pe.wait_ge(s["fly2"], b * 2 + 2)
                for kb in range(KB):
                    pe.wait_ge(s["h_free"], b * KB + kb + 1)
                    nc.tensor.matmul(h_bank[kb % 2][:], t["had"][:], z[:, kb, :], start=True,
                                     stop=True).then_inc(s["h_psum"], 1)

            output(0)
            with pe.Fori(0, B - 1) as b:
                transposes(b)
                output(b + 1)
                hadamard_128(b)
            transposes(B - 1)
            hadamard_128(B - 1)

        @block.scalar
        def _(act):
            act.sem_inc(s["tr_free"], 2)
            act.wait_ge(s["wo_loaded"], 16)
            nc.scalar.activation(wo_hi[:], wo_raw[:], ACT.Copy).then_inc(s["wo_hi_done"], 1)

            def split_hi(b):
                act.wait_ge(s["ot_loaded"], (b + 1) * 16)
                nc.scalar.activation(ot_hi[:], ot[:], ACT.Copy).then_inc(s["ot_hi_done"], 1)

            def evacuate(b):
                for kb in range(KB):
                    wait_apart(act, s["act_passed"], (s["tr_psum"], b * KB + kb + 1))
                    nc.scalar.activation(z[:, kb, :], tr_bank[kb % 2][:], ACT.Identity,
                                         bias=t["modc"][:, 2, kb, bass.ds(b, 1)],
                                         scale=t["modc"][:, 3, kb, bass.ds(b, 1)]).then_inc(s["tr_free"], 1)
                for kb in range(KB):
                    wait_apart(act, s["act_passed"], (s["h_psum"], b * KB + kb + 1))
                    nc.scalar.activation(t["h2_hi"][:, kb, bass.ds(b * T, T)], h_bank[kb % 2][:],
                                         ACT.Copy).then_inc(s["hi_done"], 1)

            split_hi(0)
            with act.Fori(0, B - 1) as b:
                split_hi(b + 1)
                evacuate(b)
            evacuate(B - 1)

        @block.vector
        def _(dve):
            dve.sem_inc(s["gated_done"], NT)
            dve.sem_inc(s["h_free"], 2)
            dve.wait_ge(s["wo_hi_done"], 1)
            nc.vector.tensor_tensor(wo_lo[:], wo_raw[:], wo_hi[:].bitcast(F32), ALU.subtract).then_inc(s["wo_split"], 1)

            def split(b):
                dve.wait_ge(s["ot_hi_done"], b + 1)
                nc.vector.tensor_tensor(ot_lo[:], ot[:], ot_hi[:].bitcast(F32), ALU.subtract).then_inc(s["ot_split"], 1)

            def residual(b):
                dve.wait_ge(s["gates_loaded"], (b + 1) * 16)
                dve.wait_ge(s["x_biased"], b + 1)
                for tt in range(NT):
                    dve.wait_ge(s["y_psum"], b * NT + tt + 1)
                    nc.vector.tensor_tensor(gated[:, tt % 2, :], y_bank[tt][:], gates[:, 0, :],
                                            ALU.mult).then_inc(s["gated_done"], 1)
                    dve.wait_ge(s["gated_done"], b * NT + tt + 1 + NT)
                    if tt == 0:
                        dve.wait_ge(s["x1_stored"], b * 16 + 1)
                    nc.vector.tensor_tensor(x1[:, tt, :], gated[:, tt % 2, :], xr[:, tt, :],
                                            ALU.add).then_inc(s["x1_done"], 1)
                for tt in range(NT):
                    dve.wait_ge(s["x1_done"], b * NT + tt + 1)
                    nc.vector.bn_stats(stats[:, tt, :], x1[:, tt, :]).then_inc(s["stats_done"], 1)
                wait_apart(dve, s["dve_passed"], (s["stats_done"], (b + 1) * NT))
                for tt in range(NT):
                    nc.vector.bn_aggr(mean_var[:, tt, :], stats[:, tt, :]).then_inc(s["aggr_done"], 1)
                dve.wait_ge(s["aggr_done"], (b + 1) * NT)
                nc.vector.tensor_scalar(var_eps[:], mean_var[:, :, 1], EPS, None, ALU.add).then_inc(s["vareps_done"], 1)
                dve.wait_ge(s["rstd_done"], b + 1)
                for tt in range(NT):
                    ins = nc.vector.tensor_scalar(xn[:, tt, :], x1[:, tt, :], mean_var[:, tt, 0:1], rstd[:, tt:tt + 1],
                                                  ALU.subtract, ALU.mult)
                ins.then_inc(s["normed"], 1)

            def transform(b):
                dve.wait_ge(s["tr_free"], (b + 1) * KB + 2)
                v = z[:].rearrange("p (m a) n -> p m a n", a=2)
                w = z2[:].rearrange("p (m a) n -> p m a n", a=2)
                nc.vector.tensor_tensor(w[:, :, 0, :], v[:, :, 0, :], v[:, :, 1, :], ALU.add).then_inc(s["fly1"], 1)
                nc.vector.tensor_tensor(w[:, :, 1, :], v[:, :, 0, :], v[:, :, 1, :], ALU.subtract).then_inc(s["fly1"], 1)
                dve.wait_ge(s["fly1"], b * 2 + 2)
                nc.vector.tensor_tensor(z[:, 0:2, :], z2[:, 0:2, :], z2[:, 2:4, :], ALU.add).then_inc(s["fly2"], 1)
                nc.vector.tensor_tensor(z[:, 2:4, :], z2[:, 0:2, :], z2[:, 2:4, :], ALU.subtract).then_inc(s["fly2"], 1)

            def split_transform(b):
                for kb in range(KB):
                    dve.wait_ge(s["hi_done"], b * KB + kb + 1)
                    cs = bass.ds(b * T, T)
                    nc.vector.tensor_tensor(t["h2_lo"][:, kb, cs], h_bank[kb % 2][:], t["h2_hi"][:, kb, cs].bitcast(F32),
                                            ALU.subtract).then_inc(s["h_free"], 1)

            split(0)
            with dve.Fori(0, B - 1) as b:
                residual(b)
                split(b + 1)
                transform(b)
                split_transform(b)
            residual(B - 1)
            transform(B - 1)
            split_transform(B - 1)

        @block.gpsimd
        def _(pool):
            with pool.Fori(0, B) as b:
                pool.wait_ge(s["x_loaded"], (b + 1) * 16)
                pool.wait_ge(s["gates_loaded"], (b + 1) * 16)
                for tt in range(NT):
                    ins = nc.gpsimd.tensor_tensor(xr[:, tt, :], xr[:, tt, :], gates[:, 1, :], ALU.add)
                ins.then_inc(s["x_biased"], 1)
                pool.wait_ge(s["vareps_done"], b + 1)
                nc.gpsimd.tensor_tensor(rstd[:], var_eps[:], t["neg_half"][:], ALU.pow).then_inc(s["rstd_done"], 1)


def stage_ffn(nc, a, sem, bank, t):
    ctx = ExitStack()
    with ctx:
        def sb(name, shape, dt=F32):
            return ctx.enter_context(nc.sbuf_tensor(name, shape, dt))

        raw = sb("raw", [P, 2, KB, H])
        wug_hi = sb("wug_hi", [P, 2, KB, QB * P], F32R)
        wug_lo = sb("wug_lo", [P, 2, KB, QB * P], F32R)
        wd_t = sb("wd_t", [P, H])
        wd_hi = sb("wd_hi", [P, QB, H], F32R)
        wd_lo = sb("wd_lo", [P, QB, H], F32R)
        act_f = sb("act_f", [P, 2, T])
        act_hi = sb("act_hi", [P, 2, QB, T], F32R)
        act_lo = sb("act_lo", [P, 2, QB, T], F32R)
        acc = sb("acc", [P, B * NT, H])
        out_gate = sb("out_gate", [P, 2, H])
        g_bank, u_bank, y_bank, prep_bank = bank[0:2], bank[2:4], bank[4:6], bank[6:8]

        names = ("up_loaded gate_loaded down_loaded prep_psum prep_hi prep_lo wdt_done g_psum u_psum silu_done "
                 "act_done act_hi_done act_split y_psum acc_done acc_zero og_loaded0 og_loaded1 x1_loaded0 x1_loaded1 "
                 "out_gated out_done out_stored act_passed")
        s = {n: sem("d_" + n) for n in names.split()}
        block = ctx.enter_context(nc.Block())
        PREP_PSUM = 2 * QB + 2 * QB
        PREP_SPLIT = 2 * QB + QB
        fs = t["ffn_scale"]
        up_rows = a["L0_ffn_W_up"].rearrange("(q i p) h -> q p i h", q=NQ, p=P)
        gate_rows = a["L0_ffn_W_gate"].rearrange("(q i p) h -> q p i h", q=NQ, p=P)
        down_cols = t["wd_d"].rearrange("k p (q n) -> q p k n", q=NQ)
        x1_by_batch = t["x1_d"].rearrange("b t p h -> b p t h")
        out_by_batch = a["out"].rearrange("b (t p) h -> b p t h", p=P)

        @block.sync
        def _(sp):
            def load_up_gate(q):
                sp.dma_start(raw[:, 0, :, :], up_rows[q]).then_inc(s["up_loaded"], 16)
                sp.dma_start(raw[:, 1, :, :], gate_rows[q]).then_inc(s["gate_loaded"], 16)

            def load_down(q):
                sp.wait_ge(s["prep_psum"], q * PREP_PSUM + QB)
                sp.dma_start(raw[:, 0, :, :], down_cols[q]).then_inc(s["down_loaded"], 16)

            load_up_gate(0)
            load_down(0)
            with sp.Fori(1, NQ) as q:
                sp.wait_ge(s["prep_psum"], q * PREP_PSUM)
                load_up_gate(q)
                load_down(q)
            sp.wait_ge(s["prep_psum"], NQ * PREP_PSUM)
            for b in range(B):
                if b >= 2:
                    sp.wait_ge(s["out_done"], (b - 1) * NT)
                sp.dma_start(raw[:, b % 2, :, :], x1_by_batch[b]).then_inc(s[f"x1_loaded{b % 2}"], 16)
                sp.dma_start(out_gate[:, b % 2, :], t["mod_rows_d"][2, b].partition_broadcast(P)).then_inc(
                    s[f"og_loaded{b % 2}"], 16)
                if b >= 1:
                    sp.wait_ge(s["out_done"], b * NT)
                    sp.dma_start(out_by_batch[b - 1], acc[:, (b - 1) * NT:b * NT, :]).then_inc(s["out_stored"], 16)
            for half in range(2):
                ts = slice((B - 1) * NT + 2 * half, (B - 1) * NT + 2 * half + 2)
                sp.wait_ge(s["out_done"], (B - 1) * NT + 2 * half + 2)
                sp.dma_start(out_by_batch[B - 1][:, 2 * half:2 * half + 2], acc[:, ts, :]).then_inc(s["out_stored"], 16)
            sp.wait_ge(s["out_stored"], 16 * (B + 1))

        @block.tensor
        def _(pe):
            pe.sem_inc(s["y_psum"], 2 * NT)

            def prepare_up_gate(q):
                for i in range(2 * QB):
                    which, ib = i // QB, i % QB
                    if ib == 0:
                        pe.wait_ge(s[("up_loaded", "gate_loaded")[which]], (q + 1) * 16)
                    pe.wait_ge(s["prep_lo"], q * PREP_SPLIT + i + 1)
                    for kb in range(KB):
                        ins = nc.tensor.transpose(prep_bank[i % 2][:, kb * P:(kb + 1) * P],
                                                  raw[:, which, ib, kb * P:(kb + 1) * P], t["ident"][:])
                    ins.then_inc(s["prep_psum"], 1)

            def prepare_down(q):
                pe.wait_ge(s["down_loaded"], (q + 1) * 16)
                pe.wait_ge(s["prep_lo"], q * PREP_SPLIT + 2 * QB + 1)
                for ib in range(QB):
                    for ht in range(KB):
                        ins = nc.tensor.transpose(prep_bank[0][:, ht * P:(ht + 1) * P],
                                                  raw[:, 0, ht, ib * P:(ib + 1) * P], t["ident"][:])
                    ins.then_inc(s["prep_psum"], 1)
                    pe.wait_ge(s["wdt_done"], q * QB + ib + 1)
                    pe.wait_ge(s["prep_lo"], q * PREP_SPLIT + 2 * QB + ib + 2)
                    nc.tensor.matmul(prep_bank[1][:], t["had"][:], wd_t[:], start=True,
                                     stop=True).then_inc(s["prep_psum"], 1)

            def up_gate(q, b, ib):
                i = q * (B * QB) + b * QB + ib
                pe.wait_ge(s["act_done"], i + 1)
                for which, bk, done in ((1, g_bank, "g_psum"), (0, u_bank, "u_psum")):
                    for kb in range(KB):
                        for n, (w, h) in enumerate(((wug_hi, t["h2_hi"]), (wug_hi, t["h2_lo"]), (wug_lo, t["h2_hi"]))):
                            ins = nc.tensor.matmul(bk[ib % 2][:], w[:, which, kb, ib * P:(ib + 1) * P],
                                                   h[:, kb, b * T:(b + 1) * T], start=kb == 0 and n == 0,
                                                   stop=kb == KB - 1 and n == 2)
                    ins.then_inc(s[done], 1)

            def down(q, b):
                n_ = q * B + b
                pe.wait_ge(s["act_split"], (n_ + 1) * QB + 2)
                for tt in range(NT):
                    ts = slice(tt * P, (tt + 1) * P)
                    pe.wait_ge(s["acc_done"], n_ * NT + tt + 1)
                    for ib in range(QB):
                        for n, (x, w) in enumerate(((act_hi, wd_hi), (act_lo, wd_hi), (act_hi, wd_lo))):
                            ins = nc.tensor.matmul(y_bank[tt % 2][:], x[:, b % 2, ib, ts], w[:, ib, :],
                                                   start=ib == 0 and n == 0, stop=ib == QB - 1 and n == 2)
                    ins.then_inc(s["y_psum"], 1)

            def quarter(q):
                pe.wait_ge(s["prep_lo"], q * PREP_SPLIT + PREP_SPLIT + 2)
                for b in range(B):
                    for ib in range(QB):
                        up_gate(q, b, ib)
                        if ib == 0 and b >= 1:
                            down(q, b - 1)

            prepare_up_gate(0)
            prepare_down(0)
            with pe.Fori(0, NQ - 1) as q:
                quarter(q)
                prepare_up_gate(q + 1)
                down(q, B - 1)
                prepare_down(q + 1)
            quarter(NQ - 1)
            down(NQ - 1, B - 1)

        @block.scalar
        def _(act):
            def prepare_up_gate(q):
                for i in range(2 * QB):
                    which, ib = i // QB, i % QB
                    act.wait_ge(s["prep_psum"], q * PREP_PSUM + i + 1)
                    nc.scalar.activation(wug_hi[:, which, :, ib * P:(ib + 1) * P],
                                         prep_bank[i % 2][:].rearrange("p (k n) -> p k n", k=KB),
                                         ACT.Copy).then_inc(s["prep_hi"], 1)

            def prepare_down(q):
                for ib in range(QB):
                    act.wait_ge(s["prep_psum"], q * PREP_PSUM + 2 * QB + 2 * ib + 1)
                    nc.scalar.activation(wd_t[:], prep_bank[0][:], ACT.Copy).then_inc(s["wdt_done"], 1)
                    act.wait_ge(s["prep_psum"], q * PREP_PSUM + 2 * QB + 2 * ib + 2)
                    nc.scalar.activation(wd_hi[:, ib, :], prep_bank[1][:], ACT.Copy).then_inc(s["prep_hi"], 1)

            def quarter(q):
                for b in range(B):
                    for ib in range(QB):
                        i = q * (B * QB) + b * QB + ib
                        wait_apart(act, s["act_passed"], (s["g_psum"], i + 1), (s["act_split"], i + 1))
                        nc.scalar.activation(act_f[:, ib % 2, :], g_bank[ib % 2][:], ACT.Silu,
                                             scale=fs[:, 1, bass.ds(q * QB + ib, 1)]).then_inc(s["silu_done"], 1)

            prepare_up_gate(0)
            prepare_down(0)
            with act.Fori(0, NQ - 1) as q:
                quarter(q)
                prepare_up_gate(q + 1)
                prepare_down(q + 1)
            quarter(NQ - 1)

        @block.vector
        def _(dve):
            dve.sem_inc(s["prep_lo"], 2)
            dve.sem_inc(s["act_done"], 2)
            dve.sem_inc(s["acc_done"], 2)
            dve.sem_inc(s["act_split"], 2)

            def prepare_up_gate(q):
                for i in range(2 * QB):
                    which, ib = i // QB, i % QB
                    cs = slice(ib * P, (ib + 1) * P)
                    dve.wait_ge(s["prep_hi"], q * PREP_SPLIT + i + 1)
                    nc.vector.tensor_tensor(wug_lo[:, which, :, cs], prep_bank[i % 2][:].rearrange("p (k n) -> p k n", k=KB),
                                            wug_hi[:, which, :, cs].bitcast(F32), ALU.subtract).then_inc(s["prep_lo"], 1)

            def prepare_down(q):
                for ib in range(QB):
                    dve.wait_ge(s["prep_hi"], q * PREP_SPLIT + 2 * QB + ib + 1)
                    nc.vector.tensor_tensor(wd_lo[:, ib, :], prep_bank[1][:], wd_hi[:, ib, :].bitcast(F32),
                                            ALU.subtract).then_inc(s["prep_lo"], 1)

            def activations(q, b, ib):
                i = q * (B * QB) + b * QB + ib
                dve.wait_ge(s["silu_done"], i + 1)
                dve.wait_ge(s["u_psum"], i + 1)
                f = act_f[:, ib % 2, :]
                nc.vector.scalar_tensor_tensor(out=f, in0=u_bank[ib % 2][:], scalar=fs[:, 0, bass.ds(q * QB + ib, 1)],
                                               in1=f, op0=ALU.mult, op1=ALU.mult).then_inc(s["act_done"], 1)
                dve.wait_ge(s["act_done"], i + 3)
                if ib == 0:
                    dve.wait_ge(s["y_psum"], (q * B + b + 1) * NT)
                nc.vector.tensor_copy(act_hi[:, b % 2, ib, :], f).then_inc(s["act_hi_done"], 1)
                dve.wait_ge(s["act_hi_done"], i + 1)
                nc.vector.tensor_tensor(act_lo[:, b % 2, ib, :], f, act_hi[:, b % 2, ib, :].bitcast(F32),
                                        ALU.subtract).then_inc(s["act_split"], 1)

            def accumulate(q, b, last):
                n_ = q * B + b
                if last:
                    dve.wait_ge(s[f"og_loaded{b % 2}"], 16 * (b // 2 + 1))
                for tt in range(NT):
                    i = n_ * NT + tt
                    at = b * NT + tt
                    dve.wait_ge(s["y_psum"], i + 2 * NT + 1)
                    dve.wait_ge(s["acc_done"], i + 1)
                    nc.vector.tensor_tensor(acc[:, at, :], y_bank[tt % 2][:], acc[:, at, :],
                                            ALU.add).then_inc(s["acc_done"], 1)
                    if last:
                        dve.wait_ge(s["acc_done"], i + 3)
                        nc.vector.tensor_tensor(acc[:, at, :], acc[:, at, :], out_gate[:, b % 2, :],
                                                ALU.mult).then_inc(s["out_gated"], 1)
                        dve.wait_ge(s[f"x1_loaded{b % 2}"], 16 * (b // 2 + 1))
                        dve.wait_ge(s["out_gated"], at + 1)
                        nc.vector.tensor_tensor(acc[:, at, :], acc[:, at, :], raw[:, b % 2, tt, :],
                                                ALU.add).then_inc(s["out_done"], 1)

            def quarter(q, last):
                for b in range(B):
                    for ib in range(QB):
                        activations(q, b, ib)
                        if ib == 0 and b >= 1:
                            accumulate(q, b - 1, last)

            prepare_up_gate(0)
            prepare_down(0)
            dve.wait_ge(s["acc_zero"], 1)
            with dve.Fori(0, NQ - 1) as q:
                quarter(q, False)
                prepare_up_gate(q + 1)
                accumulate(q, B - 1, False)
                prepare_down(q + 1)
            quarter(NQ - 1, True)
            accumulate(NQ - 1, B - 1, True)

        @block.gpsimd
        def _(pool):
            nc.gpsimd.memset(acc[:], 0.0).then_inc(s["acc_zero"], 1)


_CONSTANTS = {
    "ident": np.eye(P, dtype=np.float32),
    "had": hadamard(P),
    "qcos": rope_tables(float(HS) ** -0.5)[0],
    "qsin": rope_tables(float(HS) ** -0.5)[1],
    "kcos": rope_tables(1.0)[0],
    "ksin": rope_tables(1.0)[1],
}


def kernel(**inputs):
    import concourse.bacc as _bacc
    from concourse.bass_utils import run_bass_kernel_spmd as _run

    nc = _bacc.Bacc("TRN2", target_bir_lowering=False, num_devices=1)
    arrays, aps = {}, {}
    for name, value in [*inputs.items(), *_CONSTANTS.items()]:
        value = np.ascontiguousarray(value)
        arrays[f"in_{name}"] = value
        aps[name] = nc.dram_tensor(f"in_{name}", value.shape, mybir.dt.from_np(value.dtype), kind="ExternalInput").ap()
    aps["out"] = nc.dram_tensor("out_0", (B, T, H), F32, kind="ExternalOutput").ap()
    build_program(nc, aps)
    return _run(nc, [arrays], core_ids=[0]).results[0]["out_0"]
```

```python
from contextlib import ExitStack

import numpy as np

import concourse.bass as bass
from concourse import mybir

F32 = mybir.dt.float32
F32R = mybir.dt.float32r
ALU = mybir.AluOpType
ACT = mybir.ActivationFunctionType
AX = mybir.AxisListType

P = 128
B = 4
T = 512
H = 512
NT = T // P
KB = H // P
NH = 16
HS = H // NH
HG = P // HS
G = NH // HG
U = HG * NT
INTER = 2048
IB = INTER // P
NQ = 4
QB = IB // NQ
EPS = 1e-5
ROPE_BASE = 10000.0

R_BQ, R_BK, R_BV, R_WUG, R_SUU, R_SUD, R_C, R_N = 0, 4, 8, 12, 44, 48, 64, 80


def wait_apart(engine, passed, *waits):
    for semaphore, value in waits:
        engine.wait_ge(semaphore, value)
    engine.sem_inc(passed, 1)


def rope_tables(scale):
    inv = (np.float32(1.0) / np.float32(ROPE_BASE) ** (np.arange(0, HS, 2, dtype=np.float32) / np.float32(HS)))
    ang = np.arange(T, dtype=np.float32)[None, :] * inv.astype(np.float32)[:, None]
    cos, sin = np.cos(ang), np.sin(ang)
    c = np.repeat(cos, 2, axis=0)
    s = np.stack([-sin, sin], axis=1).reshape(HS, T)
    return [np.ascontiguousarray(np.tile(a, (HG, 1)) * np.float32(scale)).astype(np.float32) for a in (c, s)]


def hadamard(n):
    h = np.ones((1, 1), np.float32)
    while h.shape[0] < n:
        h = np.block([[h, h], [h, -h]])
    return h.astype(np.float32)


def build_program(nc, a, stop=4):
    ctx = ExitStack()

    def sem(name):
        return ctx.enter_context(nc.semaphore(name))

    def dram(name, shape):
        return nc.dram_tensor(name, shape, F32, kind="Internal").ap()

    with ctx:
        mod_rows_d = dram("mod_rows_d", (3, B, H))
        attn_d = dram("attn_d", (B, G, P, T))
        x1_d = dram("x1_d", (B, NT, P, H))
        wd_d = dram("wd_d", (KB, P, INTER))

        def keep(name, shape, dt=F32):
            return ctx.enter_context(nc.sbuf_tensor(name, shape, dt))

        ident = keep("ident", [P, P])
        had = keep("had", [P, P])
        cols = keep("cols", [P, R_N])
        modc = keep("modc", [P, 4, KB, B])
        ffn_scale = keep("ffn_scale", [P, 2, IB])
        neg_half = keep("neg_half", [P, NT])
        bank = [ctx.enter_context(nc.psum_tensor(f"bank{i}", [P, 512], F32)) for i in range(8)]

        stage_setup(nc, a, sem, bank, dict(
            ident=ident, had=had, cols=cols, modc=modc, ffn_scale=ffn_scale, neg_half=neg_half,
            mod_rows_d=mod_rows_d, wd_d=wd_d))
        if stop >= 2:
            stage_attention(nc, a, sem, bank, dict(
                ident=ident, cols=cols, modc=modc, neg_half=neg_half, attn_d=attn_d))
        if stop >= 3:
            with nc.sbuf_tensor("h2_hi", [P, KB, B * T], F32R) as h2_hi, \
                    nc.sbuf_tensor("h2_lo", [P, KB, B * T], F32R) as h2_lo:
                stage_project(nc, a, sem, bank, dict(
                    ident=ident, had=had, cols=cols, modc=modc, neg_half=neg_half, attn_d=attn_d,
                    mod_rows_d=mod_rows_d, x1_d=x1_d, h2_hi=h2_hi, h2_lo=h2_lo))
                if stop >= 4:
                    stage_ffn(nc, a, sem, bank, dict(
                        ident=ident, had=had, ffn_scale=ffn_scale, x1_d=x1_d, wd_d=wd_d,
                        mod_rows_d=mod_rows_d, h2_hi=h2_hi, h2_lo=h2_lo))


def stage_setup(nc, a, sem, bank, t):
    ctx = ExitStack()
    with ctx:
        def sb(name, shape, dt=F32):
            return ctx.enter_context(nc.sbuf_tensor(name, shape, dt))

        rows = sb("rows", [P, P])
        silu_c = sb("silu_c", [P, KB, B])
        wmod = sb("wmod", [P, KB, 6 * H])
        gate_bias = sb("gate_bias", [B, 2, H])
        gate = sb("gate", [B, 2, H])
        gate_sign = sb("gate_sign", [B, 2, H])
        gate_abs = sb("gate_abs", [B, 2, H])
        gate_out = sb("gate_out", [B, 3, H])
        wdn = sb("wdn", [P, 2, INTER])
        wdm = sb("wdm", [P, 2, INTER])

        rows_loaded, consts_loaded, wmod_loaded = sem("rows_loaded"), sem("consts_loaded"), sem("wmod_loaded")
        gbias_loaded = sem("gbias_loaded")
        wd_loaded = [sem(f"wd_loaded{i}") for i in range(2)]
        wd_stored = [sem(f"wd_stored{i}") for i in range(2)]
        cols_psum, cols_ready, silu_ready = sem("cols_psum"), sem("cols_ready"), sem("silu_ready")
        modc_psum, gate_psum = sem("modc_psum"), sem("gate_psum")
        vec_chain, gates_ready, gates_stored = sem("vec_chain"), sem("gates_ready"), sem("gates_stored")
        butterfly = sem("butterfly")
        block = ctx.enter_context(nc.Block())

        @block.sync
        def _(sp):
            sp.dma_start(t["ident"][:], a["ident"]).then_inc(consts_loaded, 16)
            for at, name in ((R_BQ, "L0_attn_bq"), (R_BK, "L0_attn_bk"), (R_BV, "L0_attn_bv"), (R_WUG, "L0_ffn_Wscale_ug"),
                             (R_SUU, "L0_ffn_SU_ug"), (R_SUD, "L0_ffn_SU_dp")):
                n = a[name].shape[0] // P
                sp.dma_start(rows[at:at + n, :], a[name].rearrange("(r p) -> r p", p=P)).then_inc(rows_loaded, 16)
            for kb in range(KB):
                sp.dma_start(rows[R_C + kb * B:R_C + (kb + 1) * B, :],
                             a["L0_c"][:, kb * P:(kb + 1) * P]).then_inc(rows_loaded, 16)
            for kb in range(KB):
                sp.dma_start(wmod[:, kb, :], a["L0_wmod"][kb * P:(kb + 1) * P, :]).then_inc(wmod_loaded, 16)
            sp.dma_start(t["had"][:], a["had"]).then_inc(consts_loaded, 16)
            sp.dma_start(gate_bias[:, 0, :], a["L0_attn_bo"].partition_broadcast(B)).then_inc(gbias_loaded, 16)
            sp.dma_start(gate_bias[:, 1, :], a["L0_ffn_Wscale_dp"].partition_broadcast(B)).then_inc(gbias_loaded, 16)
            sp.wait_ge(gates_ready, 1)
            for i in range(3):
                sp.dma_start(t["mod_rows_d"][i], gate_out[:, i, :]).then_inc(gates_stored, 16)
            sp.wait_ge(gates_stored, 48)
            sp.wait_ge(consts_loaded, 32)

        @block.scalar
        def _(act):
            for i in range(KB):
                if i >= 2:
                    act.wait_ge(butterfly, 8 * (i - 1))
                act.dma_start(wdn[:, i % 2, :], a["L0_ffn_W_down"][i * P:(i + 1) * P, :]).then_inc(wd_loaded[i % 2], 16)
                if i == 1:
                    act.wait_ge(cols_psum, 1)
                    nc.scalar.activation(silu_c[:, :, :].rearrange("p k b -> p (k b)"),
                                         bank[0][:, R_C:R_N], ACT.Silu).then_inc(silu_ready, 1)
                if i >= 1:
                    act.wait_ge(butterfly, 8 * i)
                    act.dma_start(t["wd_d"][i - 1], wdn[:, (i - 1) % 2, :]).then_inc(wd_stored[(i - 1) % 2], 16)
                    if i < KB - 1:
                        act.wait_ge(wd_stored[(i - 1) % 2], 16 * ((i - 1) // 2 + 1))
            act.wait_ge(butterfly, 8 * KB)
            act.dma_start(t["wd_d"][KB - 1], wdn[:, (KB - 1) % 2, :]).then_inc(wd_stored[(KB - 1) % 2], 16)
            for i in range(2):
                act.wait_ge(wd_stored[i], 16 * (KB // 2))

        @block.tensor
        def _(pe):
            pe.wait_ge(consts_loaded, 16)
            pe.wait_ge(rows_loaded, 16 * (6 + KB))
            nc.tensor.transpose(bank[0][:, 0:R_N], rows[0:R_N, :], t["ident"][0:R_N, 0:R_N]).then_inc(cols_psum, 1)
            pe.wait_ge(silu_ready, 1)
            pe.wait_ge(wmod_loaded, 16 * KB)
            for n, chunk in enumerate((0, 1, 3, 4)):
                for mb in range(KB):
                    for kb in range(KB):
                        last = nc.tensor.matmul(
                            bank[1][:, (n * KB + mb) * B:(n * KB + mb + 1) * B],
                            wmod[:, kb, chunk * H + mb * P:chunk * H + (mb + 1) * P], silu_c[:, kb, :],
                            start=kb == 0, stop=kb == KB - 1)
            last.then_inc(modc_psum, 1)
            for n, chunk in enumerate((2, 5)):
                for kb in range(KB):
                    last = nc.tensor.matmul(bank[2 + n][0:B, :], silu_c[:, kb, :],
                                            wmod[:, kb, chunk * H:(chunk + 1) * H],
                                            start=kb == 0, stop=kb == KB - 1)
                last.then_inc(gate_psum, 1)

        @block.vector
        def _(dve):
            chain = [0]

            def link(ins):
                chain[0] += 1
                ins.then_inc(vec_chain, 1)
                dve.wait_ge(vec_chain, chain[0])

            nc.vector.memset(t["neg_half"][:], -0.5)
            dve.wait_ge(cols_psum, 1)
            dve.wait_ge(silu_ready, 1)
            cols = t["cols"]
            link(nc.vector.tensor_copy(cols[:], bank[0][:, 0:R_N]))
            fs = t["ffn_scale"]
            link(nc.vector.tensor_scalar(fs[:, :, :], cols[:, R_WUG:R_WUG + 2 * IB].rearrange("p (n i) -> p n i", n=2),
                                         float(H) ** -0.5, None, ALU.mult))
            link(nc.vector.tensor_tensor(fs[:, 0, :], fs[:, 0, :], cols[:, R_SUD:R_SUD + IB], ALU.mult))
            dve.wait_ge(modc_psum, 1)
            modc = t["modc"]
            mp = bank[1][:, 0:4 * KB * B].rearrange("p (n k b) -> p n k b", n=4, k=KB)
            link(nc.vector.tensor_copy(modc[:, 0, :, :], mp[:, 0, :, :]))
            link(nc.vector.tensor_scalar(modc[:, 1, :, :], mp[:, 1, :, :], 1.0, None, ALU.add))
            link(nc.vector.tensor_copy(modc[:, 2, :, :], mp[:, 2, :, :]))
            link(nc.vector.tensor_scalar(modc[:, 3, :, :], mp[:, 3, :, :], 1.0, None, ALU.add))
            for n in (2, 3):
                for kb in range(KB):
                    link(nc.vector.tensor_scalar(modc[:, n, kb, :], modc[:, n, kb, :],
                                                 cols[:, R_SUU + kb:R_SUU + kb + 1], None, ALU.mult))
            dve.wait_ge(gate_psum, 2)
            for n in range(2):
                link(nc.vector.tensor_copy(gate[:, n, :], bank[2 + n][0:B, :]))
            link(nc.vector.tensor_scalar(gate_sign[:], gate[:], 0.0, 2.0, ALU.is_ge, ALU.mult))
            link(nc.vector.scalar_tensor_tensor(out=gate_abs[:], in0=gate[:], scalar=-1.0, in1=gate[:],
                                                op0=ALU.mult, op1=ALU.max))
            link(nc.vector.tensor_scalar(gate_abs[:], gate_abs[:], 0.25, None, ALU.max))
            link(nc.vector.scalar_tensor_tensor(out=gate[:], in0=gate_sign[:], scalar=-1.0, in1=gate_abs[:],
                                                op0=ALU.add, op1=ALU.mult))
            dve.wait_ge(gbias_loaded, 32)
            link(nc.vector.tensor_copy(gate_out[:, 0, :], gate[:, 0, :]))
            link(nc.vector.tensor_tensor(gate_out[:, 1, :], gate[:, 0, :], gate_bias[:, 0, :], ALU.mult))
            nc.vector.scalar_tensor_tensor(out=gate_out[:, 2, :], in0=gate[:, 1, :], scalar=float(INTER) ** -0.5,
                                           in1=gate_bias[:, 1, :], op0=ALU.mult, op1=ALU.mult).then_inc(gates_ready, 1)
            for i in range(KB):
                dve.wait_ge(wd_loaded[i % 2], 16 * (i // 2 + 1))
                src, dst = wdn[:, i % 2, :], wdm[:, i % 2, :]
                for s in range(4):
                    if i or s:
                        dve.wait_ge(butterfly, 8 * i + 2 * s)
                    n = P << s
                    v = src.rearrange("p (m a n) -> p m a n", a=2, n=n)
                    w = dst.rearrange("p (m a n) -> p m a n", a=2, n=n)
                    nc.vector.tensor_tensor(w[:, :, 0, :], v[:, :, 0, :], v[:, :, 1, :], ALU.add).then_inc(butterfly, 1)
                    nc.vector.tensor_tensor(w[:, :, 1, :], v[:, :, 0, :], v[:, :, 1, :], ALU.subtract).then_inc(butterfly, 1)
                    src, dst = dst, src


def stage_attention(nc, a, sem, bank, t):
    ctx = ExitStack()
    with ctx:
        def sb(name, shape, dt=F32):
            return ctx.enter_context(nc.sbuf_tensor(name, shape, dt))

        w_hi = [sb(f"w{n}_hi", [P, KB, H], F32R) for n in "qkv"]
        w_lo = [sb(f"w{n}_lo", [P, KB, H], F32R) for n in "qkv"]
        rope = [sb(f"rope_{n}", [P, T]) for n in ("qcos", "qsin", "kcos", "ksin")]
        xt = sb("xt", [P, NT, H])
        stats = sb("stats", [P, NT, 6])
        mean_var = sb("mean_var", [P, NT, 2])
        var_eps = sb("var_eps", [P, NT])
        rstd = sb("rstd", [P, NT])
        ht_f = sb("ht_f", [P, 2, T])
        ht_hi = sb("ht_hi", [P, KB, T], F32R)
        ht_lo = sb("ht_lo", [P, KB, T], F32R)
        qk_raw = sb("qk_raw", [P, 2, T])
        qk_swap = sb("qk_swap", [P, 2, T])
        qk_rot = sb("qk_rot", [P, 2, T])
        qk_parts = sb("qk_parts", [P, 4, T], F32R)
        stack = sb("stack", [P, 2, 2, HG, T], F32R)
        v_wide = sb("v_wide", [P, T])
        v_sb = sb("v_sb", [P, 2, NT, P])
        probs = sb("probs", [P, 4, T])
        probs_t = [sb(f"probs_t{pair}", [P, HG, 2 * (pair + 1), 2 * P]) for pair in range(2)]
        neg_max = sb("neg_max", [P, 2, U])
        row_sum = sb("row_sum", [P, 2, U])
        row_inv = sb("row_inv", [P, U])
        inv_wide = sb("inv_wide", [P, NT, HG, HS])
        inv_t = sb("inv_t", [P, T])
        attn_out = sb("attn_out", [P, 2, T])

        s_bank, pt_bank, pr, tr, vo = bank[0:3], bank[3:5], bank[5], bank[6], bank[7]
        NPT, NPB = len(pt_bank), 4
        s_of = [u % 3 for u in range(U - 1)] + [1]
        s_back = [next(d for d in range(1, U) if s_of[(u - d) % U] == s_of[u]) for u in range(U)]
        S_FREE = max(s_back)

        names = ("w_loaded0 w_loaded1 w_loaded2 tables_loaded w_split_hi w_split_lo x_loaded stats_done aggr_done "
                 "vareps_done rstd_done normed pr_done pr_free tr_done tr_free ht_hi_done ht_split swapped "
                 "sin_done cos_done rotated qk_hi_done qk_split stacked0 stacked1 sc_done neg_max_done "
                 "exp_done masked pt_psum pt_done av_done vo_free inv_done wide_done attn_stored0 attn_stored1 "
                 "act_passed dve_passed pool_passed")
        s = {n: sem("b_" + n) for n in names.split()}
        block = ctx.enter_context(nc.Block())
        swap_pairs = [j ^ 1 for j in range(32)]
        raw_b = probs_t[1][:].rearrange("p (i h) j n -> p i (h j n)", i=2)
        w_raw = (probs[:], raw_b[:, 0, :].rearrange("p (k n) -> p k n", k=KB),
                 raw_b[:, 1, :].rearrange("p (k n) -> p k n", k=KB))
        last_b = B - 1
        x_by_batch = a["L0_attn_x"].rearrange("b (t p) h -> b p t h", p=P)
        SENT = 3 * HG * 16

        V_AT, Q_AT, K_AT, PARTS = 0, 8, 12, 3
        V_TURN = U - 1
        TURN, EVAC = 1, 2
        SUMS = (11, 2)
        R_AT = 3
        OUT_AT = SUMS[1] + NT + 1
        LT_GROUP, LT_AT = G - 2, 4
        STATS_AT, NORM_AT = (4, 8, 9, 10), (14, 15, 16, 17)
        ROTATE = OUT_AT + 1

        def on_loop(engine, step, tail):
            for u in range(ROTATE):
                step(0, 0, u, True, False)
            with engine.Fori(0, last_b) as b:
                for g in range(G):
                    for u in range(U):
                        if g or u >= ROTATE:
                            step(b, g, u, False, False)
                for u in range(ROTATE):
                    step(b + 1, 0, u, False, False)
            for g in range(G):
                for u in range(U):
                    if g or u >= ROTATE:
                        step(last_b, g, u, False, True)
            for u in range(ROTATE):
                tail(u)

        def pr_use(kind, m):
            return 3 * m + "qkv".index(kind)

        def tr_use(b, g, kind, last=False, kb=0):
            lt = 0 if last else KB
            off = {"r": 0 + (lt if g > LT_GROUP else 0), "lt": 1 + kb, "v": 1 + (lt if g >= LT_GROUP else 0)}[kind]
            return b * (2 * G + KB) + KB + 2 * g + off

        def v_turned(b, g, last=False):
            if g:
                return tr_use(b, g - 1, "v", last) + 2
            return tr_use(b, 0, "r") + 1

        TR_FINAL = tr_use(last_b, G - 1, "r", True) + 1

        def sent(b, g):
            return (b * (G // 2) + g // 2 + 1) * SENT

        def stored_before(b, g):
            return (b * (G // 2) + (g - 1) // 2) * 16 + 1

        @block.sync
        def _(sp):
            sp.sem_inc(s["attn_stored0"], 1)
            sp.sem_inc(s["attn_stored1"], 1)
            sp.dma_start(xt[:], x_by_batch[0]).then_inc(s["x_loaded"], 16)
            for w, name in enumerate(("L0_attn_Wq", "L0_attn_Wk", "L0_attn_Wv")):
                sp.dma_start(w_raw[w], a[name].rearrange("(k p) n -> p k n", p=P)).then_inc(s[f"w_loaded{w}"], 16)
            for n, r in zip(("qcos", "qsin", "kcos", "ksin"), rope):
                sp.dma_start(r[:], a[n]).then_inc(s["tables_loaded"], 16)

            def send(m, slot, after_scores):
                sp.wait_ge(s["qk_split"], 2 * m + 4)
                if after_scores:
                    sp.wait_ge(s["sc_done"], (m - 1) * U + 1)
                for h in range(HG):
                    hs = slice(h * HS, (h + 1) * HS)
                    for r, parts in enumerate((slice(0, 3, 2), slice(0, 4, 3), slice(1, 3))):
                        sp.dma_start(stack[r * HS:(r + 1) * HS, slot, :, h, :].bitcast(F32),
                                     qk_parts[hs, parts, :].bitcast(F32)).then_inc(s[f"stacked{slot}"], 16)

            send(0, 0, False)

            def batch(b, last):
                for g in range(G):
                    if not (last and g == G - 1):
                        send(b * G + g + 1, (g + 1) % 2, True)
                    if g == 0 and not last:
                        sp.wait_ge(s["tr_done"], b * (2 * G + KB) + KB)
                        sp.dma_start(xt[:], x_by_batch[b + 1]).then_inc(s["x_loaded"], 16)
                    sp.wait_ge(s["vo_free"], b * G + g + 2)
                    sp.dma_start(t["attn_d"][b, g], attn_out[:, g % 2, :]).then_inc(s[f"attn_stored{g % 2}"], 16)

            with sp.Fori(0, last_b) as b:
                batch(b, False)
            batch(last_b, True)
            for i in range(2):
                sp.wait_ge(s[f"attn_stored{i}"], 16 * B * G // 2 + 1)

        @block.tensor
        def _(pe):
            def project(w, g, part, parts):
                cs = slice(g * P, (g + 1) * P)
                passes = [(kb, wt, ht) for kb in range(KB) for wt, ht in
                          ((w_hi[w], ht_hi), (w_hi[w], ht_lo), (w_lo[w], ht_hi))]
                n = len(passes) // parts
                for i in range(part * n, (part + 1) * n):
                    kb, wt, ht = passes[i]
                    ins = nc.tensor.matmul(pr[:], wt[:, kb, cs], ht[:, kb, :], start=i == 0, stop=i == len(passes) - 1)
                if part == parts - 1:
                    ins.then_inc(s["pr_done"], 1)

            def norm_transposes(kb):
                for tt in range(NT):
                    ins = nc.tensor.transpose(tr[:, tt * P:(tt + 1) * P], xt[:, tt, kb * P:(kb + 1) * P], t["ident"][:])
                ins.then_inc(s["tr_done"], 1)

            def v_transposes():
                for tt in range(NT):
                    ins = nc.tensor.transpose(tr[:, tt * P:(tt + 1) * P], v_wide[:, tt * P:(tt + 1) * P], t["ident"][:])
                ins.then_inc(s["tr_done"], 1)

            def r_transposes():
                for q in range(NT):
                    ins = nc.tensor.transpose(tr[:, q * P:(q + 1) * P],
                                              inv_wide[:, q, :, :].rearrange("p h d -> p (h d)"), t["ident"][:])
                ins.then_inc(s["tr_done"], 1)

            def scores(uu, slot, u):
                pe.wait_ge(s["exp_done"], uu + 1 + S_FREE - s_back[u])
                h, q = u % HG, u // HG
                nc.tensor.matmul(s_bank[s_of[u]][:], stack[0:3 * HS, slot, 0, h, q * P:(q + 1) * P],
                                 stack[0:3 * HS, slot, 1, h, :], start=True, stop=True).then_inc(s["sc_done"], 1)

            def sums(m, slot, pair, js):
                if js[0] == 0:
                    if pair == 0:
                        pe.wait_ge(s["vo_free"], m + 1)
                    pe.wait_ge(s["masked"], m * U + 2 * (pair + 1) * HG)
                end = 2 * pair + 1
                for j in js:
                    skip = P if j == end else 0
                    for h in range(HG):
                        hs = slice(h * HS, (h + 1) * HS)
                        ins = nc.tensor.matmul(vo[hs, 2 * pair * P + skip:2 * (pair + 1) * P], v_sb[:, slot, j, hs],
                                               probs_t[pair][:, h, j, skip:2 * P], start=j == 0, stop=j == end)
                if js[-1] == end:
                    ins.then_inc(s["av_done"], 1)

            def probs_transposes(uu, u):
                pe.wait_ge(s["exp_done"], uu + 1 + S_FREE)
                pe.wait_ge(s["pt_done"], uu + 1)
                for j in range(u // HG + 1):
                    ins = nc.tensor.transpose(pt_bank[u % NPT][:, j * P:(j + 1) * P],
                                              probs[:, u % NPB, j * P:(j + 1) * P], t["ident"][:])
                ins.then_inc(s["pt_psum"], 1)

            pe.sem_inc(s["pt_psum"], NPB)
            pe.sem_inc(s["av_done"], 2)
            pe.wait_ge(s["normed"], 1)
            for kb in range(KB):
                pe.wait_ge(s["tr_free"], kb + 1)
                norm_transposes(kb)
            pe.wait_ge(s["ht_split"], KB + 2)
            for i, (w, g) in enumerate(((0, 0), (1, 0), (2, 0), (0, 1), (1, 1))):
                pe.wait_ge(s["w_split_lo"], min(i + 1, 3))
                pe.wait_ge(s["pr_free"], i + 1)
                project(w, g, 0, 1)
            pe.wait_ge(s["pr_free"], pr_use("v", 0) + 2)
            pe.wait_ge(s["tr_free"], KB + 1)
            v_transposes()
            pe.wait_ge(s["stacked0"], sent(0, 0))
            scores(0, 0, 0)
            scores(1, 0, 1)

            def step(b, g, u, first, last):
                m, slot = b * G + g, g % 2
                uu = m * U + u
                if u < U - 2:
                    scores(uu + 2, slot, u + 2)
                elif not (last and g == G - 1):
                    if u == U - 2:
                        pe.wait_ge(s[f"stacked{1 - slot}"], sent(b, g + 1))
                    scores(uu + 2, 1 - slot, u + 2 - U)
                for w, at, ahead in ((0, Q_AT, 2), (1, K_AT, 2), (2, V_AT, 1)):
                    if at <= u < at + PARTS and not (last and g + ahead >= G):
                        part = u - at
                        if part == 0:
                            pe.wait_ge(s["pr_free"], pr_use("qkv"[w], m + ahead) + 1)
                        if w == 0 and g == LT_GROUP:
                            blocks = ((part + 1) * (3 * KB // PARTS) - 1) // 3 + 1
                            pe.wait_ge(s["ht_split"], (b + 1) * KB + blocks + 2)
                        project(w, (g + ahead) % G, part, PARTS)
                if u >= TURN or not first:
                    probs_transposes(uu - TURN, (u - TURN) % U)
                if SUMS[1] <= u < SUMS[1] + NT and not first:
                    sums(m - 1, 1 - slot, 1, (u - SUMS[1],))
                if u == SUMS[0]:
                    pe.wait_ge(s["tr_free"], v_turned(b, g, last))
                    sums(m, slot, 0, (0, 1))
                if u == R_AT and not first:
                    pe.wait_ge(s["wide_done"], m)
                    pe.wait_ge(s["tr_free"], tr_use(b, g, "r", last) + 1)
                    r_transposes()
                if g == LT_GROUP and not last and LT_AT <= u < LT_AT + KB:
                    kb = u - LT_AT
                    if kb == 0:
                        pe.wait_ge(s["normed"], b + 2)
                    pe.wait_ge(s["tr_free"], tr_use(b, g, "lt", last, kb) + 1)
                    norm_transposes(kb)
                if u == V_TURN and not (last and g == G - 1):
                    pe.wait_ge(s["pr_free"], pr_use("v", m + 1) + 2)
                    pe.wait_ge(s["tr_free"], tr_use(b, g, "v", last) + 1)
                    v_transposes()

            def tail(u):
                m = B * G
                if u < TURN:
                    probs_transposes(m * U + u - TURN, (u - TURN) % U)
                if u == SUMS[1]:
                    sums(m - 1, (G - 1) % 2, 1, range(NT))
                if u == R_AT:
                    pe.wait_ge(s["wide_done"], m)
                    pe.wait_ge(s["tr_free"], TR_FINAL + 1)
                    r_transposes()

            on_loop(pe, step, tail)

        @block.scalar
        def _(act):
            act.sem_inc(s["exp_done"], S_FREE)
            act.sem_inc(s["pt_done"], NPT)
            act.sem_inc(s["pr_free"], 1)
            act.sem_inc(s["tr_free"], 1)
            for w in range(3):
                act.wait_ge(s[f"w_loaded{w}"], 16)
                nc.scalar.activation(w_hi[w][:].rearrange("p k n -> p (k n)"),
                                     w_raw[w].rearrange("p h t -> p (h t)"), ACT.Copy).then_inc(s["w_split_hi"], 1)

            def evac_norm(b, kb, at):
                wait_apart(act, s["act_passed"], (s["tr_done"], at + 1), (s["ht_split"], b * KB + kb + 1))
                nc.scalar.activation(ht_f[:, kb % 2, :], tr[:], ACT.Identity, bias=t["modc"][:, 0, kb, bass.ds(b, 1)],
                                     scale=t["modc"][:, 1, kb, bass.ds(b, 1)]).then_inc(s["tr_free"], 1)

            def evac_qk(m, which, g):
                act.wait_ge(s["pr_done"], pr_use("qk"[which], m) + 1)
                act.wait_ge(s["qk_split"], 2 * m + which + 1)
                col = (R_BQ, R_BK)[which] + g
                nc.scalar.activation(qk_raw[:, which, :], pr[:], ACT.Identity,
                                     bias=t["cols"][:, col:col + 1]).then_inc(s["pr_free"], 1)

            def evac_v(m, g):
                act.wait_ge(s["pr_done"], pr_use("v", m) + 1)
                nc.scalar.activation(v_wide[:], pr[:], ACT.Identity,
                                     bias=t["cols"][:, R_BV + g:R_BV + g + 1]).then_inc(s["pr_free"], 1)

            def evac_turned(slot, at):
                act.wait_ge(s["tr_done"], at + 1)
                nc.scalar.activation(v_sb[:, slot, :, :].rearrange("p t n -> p (t n)"), tr[:],
                                     ACT.Copy).then_inc(s["tr_free"], 1)

            def evac_inv(at):
                act.wait_ge(s["tr_done"], at + 1)
                nc.scalar.activation(inv_t[:], tr[:], ACT.Copy).then_inc(s["tr_free"], 1)

            def evac_probs(m, uu, u):
                q, h = u // HG, u % HG
                act.wait_ge(s["pt_psum"], uu + 1 + NPB)
                if u in (0, 2 * HG):
                    act.wait_ge(s["av_done"], 2 * m + q // 2 + 1)
                nc.scalar.activation(probs_t[q // 2][:, h, 0:q + 1, q % 2 * P:(q % 2 + 1) * P],
                                     pt_bank[u % NPT][:, 0:(q + 1) * P].rearrange("p (j n) -> p j n", n=P),
                                     ACT.Copy).then_inc(s["pt_done"], 1)

            for kb in range(KB):
                evac_norm(0, kb, kb)
            evac_qk(0, 0, 0)
            evac_qk(0, 1, 0)
            evac_v(0, 0)
            evac_qk(1, 0, 1)
            evac_qk(1, 1, 1)
            evac_turned(0, KB)

            def step(b, g, u, first, last):
                m = b * G + g
                uu = m * U + u
                act.wait_ge(s["neg_max_done"], uu + 1)
                act.wait_ge(s["pt_psum"], uu + 1)
                nc.scalar.activation(probs[:, u % NPB, :], s_bank[s_of[u]][:], ACT.Exp,
                                     bias=neg_max[:, g % 2, u:u + 1],
                                     accum_out=row_sum[:, g % 2, u:u + 1]).then_inc(s["exp_done"], 1)
                if u >= EVAC:
                    evac_probs(m, uu - EVAC, u - EVAC)
                elif not first:
                    evac_probs(m - 1, uu - EVAC, u - EVAC + U)
                for at, which, ahead in ((K_AT + PARTS, 1, 2), (V_AT + PARTS, 2, 1), (Q_AT + PARTS, 0, 2)):
                    if u == at and not (last and g + ahead >= G):
                        if which == 2:
                            evac_v(m + 1, (g + 1) % G)
                        else:
                            evac_qk(m + ahead, which, (g + ahead) % G)
                if u == R_AT + 1 and not first:
                    evac_inv(tr_use(b, g, "r", last))
                if g == LT_GROUP and not last and LT_AT < u <= LT_AT + KB:
                    kb = u - LT_AT - 1
                    evac_norm(b + 1, kb, tr_use(b, g, "lt", last, kb))
                if u == 0 and not first:
                    evac_turned(g % 2, v_turned(b, g, last) - 2)

            def tail(u):
                if u < EVAC:
                    evac_probs(B * G - 1, B * G * U + u - EVAC, u - EVAC + U)
                if u == R_AT + 1:
                    evac_inv(TR_FINAL)

            on_loop(act, step, tail)

        @block.vector
        def _(dve):
            dve.sem_inc(s["vo_free"], 1)
            dve.sem_inc(s["ht_split"], 2)
            dve.sem_inc(s["qk_split"], 2)

            def norm_stats(b, tt):
                if tt == 0:
                    dve.wait_ge(s["x_loaded"], (b + 1) * 16)
                nc.vector.bn_stats(stats[:, tt, :], xt[:, tt, :]).then_inc(s["stats_done"], 1)

            def norm_aggregate(b):
                wait_apart(dve, s["dve_passed"], (s["stats_done"], (b + 1) * NT))
                for tt in range(NT):
                    nc.vector.bn_aggr(mean_var[:, tt, :], stats[:, tt, :]).then_inc(s["aggr_done"], 1)
                dve.wait_ge(s["aggr_done"], (b + 1) * NT)
                nc.vector.tensor_scalar(var_eps[:], mean_var[:, :, 1], EPS, None, ALU.add).then_inc(s["vareps_done"], 1)

            def normalize(b, tt):
                if tt == 0:
                    dve.wait_ge(s["rstd_done"], b + 1)
                ins = nc.vector.tensor_scalar(xt[:, tt, :], xt[:, tt, :], mean_var[:, tt, 0:1], rstd[:, tt:tt + 1],
                                              ALU.subtract, ALU.mult)
                if tt == NT - 1:
                    ins.then_inc(s["normed"], 1)

            def split_norm(b, kb, at):
                dve.wait_ge(s["tr_free"], at + 2)
                nc.vector.tensor_copy(ht_hi[:, kb, :], ht_f[:, kb % 2, :]).then_inc(s["ht_hi_done"], 1)
                dve.wait_ge(s["ht_hi_done"], b * KB + kb + 1)
                nc.vector.tensor_tensor(ht_lo[:, kb, :], ht_f[:, kb % 2, :], ht_hi[:, kb, :].bitcast(F32),
                                        ALU.subtract).then_inc(s["ht_split"], 1)

            def rope_swap(m, which):
                wait_apart(dve, s["dve_passed"], (s["pr_free"], pr_use("qk"[which], m) + 2))
                nc.vector.stream_shuffle(qk_swap[:, which, :], qk_raw[:, which, :], swap_pairs).then_inc(s["swapped"], 1)

            def rope_sin(m, which):
                dve.wait_ge(s["swapped"], 2 * m + which + 1)
                nc.vector.tensor_tensor(qk_swap[:, which, :], qk_swap[:, which, :], rope[2 * which + 1][:],
                                        ALU.mult).then_inc(s["sin_done"], 1)

            def rope_hi(m, which, slot, copied):
                dve.wait_ge(s["rotated"], 2 * m + which + 1)
                if copied is not None:
                    dve.wait_ge(s[f"stacked{slot}"], copied)
                nc.vector.tensor_copy(qk_parts[:, 2 * which, :], qk_rot[:, which, :]).then_inc(s["qk_hi_done"], 1)

            def rope_lo(m, which):
                dve.wait_ge(s["qk_hi_done"], 2 * m + which + 1)
                nc.vector.tensor_tensor(qk_parts[:, 2 * which + 1, :], qk_rot[:, which, :],
                                        qk_parts[:, 2 * which, :].bitcast(F32), ALU.subtract).then_inc(s["qk_split"], 1)

            def inverse(m, slot):
                dve.wait_ge(s["exp_done"], m * U + U + S_FREE)
                nc.vector.reciprocal(row_inv[:], row_sum[:, slot, :]).then_inc(s["inv_done"], 1)
                wait_apart(dve, s["dve_passed"], (s["inv_done"], m + 1))
                nc.vector.tensor_copy(
                    inv_wide[:], row_inv[:].rearrange("p (q h) -> p q h", h=HG).unsqueeze(3)
                    .to_broadcast([P, NT, HG, HS])).then_inc(s["wide_done"], 1)

            def normalize_output(m, slot, stored, at):
                dve.wait_ge(s["tr_free"], at + 2)
                dve.wait_ge(s["av_done"], 2 * m + 4)
                dve.wait_ge(s[f"attn_stored{slot}"], stored)
                nc.vector.tensor_tensor(attn_out[:, slot, :], vo[:], inv_t[:], ALU.mult).then_inc(s["vo_free"], 1)

            for tt in range(NT):
                norm_stats(0, tt)
            norm_aggregate(0)
            for tt in range(NT):
                normalize(0, tt)
            for w in range(3):
                dve.wait_ge(s["w_split_hi"], w + 1)
                nc.vector.tensor_tensor(w_lo[w][:].rearrange("p k n -> p (k n)"), w_raw[w].rearrange("p h t -> p (h t)"),
                                        w_hi[w][:].rearrange("p k n -> p (k n)").bitcast(F32),
                                        ALU.subtract).then_inc(s["w_split_lo"], 1)
            for kb in range(KB):
                split_norm(0, kb, kb)
            dve.wait_ge(s["tables_loaded"], 16 * 4)
            for which in range(2):
                rope_swap(0, which)
                rope_sin(0, which)
                rope_hi(0, which, 0, None)
                rope_lo(0, which)
            rope_swap(1, 0)
            rope_sin(1, 0)
            rope_hi(1, 0, 0, sent(0, 0))

            def step(b, g, u, first, last):
                m = b * G + g
                uu = m * U + u
                dve.wait_ge(s["sc_done"], uu + 1)
                nc.vector.tensor_reduce(neg_max[:, g % 2, u:u + 1], s_bank[s_of[u]][:], AX.X, ALU.max,
                                        negate=True).then_inc(s["neg_max_done"], 1)
                if not (last and g >= G - 2):
                    if u == Q_AT + PARTS + 1:
                        rope_swap(m + 2, 0)
                    if u == Q_AT + PARTS + 2:
                        rope_sin(m + 2, 0)
                    if u == U - 1:
                        rope_hi(m + 2, 0, (g + 1) % 2, sent(b, g + 1))
                if not (last and g == G - 1):
                    if u == 0:
                        rope_lo(m + 1, 0)
                    if u == 2:
                        rope_swap(m + 1, 1)
                    if u == 3:
                        rope_sin(m + 1, 1)
                    if u == 5:
                        rope_hi(m + 1, 1, g % 2, sent(b, g))
                    if u == 6:
                        rope_lo(m + 1, 1)
                if u == 1 and not first:
                    inverse(m - 1, 1 - g % 2)
                if u == OUT_AT and not first:
                    normalize_output(m - 1, 1 - g % 2, stored_before(b, g), tr_use(b, g, "r", last))
                if not last:
                    turn = (g - LT_GROUP + 1) * U + u
                    if turn in STATS_AT:
                        norm_stats(b + 1, STATS_AT.index(turn))
                    if turn == STATS_AT[-1] + 1:
                        norm_aggregate(b + 1)
                    if turn in NORM_AT:
                        normalize(b + 1, NORM_AT.index(turn))
                    if g == LT_GROUP and LT_AT + 1 < u <= LT_AT + 1 + KB:
                        kb = u - LT_AT - 2
                        split_norm(b + 1, kb, tr_use(b, g, "lt", last, kb))

            def tail(u):
                if u == 1:
                    inverse(B * G - 1, (G - 1) % 2)
                if u == OUT_AT:
                    normalize_output(B * G - 1, (G - 1) % 2, stored_before(B, 0), TR_FINAL)

            on_loop(dve, step, tail)

        @block.gpsimd
        def _(pool):
            def power(b):
                pool.wait_ge(s["vareps_done"], b + 1)
                nc.gpsimd.tensor_tensor(rstd[:], var_eps[:], t["neg_half"][:], ALU.pow).then_inc(s["rstd_done"], 1)

            def rope_cos(m, which):
                pool.wait_ge(s["pr_free"], pr_use("qk"[which], m) + 2)
                nc.gpsimd.tensor_tensor(qk_rot[:, which, :], qk_raw[:, which, :], rope[2 * which][:],
                                        ALU.mult).then_inc(s["cos_done"], 1)

            def rope_add(m, which):
                pool.wait_ge(s["sin_done"], 2 * m + which + 1)
                pool.wait_ge(s["cos_done"], 2 * m + which + 1)
                nc.gpsimd.tensor_tensor(qk_rot[:, which, :], qk_rot[:, which, :], qk_swap[:, which, :],
                                        ALU.add).then_inc(s["rotated"], 1)

            def mask(uu, u):
                q, h = u // HG, u % HG
                wait_apart(pool, s["pool_passed"], (s["pt_done"], uu + 1 + NPT))
                v = probs_t[q // 2][:, h, q, q % 2 * P:(q % 2 + 1) * P]
                nc.gpsimd.affine_select(out=v, in_=v, compare_op=ALU.is_ge, fill=0.0, base=0,
                                        pattern=[[1, P]], channel_multiplier=-1).then_inc(s["masked"], 1)

            power(0)
            pool.wait_ge(s["tables_loaded"], 16 * 4)
            for which in range(2):
                rope_cos(0, which)
                rope_add(0, which)
            rope_cos(1, 0)
            rope_add(1, 0)

            def step(b, g, u, first, last):
                m = b * G + g
                uu = m * U + u
                if u >= EVAC or not first:
                    mask(uu - EVAC, (u - EVAC) % U)
                if not (last and g >= G - 2):
                    if u == Q_AT + PARTS + 1:
                        rope_cos(m + 2, 0)
                    if u == Q_AT + PARTS + 2:
                        rope_add(m + 2, 0)
                if not (last and g == G - 1):
                    if u == 1:
                        rope_cos(m + 1, 1)
                    if u == 3:
                        rope_add(m + 1, 1)
                if not last and g == LT_GROUP - 1 and u == STATS_AT[-1] + 2:
                    power(b + 1)

            def tail(u):
                if u < EVAC:
                    mask(B * G * U + u - EVAC, u - EVAC + U)

            on_loop(pool, step, tail)


def stage_project(nc, a, sem, bank, t):
    ctx = ExitStack()
    with ctx:
        def sb(name, shape, dt=F32):
            return ctx.enter_context(nc.sbuf_tensor(name, shape, dt))

        wo_raw = sb("wo_raw", [P, KB, H])
        wo_hi = sb("wo_hi", [P, KB, H], F32R)
        wo_lo = sb("wo_lo", [P, KB, H], F32R)
        ot = sb("ot", [P, KB, T])
        ot_hi = sb("ot_hi", [P, KB, T], F32R)
        ot_lo = sb("ot_lo", [P, KB, T], F32R)
        gates = sb("gates", [P, 2, H])
        xr = sb("xr", [P, NT, H])
        gated = sb("gated", [P, 2, H])
        x1 = sb("x1", [P, NT, H])
        xn = sb("xn", [P, NT, H])
        stats = sb("stats2", [P, NT, 6])
        mean_var = sb("mean_var2", [P, NT, 2])
        var_eps = sb("var_eps2", [P, NT])
        rstd = sb("rstd2", [P, NT])
        z = sb("z", [P, KB, T])
        z2 = sb("z2", [P, KB, T])
        y_bank, tr_bank, h_bank = bank[0:NT], bank[4:6], bank[6:8]

        names = ("wo_loaded wo_hi_done wo_split ot_loaded gates_loaded x_loaded ot_hi_done ot_split y_psum "
                 "gated_done x1_done x_biased stats_done vareps_done rstd_done normed x1_stored tr_psum tr_free "
                 "fly1 fly2 h_psum hi_done h_free aggr_done act_passed dve_passed")
        s = {n: sem("c_" + n) for n in names.split()}
        block = ctx.enter_context(nc.Block())
        x_by_batch = a["L0_attn_x"].rearrange("b (t p) h -> b p t h", p=P)
        attn_by_batch = t["attn_d"].rearrange("b g p t -> b p g t")
        x1_by_batch = t["x1_d"].rearrange("b t p h -> b p t h")
        rows_by_batch = t["mod_rows_d"].rearrange("i b h -> b i h")

        @block.sync
        def _(sp):
            sp.dma_start(wo_raw[:], a["L0_attn_Wo"].rearrange("(k p) n -> p k n", p=P)).then_inc(s["wo_loaded"], 16)

            def load(b):
                sp.dma_start(ot[:], attn_by_batch[b]).then_inc(s["ot_loaded"], 16)
                sp.dma_start(xr[:], x_by_batch[b]).then_inc(s["x_loaded"], 16)
                sp.dma_start(gates[:], rows_by_batch[b, 0:2].partition_broadcast(P)).then_inc(s["gates_loaded"], 16)

            sp.sem_inc(s["x1_stored"], 1)
            load(0)
            with sp.Fori(0, B - 1) as b:
                sp.wait_ge(s["x1_done"], (b + 1) * NT)
                sp.dma_start(x1_by_batch[b], x1[:]).then_inc(s["x1_stored"], 16)
                load(b + 1)
            sp.wait_ge(s["x1_done"], B * NT)
            sp.dma_start(x1_by_batch[B - 1], x1[:]).then_inc(s["x1_stored"], 16)
            sp.wait_ge(s["x1_stored"], B * 16 + 1)

        @block.tensor
        def _(pe):
            pe.wait_ge(s["wo_split"], 1)

            def output(b):
                pe.wait_ge(s["ot_split"], b + 1)
                for tt in range(NT):
                    ts = slice(tt * P, (tt + 1) * P)
                    pe.wait_ge(s["gated_done"], b * NT + tt + 1)
                    for kb in range(KB):
                        for n, (ot_, wo_) in enumerate(((ot_hi, wo_hi), (ot_lo, wo_hi), (ot_hi, wo_lo))):
                            ins = nc.tensor.matmul(y_bank[tt][:], ot_[:, kb, ts], wo_[:, kb, :],
                                                   start=kb == 0 and n == 0, stop=kb == KB - 1 and n == 2)
                    ins.then_inc(s["y_psum"], 1)

            def transposes(b):
                pe.wait_ge(s["normed"], b + 1)
                for kb in range(KB):
                    pe.wait_ge(s["tr_free"], b * KB + kb + 1)
                    for tt in range(NT):
                        ins = nc.tensor.transpose(tr_bank[kb % 2][:, tt * P:(tt + 1) * P],
                                                  xn[:, tt, kb * P:(kb + 1) * P], t["ident"][:])
                    ins.then_inc(s["tr_psum"], 1)

            def hadamard_128(b):
                pe.wait_ge(s["fly2"], b * 2 + 2)
                for kb in range(KB):
                    pe.wait_ge(s["h_free"], b * KB + kb + 1)
                    nc.tensor.matmul(h_bank[kb % 2][:], t["had"][:], z[:, kb, :], start=True,
                                     stop=True).then_inc(s["h_psum"], 1)

            output(0)
            with pe.Fori(0, B - 1) as b:
                transposes(b)
                output(b + 1)
                hadamard_128(b)
            transposes(B - 1)
            hadamard_128(B - 1)

        @block.scalar
        def _(act):
            act.sem_inc(s["tr_free"], 2)
            act.wait_ge(s["wo_loaded"], 16)
            nc.scalar.activation(wo_hi[:], wo_raw[:], ACT.Copy).then_inc(s["wo_hi_done"], 1)

            def split_hi(b):
                act.wait_ge(s["ot_loaded"], (b + 1) * 16)
                nc.scalar.activation(ot_hi[:], ot[:], ACT.Copy).then_inc(s["ot_hi_done"], 1)

            def evacuate(b):
                for kb in range(KB):
                    wait_apart(act, s["act_passed"], (s["tr_psum"], b * KB + kb + 1))
                    nc.scalar.activation(z[:, kb, :], tr_bank[kb % 2][:], ACT.Identity,
                                         bias=t["modc"][:, 2, kb, bass.ds(b, 1)],
                                         scale=t["modc"][:, 3, kb, bass.ds(b, 1)]).then_inc(s["tr_free"], 1)
                for kb in range(KB):
                    wait_apart(act, s["act_passed"], (s["h_psum"], b * KB + kb + 1))
                    nc.scalar.activation(t["h2_hi"][:, kb, bass.ds(b * T, T)], h_bank[kb % 2][:],
                                         ACT.Copy).then_inc(s["hi_done"], 1)

            split_hi(0)
            with act.Fori(0, B - 1) as b:
                split_hi(b + 1)
                evacuate(b)
            evacuate(B - 1)

        @block.vector
        def _(dve):
            dve.sem_inc(s["gated_done"], NT)
            dve.sem_inc(s["h_free"], 2)
            dve.wait_ge(s["wo_hi_done"], 1)
            nc.vector.tensor_tensor(wo_lo[:], wo_raw[:], wo_hi[:].bitcast(F32), ALU.subtract).then_inc(s["wo_split"], 1)

            def split(b):
                dve.wait_ge(s["ot_hi_done"], b + 1)
                nc.vector.tensor_tensor(ot_lo[:], ot[:], ot_hi[:].bitcast(F32), ALU.subtract).then_inc(s["ot_split"], 1)

            def residual(b):
                dve.wait_ge(s["gates_loaded"], (b + 1) * 16)
                dve.wait_ge(s["x_biased"], b + 1)
                for tt in range(NT):
                    dve.wait_ge(s["y_psum"], b * NT + tt + 1)
                    nc.vector.tensor_tensor(gated[:, tt % 2, :], y_bank[tt][:], gates[:, 0, :],
                                            ALU.mult).then_inc(s["gated_done"], 1)
                    dve.wait_ge(s["gated_done"], b * NT + tt + 1 + NT)
                    if tt == 0:
                        dve.wait_ge(s["x1_stored"], b * 16 + 1)
                    nc.vector.tensor_tensor(x1[:, tt, :], gated[:, tt % 2, :], xr[:, tt, :],
                                            ALU.add).then_inc(s["x1_done"], 1)
                for tt in range(NT):
                    dve.wait_ge(s["x1_done"], b * NT + tt + 1)
                    nc.vector.bn_stats(stats[:, tt, :], x1[:, tt, :]).then_inc(s["stats_done"], 1)
                wait_apart(dve, s["dve_passed"], (s["stats_done"], (b + 1) * NT))
                for tt in range(NT):
                    nc.vector.bn_aggr(mean_var[:, tt, :], stats[:, tt, :]).then_inc(s["aggr_done"], 1)
                dve.wait_ge(s["aggr_done"], (b + 1) * NT)
                nc.vector.tensor_scalar(var_eps[:], mean_var[:, :, 1], EPS, None, ALU.add).then_inc(s["vareps_done"], 1)
                dve.wait_ge(s["rstd_done"], b + 1)
                for tt in range(NT):
                    ins = nc.vector.tensor_scalar(xn[:, tt, :], x1[:, tt, :], mean_var[:, tt, 0:1], rstd[:, tt:tt + 1],
                                                  ALU.subtract, ALU.mult)
                ins.then_inc(s["normed"], 1)

            def transform(b):
                dve.wait_ge(s["tr_free"], (b + 1) * KB + 2)
                v = z[:].rearrange("p (m a) n -> p m a n", a=2)
                w = z2[:].rearrange("p (m a) n -> p m a n", a=2)
                nc.vector.tensor_tensor(w[:, :, 0, :], v[:, :, 0, :], v[:, :, 1, :], ALU.add).then_inc(s["fly1"], 1)
                nc.vector.tensor_tensor(w[:, :, 1, :], v[:, :, 0, :], v[:, :, 1, :], ALU.subtract).then_inc(s["fly1"], 1)
                dve.wait_ge(s["fly1"], b * 2 + 2)
                nc.vector.tensor_tensor(z[:, 0:2, :], z2[:, 0:2, :], z2[:, 2:4, :], ALU.add).then_inc(s["fly2"], 1)
                nc.vector.tensor_tensor(z[:, 2:4, :], z2[:, 0:2, :], z2[:, 2:4, :], ALU.subtract).then_inc(s["fly2"], 1)

            def split_transform(b):
                for kb in range(KB):
                    dve.wait_ge(s["hi_done"], b * KB + kb + 1)
                    cs = bass.ds(b * T, T)
                    nc.vector.tensor_tensor(t["h2_lo"][:, kb, cs], h_bank[kb % 2][:], t["h2_hi"][:, kb, cs].bitcast(F32),
                                            ALU.subtract).then_inc(s["h_free"], 1)

            split(0)
            with dve.Fori(0, B - 1) as b:
                residual(b)
                split(b + 1)
                transform(b)
                split_transform(b)
            residual(B - 1)
            transform(B - 1)
            split_transform(B - 1)

        @block.gpsimd
        def _(pool):
            with pool.Fori(0, B) as b:
                pool.wait_ge(s["x_loaded"], (b + 1) * 16)
                pool.wait_ge(s["gates_loaded"], (b + 1) * 16)
                for tt in range(NT):
                    ins = nc.gpsimd.tensor_tensor(xr[:, tt, :], xr[:, tt, :], gates[:, 1, :], ALU.add)
                ins.then_inc(s["x_biased"], 1)
                pool.wait_ge(s["vareps_done"], b + 1)
                nc.gpsimd.tensor_tensor(rstd[:], var_eps[:], t["neg_half"][:], ALU.pow).then_inc(s["rstd_done"], 1)


def stage_ffn(nc, a, sem, bank, t):
    ctx = ExitStack()
    with ctx:
        def sb(name, shape, dt=F32):
            return ctx.enter_context(nc.sbuf_tensor(name, shape, dt))

        raw = sb("raw", [P, 2, KB, H])
        wug_hi = sb("wug_hi", [P, 2, KB, QB * P], F32R)
        wug_lo = sb("wug_lo", [P, 2, KB, QB * P], F32R)
        wd_t = sb("wd_t", [P, H])
        wd_hi = sb("wd_hi", [P, QB, H], F32R)
        wd_lo = sb("wd_lo", [P, QB, H], F32R)
        act_f = sb("act_f", [P, 2, T])
        act_hi = sb("act_hi", [P, 2, QB, T], F32R)
        act_lo = sb("act_lo", [P, 2, QB, T], F32R)
        acc = sb("acc", [P, B * NT, H])
        out_gate = sb("out_gate", [P, 2, H])
        g_bank, u_bank, y_bank, prep_bank = bank[0:2], bank[2:4], bank[4:6], bank[6:8]

        names = ("up_loaded gate_loaded down_loaded prep_psum prep_hi prep_lo wdt_done g_psum u_psum silu_done "
                 "act_done act_hi_done act_split y_psum acc_done acc_zero og_loaded0 og_loaded1 x1_loaded0 x1_loaded1 "
                 "out_gated out_done out_stored act_passed")
        s = {n: sem("d_" + n) for n in names.split()}
        block = ctx.enter_context(nc.Block())
        PREP_PSUM = 2 * QB + 2 * QB
        PREP_SPLIT = 2 * QB + QB
        fs = t["ffn_scale"]
        up_rows = a["L0_ffn_W_up"].rearrange("(q i p) h -> q p i h", q=NQ, p=P)
        gate_rows = a["L0_ffn_W_gate"].rearrange("(q i p) h -> q p i h", q=NQ, p=P)
        down_cols = t["wd_d"].rearrange("k p (q n) -> q p k n", q=NQ)
        x1_by_batch = t["x1_d"].rearrange("b t p h -> b p t h")
        out_by_batch = a["out"].rearrange("b (t p) h -> b p t h", p=P)

        @block.sync
        def _(sp):
            def load_up_gate(q):
                sp.dma_start(raw[:, 0, :, :], up_rows[q]).then_inc(s["up_loaded"], 16)
                sp.dma_start(raw[:, 1, :, :], gate_rows[q]).then_inc(s["gate_loaded"], 16)

            def load_down(q):
                sp.wait_ge(s["prep_psum"], q * PREP_PSUM + QB)
                sp.dma_start(raw[:, 0, :, :], down_cols[q]).then_inc(s["down_loaded"], 16)

            load_up_gate(0)
            load_down(0)
            with sp.Fori(1, NQ) as q:
                sp.wait_ge(s["prep_psum"], q * PREP_PSUM)
                load_up_gate(q)
                load_down(q)
            sp.wait_ge(s["prep_psum"], NQ * PREP_PSUM)
            for b in range(B):
                if b >= 2:
                    sp.wait_ge(s["out_done"], (b - 1) * NT)
                sp.dma_start(raw[:, b % 2, :, :], x1_by_batch[b]).then_inc(s[f"x1_loaded{b % 2}"], 16)
                sp.dma_start(out_gate[:, b % 2, :], t["mod_rows_d"][2, b].partition_broadcast(P)).then_inc(
                    s[f"og_loaded{b % 2}"], 16)
                if b >= 1:
                    sp.wait_ge(s["out_done"], b * NT)
                    sp.dma_start(out_by_batch[b - 1], acc[:, (b - 1) * NT:b * NT, :]).then_inc(s["out_stored"], 16)
            for half in range(2):
                ts = slice((B - 1) * NT + 2 * half, (B - 1) * NT + 2 * half + 2)
                sp.wait_ge(s["out_done"], (B - 1) * NT + 2 * half + 2)
                sp.dma_start(out_by_batch[B - 1][:, 2 * half:2 * half + 2], acc[:, ts, :]).then_inc(s["out_stored"], 16)
            sp.wait_ge(s["out_stored"], 16 * (B + 1))

        @block.tensor
        def _(pe):
            pe.sem_inc(s["y_psum"], 2 * NT)

            def prepare_up_gate(q):
                for i in range(2 * QB):
                    which, ib = i // QB, i % QB
                    if ib == 0:
                        pe.wait_ge(s[("up_loaded", "gate_loaded")[which]], (q + 1) * 16)
                    pe.wait_ge(s["prep_lo"], q * PREP_SPLIT + i + 1)
                    for kb in range(KB):
                        ins = nc.tensor.transpose(prep_bank[i % 2][:, kb * P:(kb + 1) * P],
                                                  raw[:, which, ib, kb * P:(kb + 1) * P], t["ident"][:])
                    ins.then_inc(s["prep_psum"], 1)

            def prepare_down(q):
                pe.wait_ge(s["down_loaded"], (q + 1) * 16)
                pe.wait_ge(s["prep_lo"], q * PREP_SPLIT + 2 * QB + 1)
                for ib in range(QB):
                    for ht in range(KB):
                        ins = nc.tensor.transpose(prep_bank[0][:, ht * P:(ht + 1) * P],
                                                  raw[:, 0, ht, ib * P:(ib + 1) * P], t["ident"][:])
                    ins.then_inc(s["prep_psum"], 1)
                    pe.wait_ge(s["wdt_done"], q * QB + ib + 1)
                    pe.wait_ge(s["prep_lo"], q * PREP_SPLIT + 2 * QB + ib + 2)
                    nc.tensor.matmul(prep_bank[1][:], t["had"][:], wd_t[:], start=True,
                                     stop=True).then_inc(s["prep_psum"], 1)

            def up_gate(q, b, ib):
                i = q * (B * QB) + b * QB + ib
                pe.wait_ge(s["act_done"], i + 1)
                for which, bk, done in ((1, g_bank, "g_psum"), (0, u_bank, "u_psum")):
                    for kb in range(KB):
                        for n, (w, h) in enumerate(((wug_hi, t["h2_hi"]), (wug_hi, t["h2_lo"]), (wug_lo, t["h2_hi"]))):
                            ins = nc.tensor.matmul(bk[ib % 2][:], w[:, which, kb, ib * P:(ib + 1) * P],
                                                   h[:, kb, b * T:(b + 1) * T], start=kb == 0 and n == 0,
                                                   stop=kb == KB - 1 and n == 2)
                    ins.then_inc(s[done], 1)

            def down(q, b):
                n_ = q * B + b
                pe.wait_ge(s["act_split"], (n_ + 1) * QB + 2)
                for tt in range(NT):
                    ts = slice(tt * P, (tt + 1) * P)
                    pe.wait_ge(s["acc_done"], n_ * NT + tt + 1)
                    for ib in range(QB):
                        for n, (x, w) in enumerate(((act_hi, wd_hi), (act_lo, wd_hi), (act_hi, wd_lo))):
                            ins = nc.tensor.matmul(y_bank[tt % 2][:], x[:, b % 2, ib, ts], w[:, ib, :],
                                                   start=ib == 0 and n == 0, stop=ib == QB - 1 and n == 2)
                    ins.then_inc(s["y_psum"], 1)

            def quarter(q):
                pe.wait_ge(s["prep_lo"], q * PREP_SPLIT + PREP_SPLIT + 2)
                for b in range(B):
                    for ib in range(QB):
                        up_gate(q, b, ib)
                        if ib == 0 and b >= 1:
                            down(q, b - 1)

            prepare_up_gate(0)
            prepare_down(0)
            with pe.Fori(0, NQ - 1) as q:
                quarter(q)
                prepare_up_gate(q + 1)
                down(q, B - 1)
                prepare_down(q + 1)
            quarter(NQ - 1)
            down(NQ - 1, B - 1)

        @block.scalar
        def _(act):
            def prepare_up_gate(q):
                for i in range(2 * QB):
                    which, ib = i // QB, i % QB
                    act.wait_ge(s["prep_psum"], q * PREP_PSUM + i + 1)
                    nc.scalar.activation(wug_hi[:, which, :, ib * P:(ib + 1) * P],
                                         prep_bank[i % 2][:].rearrange("p (k n) -> p k n", k=KB),
                                         ACT.Copy).then_inc(s["prep_hi"], 1)

            def prepare_down(q):
                for ib in range(QB):
                    act.wait_ge(s["prep_psum"], q * PREP_PSUM + 2 * QB + 2 * ib + 1)
                    nc.scalar.activation(wd_t[:], prep_bank[0][:], ACT.Copy).then_inc(s["wdt_done"], 1)
                    act.wait_ge(s["prep_psum"], q * PREP_PSUM + 2 * QB + 2 * ib + 2)
                    nc.scalar.activation(wd_hi[:, ib, :], prep_bank[1][:], ACT.Copy).then_inc(s["prep_hi"], 1)

            def quarter(q):
                for b in range(B):
                    for ib in range(QB):
                        i = q * (B * QB) + b * QB + ib
                        wait_apart(act, s["act_passed"], (s["g_psum"], i + 1), (s["act_split"], i + 1))
                        nc.scalar.activation(act_f[:, ib % 2, :], g_bank[ib % 2][:], ACT.Silu,
                                             scale=fs[:, 1, bass.ds(q * QB + ib, 1)]).then_inc(s["silu_done"], 1)

            prepare_up_gate(0)
            prepare_down(0)
            with act.Fori(0, NQ - 1) as q:
                quarter(q)
                prepare_up_gate(q + 1)
                prepare_down(q + 1)
            quarter(NQ - 1)

        @block.vector
        def _(dve):
            dve.sem_inc(s["prep_lo"], 2)
            dve.sem_inc(s["act_done"], 2)
            dve.sem_inc(s["acc_done"], 2)
            dve.sem_inc(s["act_split"], 2)

            def prepare_up_gate(q):
                for i in range(2 * QB):
                    which, ib = i // QB, i % QB
                    cs = slice(ib * P, (ib + 1) * P)
                    dve.wait_ge(s["prep_hi"], q * PREP_SPLIT + i + 1)
                    nc.vector.tensor_tensor(wug_lo[:, which, :, cs], prep_bank[i % 2][:].rearrange("p (k n) -> p k n", k=KB),
                                            wug_hi[:, which, :, cs].bitcast(F32), ALU.subtract).then_inc(s["prep_lo"], 1)

            def prepare_down(q):
                for ib in range(QB):
                    dve.wait_ge(s["prep_hi"], q * PREP_SPLIT + 2 * QB + ib + 1)
                    nc.vector.tensor_tensor(wd_lo[:, ib, :], prep_bank[1][:], wd_hi[:, ib, :].bitcast(F32),
                                            ALU.subtract).then_inc(s["prep_lo"], 1)

            def activations(q, b, ib):
                i = q * (B * QB) + b * QB + ib
                dve.wait_ge(s["silu_done"], i + 1)
                dve.wait_ge(s["u_psum"], i + 1)
                f = act_f[:, ib % 2, :]
                nc.vector.scalar_tensor_tensor(out=f, in0=u_bank[ib % 2][:], scalar=fs[:, 0, bass.ds(q * QB + ib, 1)],
                                               in1=f, op0=ALU.mult, op1=ALU.mult).then_inc(s["act_done"], 1)
                dve.wait_ge(s["act_done"], i + 3)
                if ib == 0:
                    dve.wait_ge(s["y_psum"], (q * B + b + 1) * NT)
                nc.vector.tensor_copy(act_hi[:, b % 2, ib, :], f).then_inc(s["act_hi_done"], 1)
                dve.wait_ge(s["act_hi_done"], i + 1)
                nc.vector.tensor_tensor(act_lo[:, b % 2, ib, :], f, act_hi[:, b % 2, ib, :].bitcast(F32),
                                        ALU.subtract).then_inc(s["act_split"], 1)

            def accumulate(q, b, last):
                n_ = q * B + b
                if last:
                    dve.wait_ge(s[f"og_loaded{b % 2}"], 16 * (b // 2 + 1))
                for tt in range(NT):
                    i = n_ * NT + tt
                    at = b * NT + tt
                    dve.wait_ge(s["y_psum"], i + 2 * NT + 1)
                    dve.wait_ge(s["acc_done"], i + 1)
                    nc.vector.tensor_tensor(acc[:, at, :], y_bank[tt % 2][:], acc[:, at, :],
                                            ALU.add).then_inc(s["acc_done"], 1)
                    if last:
                        dve.wait_ge(s["acc_done"], i + 3)
                        nc.vector.tensor_tensor(acc[:, at, :], acc[:, at, :], out_gate[:, b % 2, :],
                                                ALU.mult).then_inc(s["out_gated"], 1)
                        dve.wait_ge(s[f"x1_loaded{b % 2}"], 16 * (b // 2 + 1))
                        dve.wait_ge(s["out_gated"], at + 1)
                        nc.vector.tensor_tensor(acc[:, at, :], acc[:, at, :], raw[:, b % 2, tt, :],
                                                ALU.add).then_inc(s["out_done"], 1)

            def quarter(q, last):
                for b in range(B):
                    for ib in range(QB):
                        activations(q, b, ib)
                        if ib == 0 and b >= 1:
                            accumulate(q, b - 1, last)

            prepare_up_gate(0)
            prepare_down(0)
            dve.wait_ge(s["acc_zero"], 1)
            with dve.Fori(0, NQ - 1) as q:
                quarter(q, False)
                prepare_up_gate(q + 1)
                accumulate(q, B - 1, False)
                prepare_down(q + 1)
            quarter(NQ - 1, True)
            accumulate(NQ - 1, B - 1, True)

        @block.gpsimd
        def _(pool):
            nc.gpsimd.memset(acc[:], 0.0).then_inc(s["acc_zero"], 1)


_CONSTANTS = {
    "ident": np.eye(P, dtype=np.float32),
    "had": hadamard(P),
    "qcos": rope_tables(float(HS) ** -0.5)[0],
    "qsin": rope_tables(float(HS) ** -0.5)[1],
    "kcos": rope_tables(1.0)[0],
    "ksin": rope_tables(1.0)[1],
}


def kernel(**inputs):
    import concourse.bacc as _bacc
    from concourse.bass_utils import run_bass_kernel_spmd as _run

    nc = _bacc.Bacc("TRN2", target_bir_lowering=False, num_devices=1)
    arrays, aps = {}, {}
    for name, value in [*inputs.items(), *_CONSTANTS.items()]:
        value = np.ascontiguousarray(value)
        arrays[f"in_{name}"] = value
        aps[name] = nc.dram_tensor(f"in_{name}", value.shape, mybir.dt.from_np(value.dtype), kind="ExternalInput").ap()
    aps["out"] = nc.dram_tensor("out_0", (B, T, H), F32, kind="ExternalOutput").ap()
    build_program(nc, aps)
    return _run(nc, [arrays], core_ids=[0]).results[0]["out_0"]
```

```python
from contextlib import ExitStack

import numpy as np

import concourse.bass as bass
from concourse import mybir

F32 = mybir.dt.float32
F32R = mybir.dt.float32r
ALU = mybir.AluOpType
ACT = mybir.ActivationFunctionType
AX = mybir.AxisListType

P = 128
B = 4
T = 512
H = 512
NT = T // P
KB = H // P
NH = 16
HS = H // NH
HG = P // HS
G = NH // HG
U = HG * NT
INTER = 2048
IB = INTER // P
NE = 8
EB = IB // NE
WEIGHT_STEPS = 4 * EB
EPS = 1e-5
SCORE_SCALE = float(np.float32(HS) ** -0.5)
ROPE_BASE = 10000.0

R_BQ, R_BK, R_BV, R_BO, R_WUG, R_SUU, R_SUD, R_C, R_N = 0, 4, 8, 12, 16, 48, 52, 68, 84


def wait_apart(engine, passed, *waits):
    for semaphore, value in waits:
        engine.wait_ge(semaphore, value)
    engine.sem_inc(passed, 1)


def rope_tables():
    inv = (np.float32(1.0) / np.float32(ROPE_BASE) ** (np.arange(0, HS, 2, dtype=np.float32) / np.float32(HS)))
    ang = np.arange(T, dtype=np.float32)[None, :] * inv.astype(np.float32)[:, None]
    cos, sin = np.cos(ang), np.sin(ang)
    c = np.repeat(cos, 2, axis=0)
    s = np.stack([-sin, sin], axis=1).reshape(HS, T)
    return [np.ascontiguousarray(np.tile(a, (HG, 1))).astype(np.float32) for a in (c, s)]


def hadamard(n):
    h = np.ones((1, 1), np.float32)
    while h.shape[0] < n:
        h = np.block([[h, h], [h, -h]])
    return h.astype(np.float32)


def build_program(nc, a, stop=4):
    ctx = ExitStack()

    def sem(name):
        return ctx.enter_context(nc.semaphore(name))

    def dram(name, shape):
        return nc.dram_tensor(name, shape, F32, kind="Internal").ap()

    with ctx:
        out_gate_d = dram("out_gate_d", (B, H))
        attn_d = dram("attn_d", (B, G, P, T))
        x1_d = dram("x1_d", (B, NT, P, H))
        wd_d = dram("wd_d", (KB, P, INTER))

        def keep(name, shape, dt=F32):
            return ctx.enter_context(nc.sbuf_tensor(name, shape, dt))

        ident = keep("ident", [P, P])
        had = keep("had", [P, P])
        cols = keep("cols", [P, R_N])
        modc = keep("modc", [P, 4, KB, B])
        ffn_scale = keep("ffn_scale", [P, 2, IB])
        neg_half = keep("neg_half", [P, NT])
        bank = [ctx.enter_context(nc.psum_tensor(f"bank{i}", [P, 512], F32)) for i in range(8)]

        pair_w = [keep(f"pair_w_{part}", [P, KB, H], F32R) for part in ("hi", "lo")]
        pair_x = [keep(f"pair_x_{part}", [P, KB, T], F32R) for part in ("hi", "lo")]
        mod_acc = keep("mod_acc", [P, H])
        tile_a = keep("tile_a", [P, 4, H])
        tile_b = keep("tile_b", [P, 4, H])
        stage_attention(nc, a, sem, bank, dict(
            ident=ident, had=had, cols=cols, modc=modc, ffn_scale=ffn_scale, neg_half=neg_half,
            mod_acc=mod_acc, attn_d=attn_d, wd_d=wd_d, out_gate_d=out_gate_d, tile_a=tile_a, tile_b=tile_b,
            pair_w=pair_w, pair_x=pair_x))
        if stop >= 3:
            h2_hi = keep("h2_hi", [P, KB, B * T], F32R)
            h2_lo = keep("h2_lo", [P, KB, B * T], F32R)
            raw_ug = keep("raw_ug", [P, 2, EB, H])
            raw_dn = keep("raw_dn", [P, KB, EB * P])
            wd_t = keep("wd_t", [P, H])
            tensors = dict(
                ident=ident, had=had, cols=cols, modc=modc, neg_half=neg_half, attn_d=attn_d, mod_acc=mod_acc,
                out_gate_d=out_gate_d, x1_d=x1_d, wd_d=wd_d, ffn_scale=ffn_scale, h2_hi=h2_hi, h2_lo=h2_lo,
                tile_a=tile_a, tile_b=tile_b, pair_w=pair_w, pair_x=pair_x, raw_ug=raw_ug, raw_dn=raw_dn,
                wd_t=wd_t, slot0=slice_tiles(keep))
            stage_project(nc, a, sem, bank, tensors)
            if stop >= 4:
                stage_ffn(nc, a, sem, bank, tensors)


def slice_tiles(alloc):
    return [alloc(f"w{kind}0_{part}", shape, F32R)
            for kind, shape in (("ug", [P, 2, KB, EB * P]), ("dn", [P, EB, H])) for part in ("hi", "lo")]


def stage_attention(nc, a, sem, bank, t):
    ctx = ExitStack()
    with ctx:
        def sb(name, shape, dt=F32):
            return ctx.enter_context(nc.sbuf_tensor(name, shape, dt))

        w_hi, w_lo = ([t["pair_w"][part]] + [sb(f"w{n}_{name}", [P, KB, H], F32R) for n in "kv"]
                      for part, name in enumerate(("hi", "lo")))
        rope = [sb(f"rope_{n}", [P, T]) for n in ("cos", "sin")]
        xt = t["tile_a"]
        stats = sb("stats", [P, NT, 6])
        mean_var = sb("mean_var", [P, NT, 2])
        var_eps = sb("var_eps", [P, NT])
        rstd = sb("rstd", [P, NT])
        ht_f = sb("ht_f", [P, 2, T])
        ht_hi, ht_lo = t["pair_x"]
        qk_raw = sb("qk_raw", [P, 2, T])
        qk_swap = sb("qk_swap", [P, T])
        qk_rot = sb("qk_rot", [P, 2, T])
        qk_parts = sb("qk_parts", [P, 4, T], F32R)
        stack = sb("stack", [P, 2, 2, HG, T], F32R)
        v_wide = sb("v_wide", [P, T])
        v_sb = sb("v_sb", [P, 2, NT, P])
        probs = sb("probs", [P, 4, T])
        probs_t = [sb(f"probs_t{pair}", [P, HG, 2 * (pair + 1), 2 * P]) for pair in range(2)]
        neg_max = sb("neg_max", [P, 2, U])
        row_sum = sb("row_sum", [P, 2, U])
        row_inv = sb("row_inv", [P, U])
        inv_wide = sb("inv_wide", [P, NT, HG, HS])
        inv_t = sb("inv_t", [P, T])
        attn_out = sb("attn_out", [P, 2, T])
        rows = sb("rows", [P, P])
        silu_c = sb("silu_c", [P, KB, HS])
        c_wide = sb("c_wide", [P, HS])
        mod_w = t["tile_b"]
        wdn = sb("wdn", [P, 2, INTER])
        mod_w01 = wdn[:].rearrange("p i (k n) -> p (i k) n", n=2 * H)

        s_bank, pt_bank, pr, tr, vo = bank[0:3], bank[3:5], bank[5], bank[6], bank[7]
        NPT, NPB = len(pt_bank), 4
        s_of = [u % 3 for u in range(U - 1)] + [1]
        s_back = [next(d for d in range(1, U) if s_of[(u - d) % U] == s_of[u]) for u in range(U)]
        S_FREE = max(s_back)

        names = ("w_loaded0 w_loaded1 w_loaded2 tables_loaded w_split_hi w_split_lo x_loaded stats_done aggr_done "
                 "vareps_done rstd_done normed pr_done pr_free tr_done tr_free ht_hi_done ht_split swapped "
                 "sin_done cos_done rotated qk_hi_done qk_split sc_done neg_max_done "
                 "exp_done masked pt_psum pt_done av_done vo_free inv_done wide_done attn_stored0 attn_stored1 "
                 "ot_loaded ot_hi_done ot_split wo_loaded wo_hi_done wo_split out_scale_loaded gate_chain gates_ready "
                 "gates_stored ident_loaded rows_loaded scale_rows_loaded mod_loaded had_loaded cols_psum cols_done silu_done c_zero "
                 "mod_psum mod_rows modc_psum modc_done bias_scaled scale_done c_copied mod_added "
                 "wd_loaded wd_stored butterfly act_passed dve_passed pool_passed")
        s = {n: sem("b_" + n) for n in names.split()}
        mod01_loaded = [sem(f"b_mod01_loaded{kb}") for kb in range(KB)]
        stacked = [[sem(f"b_stacked{slot}_{h}") for h in range(HG)] for slot in range(2)]
        block = ctx.enter_context(nc.Block())
        swap_pairs = [j ^ 1 for j in range(32)]
        raw_b = probs_t[1][:].rearrange("p (i h) j n -> p i (h j n)", i=2)
        w_raw = (probs[:], raw_b[:, 0, :].rearrange("p (k n) -> p k n", k=KB),
                 raw_b[:, 1, :].rearrange("p (k n) -> p k n", k=KB))
        last_b = B - 1
        x_by_batch = a["L0_attn_x"].rearrange("b (t p) h -> b p t h", p=P)
        wo_raw = (qk_raw, qk_rot)
        GB = slice(3 * HS, 3 * HS + B)
        gate, gate_size, out_scale = ht_f[:, 0, :], ht_f[:, 1, :], v_wide
        WO_AT, OT_AT, GATES_AT = 2, 6, 11
        wd_rows = a["L0_ffn_W_down"].rearrange("(k p) n -> k p n", p=P)
        mod_rows_by_block = a["L0_wmod"].rearrange("(k p) (i n) -> k p i n", p=P, n=H)[:, :, 2:6, :]
        SENT = 3 * 16

        V_AT, Q_AT, K_AT, PARTS = 0, 8, 12, 3
        V_TURN = U - 1
        TURN, EVAC = 1, 2
        SUMS = (11, 2)
        R_AT = 3
        OUT_AT = SUMS[1] + NT + 1
        LT_GROUP, LT_AT = G - 2, 4
        STATS_AT, NORM_AT = (4, 8, 9, 10), (14, 15, 16, 17)
        MOD_GROUP, MOD_COPY, MOD_AT = G - 1, 4, 8
        FLY_LEVELS, FLY_PIECES = 4, 4
        FLY_AT = range(2, 2 + 3 * FLY_LEVELS * FLY_PIECES, 3)
        ROTATE = OUT_AT + 1

        def on_loop(engine, step, tail):
            for u in range(ROTATE):
                step(0, 0, u, True, False)
            with engine.Fori(0, last_b) as b:
                for g in range(G):
                    for u in range(U):
                        if g or u >= ROTATE:
                            step(b, g, u, False, False)
                for u in range(ROTATE):
                    step(b + 1, 0, u, False, False)
            for g in range(G):
                for u in range(U):
                    if g or u >= ROTATE:
                        step(last_b, g, u, False, True)
            for u in range(ROTATE):
                tail(u)

        def pr_use(kind, m):
            return 3 * m + "qkv".index(kind)

        def tr_use(b, g, kind, last=False, kb=0):
            lt = 0 if last else KB
            off = {"r": 0 + (lt if g > LT_GROUP else 0), "lt": 1 + kb, "mod": 1 + lt,
                   "v": 1 + (lt if g >= LT_GROUP else 0) + (1 if g == MOD_GROUP else 0)}[kind]
            return b * (2 * G + KB + 1) + KB + 2 * g + off

        def v_turned(b, g, last=False):
            if g:
                return tr_use(b, g - 1, "v", last) + 2
            return tr_use(b, 0, "r") + 1

        TR_FINAL = tr_use(last_b, MOD_GROUP, "mod", True) + 1

        def sent(b, g):
            return (b * (G // 2) + g // 2 + 1) * SENT

        def stored_before(b, g):
            return (b * (G // 2) + (g - 1) // 2) * 16 + 1

        @block.sync
        def _(sp):
            sp.sem_inc(s["wd_stored"], 1)
            sp.sem_inc(s["attn_stored0"], 1)
            sp.sem_inc(s["attn_stored1"], 1)
            sp.dma_start(t["ident"][:], a["ident"]).then_inc(s["ident_loaded"], 16)
            sp.dma_start(rows[R_C:R_N, :], a["L0_c"].rearrange("b (k p) -> (b k) p", p=P)).then_inc(s["rows_loaded"], 16)
            for at, name in ((R_BQ, "L0_attn_bq"), (R_BK, "L0_attn_bk"), (R_BV, "L0_attn_bv")):
                sp.dma_start(rows[at:at + KB, :], a[name].rearrange("(r p) -> r p", p=P)).then_inc(s["rows_loaded"], 16)
            for i, table in enumerate(("cos", "sin")):
                sp.dma_start(rope[i][:], a[table]).then_inc(s["tables_loaded"], 16)
            sp.dma_start(t["had"][:], a["had"]).then_inc(s["had_loaded"], 16)

            def send(m, slot, after_scores):
                sp.wait_ge(s["qk_split"], 2 * m + 4)
                if after_scores:
                    sp.wait_ge(s["sc_done"], (m - 1) * U + 1)
                for h in range(HG):
                    hs = slice(h * HS, (h + 1) * HS)
                    for r, parts in enumerate((slice(0, 3, 2), slice(0, 4, 3), slice(1, 3))):
                        sp.dma_start(stack[r * HS:(r + 1) * HS, slot, :, h, :].bitcast(F32),
                                     qk_parts[hs, parts, :].bitcast(F32)).then_inc(stacked[slot][h], 16)

            send(0, 0, False)

            def batch(b, last):
                for g in range(G):
                    if not (last and g == G - 1):
                        send(b * G + g + 1, (g + 1) % 2, True)
                    if g == 0:
                        sp.wait_ge(s["wd_stored"], b * 16 + 1)
                        sp.wait_ge(s["modc_done"], 2)
                        sp.dma_start(wdn[:, 0, :], wd_rows[b]).then_inc(s["wd_loaded"], 16)
                    if g == 0 and not last:
                        sp.wait_ge(s["tr_done"], b * (2 * G + KB + 1) + KB)
                        sp.dma_start(xt[:], x_by_batch[b + 1]).then_inc(s["x_loaded"], 16)
                    if g == MOD_GROUP - 1:
                        sp.wait_ge(s["mod_added"], b + 1)
                        sp.dma_start(mod_w[:], mod_rows_by_block[b]).then_inc(s["mod_loaded"], 16)
                    if g == G - 1:
                        sp.wait_ge(s["butterfly"], (b + 1) * len(FLY_AT))
                        sp.dma_start(t["wd_d"][b], wdn[:, 0, :]).then_inc(s["wd_stored"], 16)
                    if last and g == G - 1:
                        sp.wait_ge(s["gates_ready"], 1)
                        sp.dma_start(t["out_gate_d"], gate[GB, :]).then_inc(s["gates_stored"], 16)
                    sp.wait_ge(s["vo_free"], b * G + g + 2)
                    sp.dma_start(t["attn_d"][b, g], attn_out[:, g % 2, :]).then_inc(s[f"attn_stored{g % 2}"], 16)
                    if last and g == 0:
                        sp.wait_ge(s["tr_done"], b * (2 * G + KB + 1) + KB)
                        sp.dma_start(xt[:], t["attn_d"][0].rearrange("g p t -> p g t")).then_inc(s["ot_loaded"], 16)
                    if last and g == G - 3:
                        sp.wait_ge(s["qk_split"], 2 * B * G + 2)
                        for i in range(2):
                            sp.dma_start(wo_raw[i][:], a["L0_attn_Wo"].rearrange("(i k p) n -> i p k n", k=2, p=P)[i]
                                         ).then_inc(s["wo_loaded"], 16)
                    if last and g == G - 2:
                        sp.wait_ge(s["tr_done"], tr_use(b, g, "v", True) + 1)
                        sp.dma_start(out_scale[GB, :], a["L0_ffn_Wscale_dp"].partition_broadcast(B)).then_inc(
                            s["out_scale_loaded"], 16)

            with sp.Fori(0, last_b) as b:
                batch(b, False)
            batch(last_b, True)
            for i in range(2):
                sp.wait_ge(s[f"attn_stored{i}"], 16 * B * G // 2 + 1)
            sp.wait_ge(s["wd_stored"], KB * 16 + 1)
            sp.wait_ge(s["gates_stored"], 16)
            sp.wait_ge(s["had_loaded"], 16)

        @block.tensor
        def _(pe):
            def project(w, g, part, parts):
                cs = slice(g * P, (g + 1) * P)
                passes = [(kb, wt, ht) for kb in range(KB) for wt, ht in
                          ((w_hi[w], ht_hi), (w_hi[w], ht_lo), (w_lo[w], ht_hi))]
                n = len(passes) // parts
                for i in range(part * n, (part + 1) * n):
                    kb, wt, ht = passes[i]
                    ins = nc.tensor.matmul(pr[:], wt[:, kb, cs], ht[:, kb, :], start=i == 0, stop=i == len(passes) - 1)
                if part == parts - 1:
                    ins.then_inc(s["pr_done"], 1)

            def norm_transposes(kb):
                for tt in range(NT):
                    ins = nc.tensor.transpose(tr[:, tt * P:(tt + 1) * P], xt[:, tt, kb * P:(kb + 1) * P], t["ident"][:])
                ins.then_inc(s["tr_done"], 1)

            def v_transposes():
                for tt in range(NT):
                    ins = nc.tensor.transpose(tr[:, tt * P:(tt + 1) * P], v_wide[:, tt * P:(tt + 1) * P], t["ident"][:])
                ins.then_inc(s["tr_done"], 1)

            def r_transposes():
                for q in range(NT):
                    ins = nc.tensor.transpose(tr[:, q * P:(q + 1) * P],
                                              inv_wide[:, q, :, :].rearrange("p h d -> p (h d)"), t["ident"][:])
                ins.then_inc(s["tr_done"], 1)

            def scores(uu, slot, u, copied):
                pe.wait_ge(s["exp_done"], uu + 1 + S_FREE - s_back[u])
                h, q = u % HG, u // HG
                if q == 0:
                    pe.wait_ge(stacked[slot][h], copied)
                nc.tensor.matmul(s_bank[s_of[u]][:], stack[0:3 * HS, slot, 0, h, q * P:(q + 1) * P],
                                 stack[0:3 * HS, slot, 1, h, :], start=True, stop=True).then_inc(s["sc_done"], 1)

            def sums(m, slot, pair, js):
                if js[0] == 0:
                    if pair == 0:
                        pe.wait_ge(s["vo_free"], m + 1)
                    pe.wait_ge(s["masked"], m * U + 2 * (pair + 1) * HG)
                end = 2 * pair + 1
                for j in js:
                    skip = P if j == end else 0
                    for h in range(HG):
                        hs = slice(h * HS, (h + 1) * HS)
                        ins = nc.tensor.matmul(vo[hs, 2 * pair * P + skip:2 * (pair + 1) * P], v_sb[:, slot, j, hs],
                                               probs_t[pair][:, h, j, skip:2 * P], start=j == 0, stop=j == end)
                if js[-1] == end:
                    ins.then_inc(s["av_done"], 1)

            def probs_transposes(uu, u):
                pe.wait_ge(s["exp_done"], uu + 1 + S_FREE)
                pe.wait_ge(s["pt_done"], uu + 1)
                for j in range(u // HG + 1):
                    ins = nc.tensor.transpose(pt_bank[u % NPT][:, j * P:(j + 1) * P],
                                              probs[:, u % NPB, j * P:(j + 1) * P], t["ident"][:])
                ins.then_inc(s["pt_psum"], 1)

            pe.sem_inc(s["pt_psum"], NPB)
            pe.sem_inc(s["av_done"], 2)
            pe.wait_ge(s["ident_loaded"], 16)
            pe.wait_ge(s["rows_loaded"], 16 * 4)
            pe.wait_ge(s["scale_rows_loaded"], 16 * 4)
            nc.tensor.transpose(s_bank[0][:, 0:R_N], rows[0:R_N, :], t["ident"][0:R_N, 0:R_N]).then_inc(s["cols_psum"], 1)
            pe.wait_ge(s["silu_done"], 1)
            for kb in range(KB):
                pe.wait_ge(mod01_loaded[kb], 16)
                for n in range(2):
                    ins = nc.tensor.matmul(s_bank[1][n * HS:(n + 1) * HS, :], silu_c[:, kb, :],
                                           mod_w01[:, kb, n * H:(n + 1) * H], start=kb == 0, stop=kb == KB - 1)
            ins.then_inc(s["mod_psum"], 1)
            pe.wait_ge(s["mod_rows"], 2)
            for n in range(2):
                for kb in range(KB):
                    rs = slice(n * HS, n * HS + B)
                    ins = nc.tensor.transpose(pt_bank[n][:, kb * B:(kb + 1) * B],
                                              mod_w[rs, 0, kb * P:(kb + 1) * P], t["ident"][rs, rs])
                ins.then_inc(s["modc_psum"], 1)
            pe.wait_ge(s["normed"], 1)
            for kb in range(KB):
                pe.wait_ge(s["tr_free"], kb + 1)
                norm_transposes(kb)
            pe.wait_ge(s["ht_split"], KB + 2)
            for i, (w, g) in enumerate(((0, 0), (1, 0), (2, 0), (0, 1), (1, 1))):
                pe.wait_ge(s["w_split_lo"], w + 1)
                pe.wait_ge(s["pr_free"], i + 1)
                project(w, g, 0, 1)
            pe.wait_ge(s["pr_free"], pr_use("v", 0) + 2)
            pe.wait_ge(s["tr_free"], KB + 1)
            v_transposes()
            scores(0, 0, 0, sent(0, 0))
            scores(1, 0, 1, sent(0, 0))

            def step(b, g, u, first, last):
                m, slot = b * G + g, g % 2
                uu = m * U + u
                if u < U - 2:
                    scores(uu + 2, slot, u + 2, sent(b, g))
                elif not (last and g == G - 1):
                    scores(uu + 2, 1 - slot, u + 2 - U, sent(b, g + 1))
                for w, at, ahead in ((0, Q_AT, 2), (1, K_AT, 2), (2, V_AT, 1)):
                    if at <= u < at + PARTS and not (last and g + ahead >= G):
                        part = u - at
                        if part == 0:
                            pe.wait_ge(s["pr_free"], pr_use("qkv"[w], m + ahead) + 1)
                        if w == 0 and g == LT_GROUP:
                            blocks = ((part + 1) * (3 * KB // PARTS) - 1) // 3 + 1
                            pe.wait_ge(s["ht_split"], (b + 1) * KB + blocks + 2)
                        project(w, (g + ahead) % G, part, PARTS)
                if u >= TURN or not first:
                    probs_transposes(uu - TURN, (u - TURN) % U)
                if SUMS[1] <= u < SUMS[1] + NT and not first:
                    sums(m - 1, 1 - slot, 1, (u - SUMS[1],))
                if u == SUMS[0]:
                    pe.wait_ge(s["tr_free"], v_turned(b, g, last))
                    sums(m, slot, 0, (0, 1))
                if u == R_AT and not first:
                    pe.wait_ge(s["wide_done"], m)
                    pe.wait_ge(s["tr_free"], tr_use(b, g, "r", last) + 1)
                    r_transposes()
                if g == LT_GROUP and not last and LT_AT <= u < LT_AT + KB:
                    kb = u - LT_AT
                    if kb == 0:
                        pe.wait_ge(s["normed"], b + 2)
                    pe.wait_ge(s["tr_free"], tr_use(b, g, "lt", last, kb) + 1)
                    norm_transposes(kb)
                if g == MOD_GROUP and u == MOD_AT:
                    pe.wait_ge(s["mod_loaded"], (b + 1) * 16)
                    pe.wait_ge(s["c_copied"], b + 1)
                    pe.wait_ge(s["tr_free"], tr_use(b, g, "mod", last) + 1)
                    for n in range(4):
                        ins = nc.tensor.matmul(tr[n * HS:(n + 1) * HS, :], c_wide[:], mod_w[:, n, :], start=True, stop=True)
                    ins.then_inc(s["tr_done"], 1)
                if u == V_TURN and not (last and g == G - 1):
                    pe.wait_ge(s["pr_free"], pr_use("v", m + 1) + 2)
                    pe.wait_ge(s["tr_free"], tr_use(b, g, "v", last) + 1)
                    v_transposes()

            def tail(u):
                m = B * G
                if u < TURN:
                    probs_transposes(m * U + u - TURN, (u - TURN) % U)
                if u == SUMS[1]:
                    sums(m - 1, (G - 1) % 2, 1, range(NT))
                if u == R_AT:
                    pe.wait_ge(s["wide_done"], m)
                    pe.wait_ge(s["tr_free"], TR_FINAL + 1)
                    r_transposes()

            on_loop(pe, step, tail)

        @block.scalar
        def _(act):
            act.sem_inc(s["exp_done"], S_FREE)
            act.sem_inc(s["pt_done"], NPT)
            act.sem_inc(s["pr_free"], 1)
            act.sem_inc(s["tr_free"], 1)
            def split_hi(w):
                act.wait_ge(s[f"w_loaded{w}"], 16)
                nc.scalar.activation(w_hi[w][:], w_raw[w], ACT.Copy).then_inc(s["w_split_hi"], 1)

            act.dma_start(xt[:], x_by_batch[0]).then_inc(s["x_loaded"], 16)
            for kb in range(KB):
                act.dma_start(mod_w01[:, kb, :], a["L0_wmod"][kb * P:(kb + 1) * P, 0:2 * H]).then_inc(mod01_loaded[kb], 16)
            for w, name in enumerate(("L0_attn_Wq", "L0_attn_Wk", "L0_attn_Wv")):
                act.dma_start(w_raw[w], a[name].rearrange("(k p) n -> p k n", p=P)).then_inc(s[f"w_loaded{w}"], 16)
            act.wait_ge(s["cols_psum"], 1)
            act.wait_ge(s["c_zero"], 2)
            nc.scalar.activation(silu_c[:, :, 0:B], s_bank[0][:, R_C:R_N].rearrange("p (b k) -> p k b", b=B),
                                 ACT.Silu).then_inc(s["silu_done"], 1)
            split_hi(0)
            act.wait_ge(s["mod_psum"], 1)
            for n in range(2):
                rs = slice(n * HS, n * HS + B)
                nc.scalar.activation(mod_w[rs, 0, :], s_bank[1][rs, :], ACT.Copy).then_inc(s["mod_rows"], 1)

            def evac_norm(b, kb, at):
                wait_apart(act, s["act_passed"], (s["tr_done"], at + 1), (s["ht_split"], b * KB + kb + 1))
                nc.scalar.activation(ht_f[:, kb % 2, :], tr[:], ACT.Identity, bias=t["modc"][:, 0, kb, bass.ds(b, 1)],
                                     scale=t["modc"][:, 1, kb, bass.ds(b, 1)]).then_inc(s["tr_free"], 1)

            def evac_qk(m, which, g):
                act.wait_ge(s["pr_done"], pr_use("qk"[which], m) + 1)
                act.wait_ge(s["qk_split"], 2 * m + which + 1)
                col = (R_BQ, R_BK)[which] + g
                nc.scalar.activation(qk_raw[:, which, :], pr[:], ACT.Identity, bias=t["cols"][:, col:col + 1],
                                     scale=(SCORE_SCALE, 1.0)[which]).then_inc(s["pr_free"], 1)

            def evac_v(m, g):
                act.wait_ge(s["pr_done"], pr_use("v", m) + 1)
                nc.scalar.activation(v_wide[:], pr[:], ACT.Identity,
                                     bias=t["cols"][:, R_BV + g:R_BV + g + 1]).then_inc(s["pr_free"], 1)

            def evac_turned(slot, at):
                act.wait_ge(s["tr_done"], at + 1)
                nc.scalar.activation(v_sb[:, slot, :, :].rearrange("p t n -> p (t n)"), tr[:],
                                     ACT.Copy).then_inc(s["tr_free"], 1)

            def evac_inv(at):
                act.wait_ge(s["tr_done"], at + 1)
                nc.scalar.activation(inv_t[:], tr[:], ACT.Copy).then_inc(s["tr_free"], 1)

            def evac_probs(m, uu, u):
                q, h = u // HG, u % HG
                act.wait_ge(s["pt_psum"], uu + 1 + NPB)
                if u in (0, 2 * HG):
                    act.wait_ge(s["av_done"], 2 * m + q // 2 + 1)
                nc.scalar.activation(probs_t[q // 2][:, h, 0:q + 1, q % 2 * P:(q % 2 + 1) * P],
                                     pt_bank[u % NPT][:, 0:(q + 1) * P].rearrange("p (j n) -> p j n", n=P),
                                     ACT.Copy).then_inc(s["pt_done"], 1)

            act.wait_ge(s["modc_done"], 2)
            for kb in range(KB):
                evac_norm(0, kb, kb)
            split_hi(1)
            split_hi(2)
            act.wait_ge(s["bias_scaled"], 1)
            evac_qk(0, 0, 0)
            evac_qk(0, 1, 0)
            evac_v(0, 0)
            evac_qk(1, 0, 1)
            evac_qk(1, 1, 1)
            evac_turned(0, KB)

            def step(b, g, u, first, last):
                m = b * G + g
                uu = m * U + u
                act.wait_ge(s["neg_max_done"], uu + 1)
                act.wait_ge(s["pt_psum"], uu + 1)
                nc.scalar.activation(probs[:, u % NPB, :], s_bank[s_of[u]][:], ACT.Exp,
                                     bias=neg_max[:, g % 2, u:u + 1],
                                     accum_out=row_sum[:, g % 2, u:u + 1]).then_inc(s["exp_done"], 1)
                if u >= EVAC:
                    evac_probs(m, uu - EVAC, u - EVAC)
                elif not first:
                    evac_probs(m - 1, uu - EVAC, u - EVAC + U)
                for at, which, ahead in ((K_AT + PARTS, 1, 2), (V_AT + PARTS, 2, 1), (Q_AT + PARTS, 0, 2)):
                    if u == at and not (last and g + ahead >= G):
                        if which == 2:
                            evac_v(m + 1, (g + 1) % G)
                        else:
                            evac_qk(m + ahead, which, (g + ahead) % G)
                if last and g == G - 1 and WO_AT <= u < WO_AT + KB:
                    kb = u - WO_AT
                    act.wait_ge(s["wo_loaded"], 32)
                    nc.scalar.activation(w_hi[0][:, kb, :], wo_raw[kb // 2][:, kb % 2, :], ACT.Copy).then_inc(s["wo_hi_done"], 1)
                if last and g == G - 1 and OT_AT <= u < OT_AT + NT:
                    tt = u - OT_AT
                    act.wait_ge(s["ot_loaded"], 16)
                    ts = slice(tt * P, (tt + 1) * P)
                    nc.scalar.activation(ht_hi[:, :, ts], xt[:, :, ts], ACT.Copy).then_inc(s["ot_hi_done"], 1)
                if u == R_AT + 1 and not first:
                    evac_inv(tr_use(b, g, "r", last))
                if g == LT_GROUP and not last and LT_AT < u <= LT_AT + KB:
                    kb = u - LT_AT - 1
                    evac_norm(b + 1, kb, tr_use(b, g, "lt", last, kb))
                if u == 0 and not first:
                    evac_turned(g % 2, v_turned(b, g, last) - 2)

            def tail(u):
                if u < EVAC:
                    evac_probs(B * G - 1, B * G * U + u - EVAC, u - EVAC + U)
                if u == R_AT + 1:
                    evac_inv(TR_FINAL)

            on_loop(act, step, tail)

        @block.vector
        def _(dve):
            dve.sem_inc(s["vo_free"], 1)
            dve.sem_inc(s["ht_split"], 2)
            dve.sem_inc(s["qk_split"], 2)

            def split_lo(w):
                dve.wait_ge(s["w_split_hi"], w + 1)
                nc.vector.tensor_tensor(w_lo[w][:], w_raw[w], w_hi[w][:].bitcast(F32), ALU.subtract).then_inc(s["w_split_lo"], 1)

            def norm_stats(b, tt):
                if tt == 0:
                    dve.wait_ge(s["x_loaded"], (b + 1) * 16)
                nc.vector.bn_stats(stats[:, tt, :], xt[:, tt, :]).then_inc(s["stats_done"], 1)

            def norm_aggregate(b):
                wait_apart(dve, s["dve_passed"], (s["stats_done"], (b + 1) * NT))
                for tt in range(NT):
                    nc.vector.bn_aggr(mean_var[:, tt, :], stats[:, tt, :]).then_inc(s["aggr_done"], 1)
                dve.wait_ge(s["aggr_done"], (b + 1) * NT)
                nc.vector.tensor_scalar(var_eps[:], mean_var[:, :, 1], EPS, None, ALU.add).then_inc(s["vareps_done"], 1)

            def normalize(b, tt):
                if tt == 0:
                    dve.wait_ge(s["rstd_done"], b + 1)
                ins = nc.vector.tensor_scalar(xt[:, tt, :], xt[:, tt, :], mean_var[:, tt, 0:1], rstd[:, tt:tt + 1],
                                              ALU.subtract, ALU.mult)
                if tt == NT - 1:
                    ins.then_inc(s["normed"], 1)

            def split_norm(b, kb, at):
                dve.wait_ge(s["tr_free"], at + 2)
                nc.vector.tensor_copy(ht_hi[:, kb, :], ht_f[:, kb % 2, :]).then_inc(s["ht_hi_done"], 1)
                dve.wait_ge(s["ht_hi_done"], b * KB + kb + 1)
                nc.vector.tensor_tensor(ht_lo[:, kb, :], ht_f[:, kb % 2, :], ht_hi[:, kb, :].bitcast(F32),
                                        ALU.subtract).then_inc(s["ht_split"], 1)

            def rope_swap(m, which):
                waits = [(s["pr_free"], pr_use("qk"[which], m) + 2)]
                if not (isinstance(m, int) and m == 0 and which == 0):
                    waits.append((s["rotated"], 2 * m + which))
                wait_apart(dve, s["dve_passed"], *waits)
                nc.vector.stream_shuffle(qk_swap[:], qk_raw[:, which, :], swap_pairs).then_inc(s["swapped"], 1)

            def rope_sin(m, which):
                dve.wait_ge(s["swapped"], 2 * m + which + 1)
                nc.vector.tensor_tensor(qk_swap[:], qk_swap[:], rope[1][:],
                                        ALU.mult).then_inc(s["sin_done"], 1)

            def rope_hi(m, which, slot, copied):
                dve.wait_ge(s["rotated"], 2 * m + which + 1)
                if copied is not None:
                    for h in range(HG):
                        dve.wait_ge(stacked[slot][h], copied)
                nc.vector.tensor_copy(qk_parts[:, 2 * which, :], qk_rot[:, which, :]).then_inc(s["qk_hi_done"], 1)

            def rope_lo(m, which):
                dve.wait_ge(s["qk_hi_done"], 2 * m + which + 1)
                nc.vector.tensor_tensor(qk_parts[:, 2 * which + 1, :], qk_rot[:, which, :],
                                        qk_parts[:, 2 * which, :].bitcast(F32), ALU.subtract).then_inc(s["qk_split"], 1)

            def inverse(m, slot):
                dve.wait_ge(s["exp_done"], m * U + U + S_FREE)
                nc.vector.reciprocal(row_inv[:], row_sum[:, slot, :]).then_inc(s["inv_done"], 1)
                wait_apart(dve, s["dve_passed"], (s["inv_done"], m + 1))
                nc.vector.tensor_copy(
                    inv_wide[:], row_inv[:].rearrange("p (q h) -> p q h", h=HG).unsqueeze(3)
                    .to_broadcast([P, NT, HG, HS])).then_inc(s["wide_done"], 1)

            def normalize_output(m, slot, stored, at):
                dve.wait_ge(s["tr_free"], at + 2)
                dve.wait_ge(s["av_done"], 2 * m + 4)
                dve.wait_ge(s[f"attn_stored{slot}"], stored)
                nc.vector.tensor_tensor(attn_out[:, slot, :], vo[:], inv_t[:], ALU.mult).then_inc(s["vo_free"], 1)

            nc.vector.memset(t["neg_half"][:], -0.5).then_inc(s["c_zero"], 1)
            nc.vector.memset(silu_c[:], 0.0).then_inc(s["c_zero"], 1)
            nc.vector.memset(t["mod_acc"][:], 0.0).then_inc(s["mod_added"], 1)
            for tt in range(NT):
                norm_stats(0, tt)
            norm_aggregate(0)
            for tt in range(NT):
                normalize(0, tt)
            dve.wait_ge(s["cols_psum"], 1)
            dve.wait_ge(s["silu_done"], 1)
            cols = t["cols"]
            nc.vector.tensor_copy(cols[:], s_bank[0][:, 0:R_N]).then_inc(s["cols_done"], 1)
            dve.wait_ge(s["cols_done"], 1)
            nc.vector.tensor_scalar(cols[:, R_BQ:R_BQ + KB], cols[:, R_BQ:R_BQ + KB], SCORE_SCALE, None,
                                    ALU.mult).then_inc(s["bias_scaled"], 1)
            split_lo(0)
            dve.wait_ge(s["modc_psum"], 2)
            shift, scale = (pt_bank[n][:, 0:KB * B].rearrange("p (k b) -> p k b", k=KB) for n in range(2))
            nc.vector.tensor_copy(t["modc"][:, 0, :, :], shift).then_inc(s["modc_done"], 1)
            nc.vector.tensor_scalar(t["modc"][:, 1, :, :], scale, 1.0, None, ALU.add).then_inc(s["modc_done"], 1)
            for kb in range(KB):
                split_norm(0, kb, kb)
            split_lo(1)
            fs = t["ffn_scale"]
            nc.vector.tensor_scalar(fs[:, :, :], cols[:, R_WUG:R_WUG + 2 * IB].rearrange("p (n i) -> p n i", n=2),
                                    float(H) ** -0.5, None, ALU.mult).then_inc(s["scale_done"], 1)
            dve.wait_ge(s["scale_done"], 1)
            nc.vector.tensor_tensor(fs[:, 0, :], fs[:, 0, :], cols[:, R_SUD:R_SUD + IB], ALU.mult)
            dve.wait_ge(s["tables_loaded"], 16 * 2)
            for which in range(2):
                rope_swap(0, which)
                rope_sin(0, which)
                if which == 0:
                    split_lo(2)
                rope_hi(0, which, 0, None)
                rope_lo(0, which)
            rope_swap(1, 0)
            rope_sin(1, 0)
            rope_hi(1, 0, 0, sent(0, 0))

            def gates(i):
                gb, sign, size = t["mod_acc"][GB, :], gate[GB, :], gate_size[GB, :]
                if i == 0:
                    nc.vector.tensor_scalar(sign, gb, 0.0, 2.0, ALU.is_ge, ALU.mult).then_inc(s["gate_chain"], 1)
                if i == 1:
                    nc.vector.scalar_tensor_tensor(out=size, in0=gb, scalar=-1.0, in1=gb,
                                                   op0=ALU.mult, op1=ALU.max).then_inc(s["gate_chain"], 1)
                if i == 2:
                    dve.wait_ge(s["gate_chain"], 2)
                    nc.vector.tensor_scalar(size, size, 0.25, None, ALU.max).then_inc(s["gate_chain"], 1)
                if i == 3:
                    dve.wait_ge(s["gate_chain"], 3)
                    nc.vector.scalar_tensor_tensor(out=sign, in0=sign, scalar=-1.0, in1=size,
                                                   op0=ALU.add, op1=ALU.mult).then_inc(s["gate_chain"], 1)
                if i == 4:
                    dve.wait_ge(s["gate_chain"], 4)
                    dve.wait_ge(s["out_scale_loaded"], 16)
                    nc.vector.scalar_tensor_tensor(out=sign, in0=sign, scalar=float(INTER) ** -0.5,
                                                   in1=out_scale[GB, :], op0=ALU.mult, op1=ALU.mult).then_inc(
                        s["gates_ready"], 1)

            def step(b, g, u, first, last):
                m = b * G + g
                uu = m * U + u
                dve.wait_ge(s["sc_done"], uu + 1)
                nc.vector.tensor_reduce(neg_max[:, g % 2, u:u + 1], s_bank[s_of[u]][:], AX.X, ALU.max,
                                        negate=True).then_inc(s["neg_max_done"], 1)
                if not (last and g >= G - 2):
                    if u == Q_AT + PARTS + 1:
                        rope_swap(m + 2, 0)
                    if u == Q_AT + PARTS + 2:
                        rope_sin(m + 2, 0)
                    if u == U - 1:
                        rope_hi(m + 2, 0, (g + 1) % 2, sent(b, g + 1))
                if not (last and g == G - 1):
                    if u == 0:
                        rope_lo(m + 1, 0)
                    if u == 2:
                        rope_swap(m + 1, 1)
                    if u == 3:
                        rope_sin(m + 1, 1)
                    if u == 5:
                        rope_hi(m + 1, 1, g % 2, sent(b, g))
                    if u == 6:
                        rope_lo(m + 1, 1)
                if g == MOD_GROUP and u == MOD_COPY:
                    dve.wait_ge(s["mod_added"], b + 1)
                    nc.vector.tensor_copy(c_wide[:], silu_c[:, bass.ds(b, 1), :].rearrange("p k b -> p (k b)")
                                          ).then_inc(s["c_copied"], 1)
                if g == MOD_GROUP and u == MOD_AT + 1:
                    dve.wait_ge(s["tr_done"], tr_use(b, g, "mod", last) + 1)
                    dve.wait_ge(s["mod_added"], b + 1)
                    nc.vector.tensor_tensor(t["mod_acc"][:], tr[:], t["mod_acc"][:], ALU.add).then_inc(s["tr_free"], 1)
                if g == MOD_GROUP and u == MOD_AT + 2:
                    dve.wait_ge(s["tr_free"], tr_use(b, g, "mod", last) + 2)
                    dve.sem_inc(s["mod_added"], 1)
                if u == 1 and not first:
                    inverse(m - 1, 1 - g % 2)
                if last and g == G - 1 and WO_AT < u <= WO_AT + KB:
                    kb = u - WO_AT - 1
                    dve.wait_ge(s["wo_hi_done"], kb + 1)
                    nc.vector.tensor_tensor(w_lo[0][:, kb, :], wo_raw[kb // 2][:, kb % 2, :], w_hi[0][:, kb, :].bitcast(F32),
                                            ALU.subtract).then_inc(s["wo_split"], 1)
                if last and g == G - 1 and OT_AT < u <= OT_AT + NT:
                    tt = u - OT_AT - 1
                    ts = slice(tt * P, (tt + 1) * P)
                    dve.wait_ge(s["ot_hi_done"], tt + 1)
                    nc.vector.tensor_tensor(ht_lo[:, :, ts], xt[:, :, ts], ht_hi[:, :, ts].bitcast(F32),
                                            ALU.subtract).then_inc(s["ot_split"], 1)
                if last and g == G - 1 and GATES_AT <= u:
                    gates(u - GATES_AT)
                if u == OUT_AT and not first:
                    normalize_output(m - 1, 1 - g % 2, stored_before(b, g), tr_use(b, g, "r", last))
                if not last:
                    turn = (g - LT_GROUP + 1) * U + u
                    if turn in STATS_AT:
                        norm_stats(b + 1, STATS_AT.index(turn))
                    if turn == STATS_AT[-1] + 1:
                        norm_aggregate(b + 1)
                    if turn in NORM_AT:
                        normalize(b + 1, NORM_AT.index(turn))
                    if g == LT_GROUP and LT_AT + 1 < u <= LT_AT + 1 + KB:
                        kb = u - LT_AT - 2
                        split_norm(b + 1, kb, tr_use(b, g, "lt", last, kb))

            def tail(u):
                if u == 1:
                    inverse(B * G - 1, (G - 1) % 2)
                if u == OUT_AT:
                    normalize_output(B * G - 1, (G - 1) % 2, stored_before(B, 0), TR_FINAL)

            on_loop(dve, step, tail)

        @block.gpsimd
        def _(pool):
            for at, name in ((R_BO, "L0_attn_bo"), (R_WUG, "L0_ffn_Wscale_ug"), (R_SUU, "L0_ffn_SU_ug"),
                             (R_SUD, "L0_ffn_SU_dp")):
                src = a[name].rearrange("(r p) -> r p", p=P)
                pool.dma_start(rows[at:at + src.shape[0], :], src).then_inc(s["scale_rows_loaded"], 16)
            def power(b):
                pool.wait_ge(s["vareps_done"], b + 1)
                nc.gpsimd.tensor_tensor(rstd[:], var_eps[:], t["neg_half"][:], ALU.pow).then_inc(s["rstd_done"], 1)

            def rope_cos(m, which):
                pool.wait_ge(s["pr_free"], pr_use("qk"[which], m) + 2)
                nc.gpsimd.tensor_tensor(qk_rot[:, which, :], qk_raw[:, which, :], rope[0][:],
                                        ALU.mult).then_inc(s["cos_done"], 1)

            def rope_add(m, which):
                pool.wait_ge(s["sin_done"], 2 * m + which + 1)
                pool.wait_ge(s["cos_done"], 2 * m + which + 1)
                nc.gpsimd.tensor_tensor(qk_rot[:, which, :], qk_rot[:, which, :], qk_swap[:],
                                        ALU.add).then_inc(s["rotated"], 1)

            def mask(uu, u):
                q, h = u // HG, u % HG
                wait_apart(pool, s["pool_passed"], (s["pt_done"], uu + 1 + NPT))
                v = probs_t[q // 2][:, h, q, q % 2 * P:(q % 2 + 1) * P]
                nc.gpsimd.affine_select(out=v, in_=v, compare_op=ALU.is_ge, fill=0.0, base=0,
                                        pattern=[[1, P]], channel_multiplier=-1).then_inc(s["masked"], 1)

            def fly(b, i):
                level, (half, op) = i // FLY_PIECES, divmod(i % FLY_PIECES, 2)
                if level == 0:
                    pool.wait_ge(s["wd_loaded"], (b + 1) * 16)
                else:
                    pool.wait_ge(s["butterfly"], b * len(FLY_AT) + level * FLY_PIECES)
                n = P << level
                v, w = (wdn[:, (level + k) % 2, :].rearrange("p (m a n) -> p m a n", a=2, n=n) for k in range(2))
                m = INTER // (2 * n)
                ms, ns = ((slice(half * m // 2, (half + 1) * m // 2), slice(0, n)) if m > 1
                          else (slice(0, 1), slice(half * n // 2, (half + 1) * n // 2)))
                nc.gpsimd.tensor_tensor(w[:, ms, op, ns], v[:, ms, 0, ns], v[:, ms, 1, ns],
                                        (ALU.add, ALU.subtract)[op]).then_inc(s["butterfly"], 1)

            pool.wait_ge(s["c_zero"], 1)
            power(0)
            pool.wait_ge(s["tables_loaded"], 16 * 2)
            for which in range(2):
                rope_cos(0, which)
                rope_add(0, which)
            rope_cos(1, 0)
            rope_add(1, 0)

            def step(b, g, u, first, last):
                m = b * G + g
                uu = m * U + u
                if u >= EVAC or not first:
                    mask(uu - EVAC, (u - EVAC) % U)
                if not (last and g >= G - 2):
                    if u == Q_AT + PARTS + 1:
                        rope_cos(m + 2, 0)
                    if u == Q_AT + PARTS + 2:
                        rope_add(m + 2, 0)
                if not (last and g == G - 1):
                    if u == 1:
                        rope_cos(m + 1, 1)
                    if u == 3:
                        rope_add(m + 1, 1)
                turn = (g - 1) * U + u
                if turn in FLY_AT:
                    fly(b, FLY_AT.index(turn))
                if not last and g == LT_GROUP - 1 and u == STATS_AT[-1] + 2:
                    power(b + 1)

            def tail(u):
                if u < EVAC:
                    mask(B * G * U + u - EVAC, u - EVAC + U)

            on_loop(pool, step, tail)


def weight_step(nc, t, j, out):
    if j < 2 * EB:
        which, ib = divmod(j, EB)
        for kb in range(KB):
            ins = nc.tensor.transpose(out[:, kb * P:(kb + 1) * P], t["raw_ug"][:, which, ib, kb * P:(kb + 1) * P],
                                      t["ident"][:])
    elif j % 2 == 0:
        ib = j // 2 - EB
        for ht in range(KB):
            ins = nc.tensor.transpose(out[:, ht * P:(ht + 1) * P], t["raw_dn"][:, ht, ib * P:(ib + 1) * P], t["ident"][:])
    else:
        ins = nc.tensor.matmul(out[:], t["had"][:], t["wd_t"][:], start=True, stop=True)
    return ins


def weight_parts(slot, j):
    if j < 2 * EB:
        which, ib = divmod(j, EB)
        return [w[:, which, :, ib * P:(ib + 1) * P] for w in slot[0:2]]
    return [w[:, j // 2 - EB, :] for w in slot[2:4]]


def weight_source(j, out):
    return out[:].rearrange("p (k n) -> p k n", k=KB) if j < 2 * EB else out[:]


def is_turned_down(j):
    return j >= 2 * EB and j % 2 == 0


def slice_rows(a, t):
    return (a["L0_ffn_W_up"].rearrange("(e i p) h -> e p i h", i=EB, p=P),
            a["L0_ffn_W_gate"].rearrange("(e i p) h -> e p i h", i=EB, p=P),
            t["wd_d"].rearrange("k p (e n) -> e p k n", n=EB * P))


def stage_project(nc, a, sem, bank, t):
    ctx = ExitStack()
    with ctx:
        def sb(name, shape, dt=F32):
            return ctx.enter_context(nc.sbuf_tensor(name, shape, dt))

        wo_hi, wo_lo = t["pair_w"]
        ot = (t["tile_a"][:], t["raw_ug"][:].rearrange("p a i n -> p (a i) n"))
        ot_parts = (t["pair_x"], [sb(f"ot_odd_{part}", [P, KB, T], F32R) for part in ("hi", "lo")])
        gate_cols = sb("gate_cols", [P, 3, KB, B])
        gated = sb("gated", [P, 2, T])
        xs = sb("xs", [P, 2, NT, H])
        xn = sb("xn", [P, NT, H])
        stats = sb("stats2", [P, NT, 6])
        mean_var = sb("mean_var2", [P, NT, 2])
        var_eps = sb("var_eps2", [P, NT])
        rstd = sb("rstd2", [P, NT])
        shift = sb("shift2", [P, NT])
        z = sb("z", [P, KB, T])
        z2 = t["tile_b"]
        y_bank, back_bank, t_bank = bank[0:2], bank[2:2 + NT], bank[6:8]
        prep_bank = y_bank

        names = ("ot_loaded0 ot_loaded1 x_loaded0 x_loaded1 ot_hi_done ot_split y_psum gated_done "
                 "back_psum x1_done stats_done aggr_done vareps_done rstd_done shift_done normed tr_psum tr_free "
                 "x1_stored0 x1_stored1 x1_stored2 x1_stored3 fly1 fly2 h_psum hi_done h_free "
                 "modc_psum modc_chain gate_chain ug_loaded dn_loaded prep_psum prep_hi prep_lo wdt_done")
        s = {n: sem("c_" + n) for n in names.split()}
        block = ctx.enter_context(nc.Block())
        GA, SB, CB = (slice(n * HS, n * HS + B) for n in range(3))
        x_by_batch = a["L0_attn_x"].rearrange("b (t p) h -> b p t h", p=P)
        attn_by_batch = t["attn_d"].rearrange("b g p t -> b p g t")
        def flown(b):
            return 2 * b + 2

        def h_bank(b, kb):
            return back_bank[kb] if b >= B - 2 else t_bank[kb % 2]

        modc_bank = (t_bank[0], t_bank[1], back_bank[0])

        @block.sync
        def _(sp):
            up_rows, gate_rows, down_cols = slice_rows(a, t)

            def load_x(b):
                if b >= 2:
                    sp.wait_ge(s["normed"], (b - 1) * NT)
                    for tt in range(NT):
                        sp.wait_ge(s[f"x1_stored{tt}"], (b - 1) * 16)
                sp.dma_start(xs[:, b % 2, :, :], x_by_batch[b]).then_inc(s[f"x_loaded{b % 2}"], 16)

            def load_ot(b):
                if b >= 3:
                    sp.wait_ge(s["ot_split"], (b - 2) * KB)
                sp.dma_start(ot[b % 2], attn_by_batch[b]).then_inc(s[f"ot_loaded{b % 2}"], 16)

            load_ot(1)
            load_x(0)
            load_ot(2)
            load_x(1)
            for b in range(B):
                for tt in range(NT):
                    sp.wait_ge(s["x1_done"], b * NT + tt + 1)
                    sp.dma_start(t["x1_d"][b, tt], xs[:, b % 2, tt, :]).then_inc(s[f"x1_stored{tt}"], 16)
                if b + 3 < B:
                    load_ot(b + 3)
                if b + 2 < B:
                    load_x(b + 2)
                if b == 1:
                    sp.dma_start(t["raw_dn"][:], down_cols[0]).then_inc(s["dn_loaded"], 16)
                    sp.wait_ge(s["ot_split"], (B - 1) * KB)
                    sp.dma_start(t["raw_ug"][:, 0, :, :], up_rows[0]).then_inc(s["ug_loaded"], 16)
                    sp.dma_start(t["raw_ug"][:, 1, :, :], gate_rows[0]).then_inc(s["ug_loaded"], 16)
            for tt in range(NT):
                sp.wait_ge(s[f"x1_stored{tt}"], B * 16)

        @block.tensor
        def _(pe):
            def output(b, f):
                i = b * KB + f
                hi, lo = ot_parts[b % 2]
                fs = slice(f * P, (f + 1) * P)
                if i >= 2:
                    pe.wait_ge(s["gated_done"], i - 1)
                for kb in range(KB):
                    if b and f == 0:
                        pe.wait_ge(s["ot_split"], (b - 1) * KB + kb + 1)
                    for n, (wo_, ot_) in enumerate(((wo_hi, hi), (wo_hi, lo), (wo_lo, hi))):
                        ins = nc.tensor.matmul(y_bank[f % 2][:], wo_[:, kb, fs], ot_[:, kb, :],
                                               start=kb == 0 and n == 0, stop=kb == KB - 1 and n == 2)
                ins.then_inc(s["y_psum"], 1)

            def back(b, f):
                i = b * KB + f
                pe.wait_ge(s["gated_done"], i + 1)
                if f == 0 and b:
                    pe.wait_ge(s["x1_done"], b * NT)
                for tt in range(NT):
                    ins = nc.tensor.transpose(back_bank[tt][:, f * P:(f + 1) * P], gated[:, f % 2, tt * P:(tt + 1) * P],
                                              t["ident"][:])
                ins.then_inc(s["back_psum"], 1)

            def project(b):
                for f in range(KB):
                    output(b, f)
                    if f:
                        back(b, f - 1)

            def transposes(b):
                for kb in range(KB):
                    if kb < 2 and 0 < b < B - 1:
                        pe.wait_ge(s["h_free"], (b - 1) * KB + kb + 3)
                    if kb < 2 and b == B - 1:
                        pe.wait_ge(s["tr_free"], b * KB + kb - 1)
                    if kb >= 2:
                        pe.wait_ge(s["tr_free"], b * KB + kb - 1)
                    for tt in range(NT):
                        if kb == 0:
                            pe.wait_ge(s["normed"], b * NT + tt + 1)
                        ins = nc.tensor.transpose(t_bank[kb % 2][:, tt * P:(tt + 1) * P],
                                                  xn[:, tt, kb * P:(kb + 1) * P], t["ident"][:])
                    ins.then_inc(s["tr_psum"], 1)

            def hadamard_128(b):
                pe.wait_ge(s["fly2"], flown(b))
                if b == B - 2:
                    pe.wait_ge(s["x1_done"], B * NT)
                if b == B - 1:
                    pe.wait_ge(s["h_free"], b * KB)
                for kb in range(KB):
                    if kb >= 2 and b < B - 2:
                        pe.wait_ge(s["h_free"], b * KB + kb - 1)
                    nc.tensor.matmul(h_bank(b, kb)[:], t["had"][:], z[:, kb, :], start=True,
                                     stop=True).then_inc(s["h_psum"], 1)

            def weights(steps):
                for j in steps:
                    if j == 0:
                        pe.wait_ge(s["gated_done"], B * KB)
                        pe.wait_ge(s["ug_loaded"], 32)
                    if j == 2 * EB:
                        pe.wait_ge(s["dn_loaded"], 16)
                    if j >= 2:
                        pe.wait_ge(s["prep_lo"], sum(not is_turned_down(i) for i in range(j - 1)))
                    if j > 2 * EB:
                        pe.wait_ge(s["wdt_done"], sum(is_turned_down(i) for i in range(j)))
                    weight_step(nc, t, j, prep_bank[j % 2]).then_inc(s["prep_psum"], 1)

            output(0, 0)
            for out, rs in zip(modc_bank, (SB, CB, GA)):
                for kb in range(KB):
                    ins = nc.tensor.transpose(out[:, kb * B:(kb + 1) * B], t["mod_acc"][rs, kb * P:(kb + 1) * P],
                                              t["ident"][rs, rs])
                ins.then_inc(s["modc_psum"], 1)
            for f in range(1, KB):
                output(0, f)
                if f == 1:
                    pe.wait_ge(s["modc_chain"], 3)
                back(0, f - 1)
            back(0, KB - 1)
            for b in range(B - 1):
                project(b + 1)
                if b:
                    hadamard_128(b - 1)
                back(b + 1, KB - 1)
                transposes(b)
            weights(range(4))
            hadamard_128(B - 2)
            transposes(B - 1)
            weights(range(4, 6))
            hadamard_128(B - 1)
            weights(range(6, WEIGHT_STEPS))

        @block.scalar
        def _(act):
            def weights(steps):
                for j in steps:
                    act.wait_ge(s["prep_psum"], j + 1)
                    if is_turned_down(j):
                        nc.scalar.activation(t["wd_t"][:], prep_bank[j % 2][:], ACT.Copy).then_inc(s["wdt_done"], 1)
                    else:
                        nc.scalar.activation(weight_parts(t["slot0"], j)[0], weight_source(j, prep_bank[j % 2]),
                                             ACT.Copy).then_inc(s["prep_hi"], 1)

            def split_hi(b):
                act.wait_ge(s[f"ot_loaded{b % 2}"], (b + 1) // 2 * 16)
                if b >= 2:
                    act.wait_ge(s["y_psum"], (b - 1) * KB)
                for kb in range(KB):
                    nc.scalar.activation(ot_parts[b % 2][0][:, kb, :], ot[b % 2][:, kb, :],
                                         ACT.Copy).then_inc(s["ot_hi_done"], 1)

            def apply_gate(b, f):
                i = b * KB + f
                act.wait_ge(s["y_psum"], i + 1)
                if i >= 2:
                    act.wait_ge(s["back_psum"], i - 1)
                nc.scalar.activation(gated[:, f % 2, :], y_bank[f % 2][:], ACT.Identity,
                                     bias=gate_cols[:, 1, f, b:b + 1],
                                     scale=gate_cols[:, 0, f, b:b + 1]).then_inc(s["gated_done"], 1)

            def normalize(b):
                act.wait_ge(s["shift_done"], b + 1)
                if b:
                    act.wait_ge(s["tr_psum"], b * KB)
                for tt in range(NT):
                    nc.scalar.activation(xn[:, tt, :], xs[:, b % 2, tt, :], ACT.Identity, bias=shift[:, tt:tt + 1],
                                         scale=rstd[:, tt:tt + 1]).then_inc(s["normed"], 1)

            def evacuate(b):
                if b:
                    act.wait_ge(s["h_psum"], b * KB)
                for kb in range(KB):
                    act.wait_ge(s["tr_psum"], b * KB + kb + 1)
                    nc.scalar.activation(z[:, kb, :], t_bank[kb % 2][:], ACT.Identity,
                                         bias=t["modc"][:, 2, kb, b:b + 1],
                                         scale=t["modc"][:, 3, kb, b:b + 1]).then_inc(s["tr_free"], 1)

            def transform_hi(b):
                for kb in range(KB):
                    act.wait_ge(s["h_psum"], b * KB + kb + 1)
                    nc.scalar.activation(t["h2_hi"][:, kb, b * T:(b + 1) * T], h_bank(b, kb)[:],
                                         ACT.Copy).then_inc(s["hi_done"], 1)

            act.wait_ge(s["gate_chain"], 6)
            for f in range(KB - 1):
                apply_gate(0, f)
            split_hi(1)
            apply_gate(0, KB - 1)
            act.wait_ge(s["modc_chain"], 3 + 2 * KB)
            for b in range(B - 1):
                apply_gate(b + 1, 0)
                if b + 2 < B:
                    split_hi(b + 2)
                for f in range(1, KB - 1):
                    apply_gate(b + 1, f)
                normalize(b)
                apply_gate(b + 1, KB - 1)
                if b:
                    transform_hi(b - 1)
                evacuate(b)
            weights(range(4))
            normalize(B - 1)
            transform_hi(B - 2)
            evacuate(B - 1)
            weights(range(4, 6))
            transform_hi(B - 1)
            weights(range(6, WEIGHT_STEPS))

        @block.vector
        def _(dve):
            def residual(b):
                dve.wait_ge(s["back_psum"], (b + 1) * KB)
                dve.wait_ge(s[f"x_loaded{b % 2}"], (b // 2 + 1) * 16)
                for tt in range(NT):
                    x = xs[:, b % 2, tt, :]
                    nc.vector.tensor_tensor(x, back_bank[tt][:], x, ALU.add).then_inc(s["x1_done"], 1)

            def statistics(b):
                for tt in range(NT):
                    dve.wait_ge(s["x1_done"], b * NT + tt + 1)
                    nc.vector.bn_stats(stats[:, tt, :], xs[:, b % 2, tt, :]).then_inc(s["stats_done"], 1)
                dve.wait_ge(s["stats_done"], (b + 1) * NT)
                for tt in range(NT):
                    nc.vector.bn_aggr(mean_var[:, tt, :], stats[:, tt, :]).then_inc(s["aggr_done"], 1)
                dve.wait_ge(s["aggr_done"], (b + 1) * NT)
                nc.vector.tensor_scalar(var_eps[:], mean_var[:, :, 1], EPS, None, ALU.add).then_inc(s["vareps_done"], 1)

            def shift_of(b):
                dve.wait_ge(s["rstd_done"], b + 1)
                nc.vector.scalar_tensor_tensor(out=shift[:], in0=mean_var[:, :, 0], scalar=-1.0, in1=rstd[:],
                                               op0=ALU.mult, op1=ALU.mult).then_inc(s["shift_done"], 1)

            def differences_1(b):
                dve.wait_ge(s["tr_free"], (b + 1) * KB)
                v = z[:].rearrange("p (m a) n -> p m a n", a=2)
                w = z2[:].rearrange("p (m a) n -> p m a n", a=2)
                nc.vector.tensor_tensor(w[:, :, 1, :], v[:, :, 0, :], v[:, :, 1, :], ALU.subtract).then_inc(s["fly1"], 1)

            def differences_2(b):
                dve.wait_ge(s["fly1"], flown(b))
                nc.vector.tensor_tensor(z[:, 2:4, :], z2[:, 0:2, :], z2[:, 2:4, :], ALU.subtract).then_inc(s["fly2"], 1)

            def weights(steps):
                for j in steps:
                    if not is_turned_down(j):
                        dve.wait_ge(s["prep_hi"], sum(not is_turned_down(i) for i in range(j + 1)))
                        hi, lo = weight_parts(t["slot0"], j)
                        nc.vector.tensor_tensor(lo, weight_source(j, prep_bank[j % 2]), hi.bitcast(F32),
                                                ALU.subtract).then_inc(s["prep_lo"], 1)

            def transform_lo(b):
                for kb in range(KB):
                    dve.wait_ge(s["hi_done"], b * KB + kb + 1)
                    cs = slice(b * T, (b + 1) * T)
                    nc.vector.tensor_tensor(t["h2_lo"][:, kb, cs], h_bank(b, kb)[:], t["h2_hi"][:, kb, cs].bitcast(F32),
                                            ALU.subtract).then_inc(s["h_free"], 1)

            dve.wait_ge(s["modc_psum"], 3)
            modc = t["modc"]
            to_shift, to_scale, to_gate = (bk[:, 0:KB * B].rearrange("p (k b) -> p k b", k=KB) for bk in modc_bank)
            nc.vector.tensor_copy(gate_cols[:, 0, :, :], to_gate).then_inc(s["modc_chain"], 1)
            nc.vector.tensor_copy(modc[:, 2, :, :], to_shift).then_inc(s["modc_chain"], 1)
            nc.vector.tensor_scalar(modc[:, 3, :, :], to_scale, 1.0, None, ALU.add).then_inc(s["modc_chain"], 1)
            ga, ga_bo, size = (gate_cols[:, i, :, :].rearrange("p k b -> p (k b)") for i in range(3))
            dve.wait_ge(s["modc_chain"], 3)
            nc.vector.scalar_tensor_tensor(out=size, in0=ga, scalar=-1.0, in1=ga, op0=ALU.mult,
                                           op1=ALU.max).then_inc(s["gate_chain"], 1)
            dve.wait_ge(s["gate_chain"], 1)
            nc.vector.tensor_scalar(size, size, 0.25, None, ALU.max).then_inc(s["gate_chain"], 1)
            nc.vector.tensor_scalar(ga, ga, 0.0, 2.0, ALU.is_ge, ALU.mult).then_inc(s["gate_chain"], 1)
            dve.wait_ge(s["gate_chain"], 3)
            nc.vector.scalar_tensor_tensor(out=ga, in0=ga, scalar=-1.0, in1=size, op0=ALU.add,
                                           op1=ALU.mult).then_inc(s["gate_chain"], 1)
            dve.wait_ge(s["gate_chain"], 4)
            bo = t["cols"][:, R_BO:R_BO + KB].unsqueeze(2).to_broadcast([P, KB, B])
            nc.vector.tensor_tensor(gate_cols[:, 1, :, :], gate_cols[:, 0, :, :], bo, ALU.mult).then_inc(s["gate_chain"], 2)
            for n in (2, 3):
                for kb in range(KB):
                    nc.vector.tensor_scalar(modc[:, n, kb, :], modc[:, n, kb, :], t["cols"][:, R_SUU + kb:R_SUU + kb + 1],
                                            None, ALU.mult).then_inc(s["modc_chain"], 1)
            residual(0)
            statistics(0)
            shift_of(0)
            for b in range(B - 1):
                if b:
                    transform_lo(b - 1)
                residual(b + 1)
                if b == B - 2:
                    weights(range(2))
                differences_1(b)
                statistics(b + 1)
                differences_2(b)
                shift_of(b + 1)
            weights(range(2, 4))
            transform_lo(B - 2)
            differences_1(B - 1)
            differences_2(B - 1)
            weights(range(4, 6))
            transform_lo(B - 1)
            weights(range(6, WEIGHT_STEPS))

        @block.gpsimd
        def _(pool):
            def split_lo(b):
                for kb in range(KB):
                    pool.wait_ge(s["ot_hi_done"], (b - 1) * KB + kb + 1)
                    hi, lo = ot_parts[b % 2]
                    nc.gpsimd.tensor_tensor(lo[:, kb, :], ot[b % 2][:, kb, :], hi[:, kb, :].bitcast(F32),
                                            ALU.subtract).then_inc(s["ot_split"], 1)

            def power(b):
                pool.wait_ge(s["vareps_done"], b + 1)
                if b:
                    pool.wait_ge(s["normed"], b * NT)
                nc.gpsimd.tensor_tensor(rstd[:], var_eps[:], t["neg_half"][:], ALU.pow).then_inc(s["rstd_done"], 1)

            def sums_1(b):
                pool.wait_ge(s["tr_free"], (b + 1) * KB)
                v = z[:].rearrange("p (m a) n -> p m a n", a=2)
                w = z2[:].rearrange("p (m a) n -> p m a n", a=2)
                nc.gpsimd.tensor_tensor(w[:, :, 0, :], v[:, :, 0, :], v[:, :, 1, :], ALU.add).then_inc(s["fly1"], 1)

            def sums_2(b):
                pool.wait_ge(s["fly1"], flown(b))
                nc.gpsimd.tensor_tensor(z[:, 0:2, :], z2[:, 0:2, :], z2[:, 2:4, :], ALU.add).then_inc(s["fly2"], 1)

            split_lo(1)
            power(0)
            split_lo(2)
            for b in range(B - 1):
                sums_1(b)
                sums_2(b)
                power(b + 1)
                if b + 3 < B:
                    split_lo(b + 3)
            sums_1(B - 1)
            sums_2(B - 1)


def stage_ffn(nc, a, sem, bank, t):
    ctx = ExitStack()
    with ctx:
        def sb(name, shape, dt=F32):
            return ctx.enter_context(nc.sbuf_tensor(name, shape, dt))

        slots = [t["slot0"], [w[:].rearrange("p a n -> p (a n)").rearrange("p (w k n) -> p w k n", w=2, k=KB)
                              for w in t["pair_w"]] + [sb(f"wdn1_{part}", [P, EB, H], F32R) for part in ("hi", "lo")]]
        act_f = sb("act_f", [P, 2, T])
        act_hi, act_lo = (x[:].rearrange("p (a i) t -> p a i t", a=2) for x in t["pair_x"])
        acc = sb("acc", [P, B * NT, H])
        out_gate = sb("out_gate", [P, 2, H])
        x1 = (t["tile_a"], t["tile_b"])
        g_bank, u_bank, y_bank, prep_bank = bank[0:2], bank[2:4], bank[4:6], bank[6:8]

        names = ("ug_loaded dn_loaded prep_psum prep_hi prep_lo wdt_done g_psum u_psum silu_done "
                 "act_done act_hi_done act_split y_psum acc_done acc_zero og_loaded0 og_loaded1 x1_loaded0 x1_loaded1 "
                 "out_gated out_done out_stored act_passed")
        s = {n: sem("d_" + n) for n in names.split()}
        block = ctx.enter_context(nc.Block())
        STEPS = 2 * B * EB
        PAIRS = NE // 2
        SPLITS = sum(not is_turned_down(j) for j in range(WEIGHT_STEPS))
        TURNS = WEIGHT_STEPS - SPLITS
        fs = t["ffn_scale"]
        x1_by_batch = t["x1_d"].rearrange("b t p h -> b p t h")
        out_by_batch = a["out"].rearrange("b (t p) h -> b p t h", p=P)

        def on_loop(engine, step, tail):
            step(0, 0, True, False)
            with engine.Fori(0, PAIRS - 1) as pair:
                for w in range(1, STEPS):
                    step(pair, w, False, False)
                step(pair + 1, 0, False, False)
            for w in range(1, STEPS):
                step(PAIRS - 1, w, False, True)
            tail()

        @block.sync
        def _(sp):
            up_rows, gate_rows, down_cols = slice_rows(a, t)

            def load(e):
                sp.dma_start(t["raw_ug"][:, 0, :, :], up_rows[e]).then_inc(s["ug_loaded"], 16)
                sp.dma_start(t["raw_ug"][:, 1, :, :], gate_rows[e]).then_inc(s["ug_loaded"], 16)

            load(1)
            sp.dma_start(t["raw_dn"][:], down_cols[1]).then_inc(s["dn_loaded"], 16)
            for b in range(2):
                sp.dma_start(x1[b][:], x1_by_batch[b]).then_inc(s[f"x1_loaded{b}"], 16)
                sp.dma_start(out_gate[:, b, :], t["out_gate_d"][b].partition_broadcast(P)).then_inc(s[f"og_loaded{b}"], 16)
            with sp.Fori(2, NE) as e:
                sp.wait_ge(s["prep_psum"], e * WEIGHT_STEPS - 2 * WEIGHT_STEPS + 2 * EB)
                load(e)
                sp.wait_ge(s["prep_psum"], e * WEIGHT_STEPS - WEIGHT_STEPS - 1)
                sp.dma_start(t["raw_dn"][:], down_cols[e]).then_inc(s["dn_loaded"], 16)
            for b in range(1, B):
                sp.wait_ge(s["out_done"], b * NT)
                sp.dma_start(out_by_batch[b - 1], acc[:, (b - 1) * NT:b * NT, :]).then_inc(s["out_stored"], 16)
                if b + 1 < B:
                    sp.dma_start(x1[(b + 1) % 2][:], x1_by_batch[b + 1]).then_inc(s[f"x1_loaded{(b + 1) % 2}"], 16)
                    sp.dma_start(out_gate[:, (b + 1) % 2, :], t["out_gate_d"][b + 1].partition_broadcast(P)).then_inc(
                        s[f"og_loaded{(b + 1) % 2}"], 16)
            for tt in range(NT):
                at = (B - 1) * NT + tt
                sp.wait_ge(s["out_done"], at + 1)
                sp.dma_start(out_by_batch[B - 1][:, tt, :], acc[:, at, :]).then_inc(s["out_stored"], 16)
            sp.wait_ge(s["out_stored"], 16 * (B - 1 + NT))

        @block.tensor
        def _(pe):
            pe.sem_inc(s["y_psum"], 2 * NT)

            def up_gate(i, slot, b, ib):
                hi, lo = slot[0:2]
                pe.wait_ge(s["act_done"], i + 1)
                for which, bk, done in ((1, g_bank, "g_psum"), (0, u_bank, "u_psum")):
                    for kb in range(KB):
                        for n, (w, h) in enumerate(((hi, t["h2_hi"]), (hi, t["h2_lo"]), (lo, t["h2_hi"]))):
                            ins = nc.tensor.matmul(bk[ib % 2][:], w[:, which, kb, ib * P:(ib + 1) * P],
                                                   h[:, kb, b * T:(b + 1) * T], start=kb == 0 and n == 0,
                                                   stop=kb == KB - 1 and n == 2)
                    ins.then_inc(s[done], 1)

            def down(n_, slot, half):
                hi, lo = slot[2:4]
                pe.wait_ge(s["act_split"], n_ * EB + EB + 2)
                for tt in range(NT):
                    ts = slice(tt * P, (tt + 1) * P)
                    pe.wait_ge(s["acc_done"], n_ * NT + tt + 1)
                    for ib in range(EB):
                        for n, (x, w) in enumerate(((act_hi, hi), (act_lo, hi), (act_hi, lo))):
                            ins = nc.tensor.matmul(y_bank[tt % 2][:], x[:, half, ib, ts], w[:, ib, :],
                                                   start=ib == 0 and n == 0, stop=ib == EB - 1 and n == 2)
                    ins.then_inc(s["y_psum"], 1)

            def step(pair, w, first, last):
                odd, j = divmod(w, B * EB)
                b, ib = divmod(j, EB)
                e = pair * 2 + odd
                if j == 0 and not first:
                    pe.wait_ge(s["prep_lo"], (e - 1) * SPLITS + 2 * EB + 1)
                up_gate(pair * STEPS + w, slots[odd], b, ib)
                if not (last and odd):
                    if j == 0:
                        pe.wait_ge(s["ug_loaded"], 32 * e + 32)
                    if j == 2 * EB:
                        pe.wait_ge(s["dn_loaded"], 16 * e + 16)
                    if j:
                        pe.wait_ge(s["prep_lo"], e * SPLITS + 1 + sum(not is_turned_down(i) for i in range(j - 1)))
                    if j > 2 * EB:
                        pe.wait_ge(s["wdt_done"], e * TURNS + sum(is_turned_down(i) for i in range(j)))
                    weight_step(nc, t, j, prep_bank[j % 2]).then_inc(s["prep_psum"], 1)
                if ib == 0 and not first:
                    n_ = pair * 2 * B + w // EB
                    before = (w // EB - 1) % (2 * B)
                    if b == 1:
                        pe.wait_ge(s["prep_lo"], e * SPLITS + 1)
                    down(n_ - 1, slots[before // B], before % 2)

            def tail():
                down(NE * B - 1, slots[1], (B - 1) % 2)

            on_loop(pe, step, tail)

        @block.scalar
        def _(act):
            def step(pair, w, first, last):
                odd, j = divmod(w, B * EB)
                ib = j % EB
                i = pair * STEPS + w
                e = pair * 2 + odd
                wait_apart(act, s["act_passed"], (s["g_psum"], i + 1), (s["act_split"], i + 1))
                nc.scalar.activation(act_f[:, ib % 2, :], g_bank[ib % 2][:], ACT.Silu,
                                     scale=fs[:, 1, bass.ds(e * EB + ib, 1)]).then_inc(s["silu_done"], 1)
                if not (last and odd):
                    act.wait_ge(s["prep_psum"], e * WEIGHT_STEPS + j + 1)
                    if is_turned_down(j):
                        nc.scalar.activation(t["wd_t"][:], prep_bank[j % 2][:], ACT.Copy).then_inc(s["wdt_done"], 1)
                    else:
                        nc.scalar.activation(weight_parts(slots[1 - odd], j)[0], weight_source(j, prep_bank[j % 2]),
                                             ACT.Copy).then_inc(s["prep_hi"], 1)

            on_loop(act, step, lambda: None)

        @block.vector
        def _(dve):
            dve.sem_inc(s["prep_lo"], 1)
            dve.sem_inc(s["act_done"], 2)
            dve.sem_inc(s["acc_done"], 2)
            dve.sem_inc(s["act_split"], 2)

            def activations(i, e, n_, half, ib):
                dve.wait_ge(s["silu_done"], i + 1)
                dve.wait_ge(s["u_psum"], i + 1)
                f = act_f[:, ib % 2, :]
                nc.vector.scalar_tensor_tensor(out=f, in0=u_bank[ib % 2][:], scalar=fs[:, 0, bass.ds(e * EB + ib, 1)],
                                               in1=f, op0=ALU.mult, op1=ALU.mult).then_inc(s["act_done"], 1)
                dve.wait_ge(s["act_done"], i + 3)
                if ib == 0:
                    dve.wait_ge(s["y_psum"], (n_ + 1) * NT)
                nc.vector.tensor_copy(act_hi[:, half, ib, :], f).then_inc(s["act_hi_done"], 1)
                dve.wait_ge(s["act_hi_done"], i + 1)
                nc.vector.tensor_tensor(act_lo[:, half, ib, :], f, act_hi[:, half, ib, :].bitcast(F32),
                                        ALU.subtract).then_inc(s["act_split"], 1)

            def accumulate(n_, b, last):
                dve.wait_ge(s["acc_zero"], 1)
                if last:
                    dve.wait_ge(s[f"og_loaded{b % 2}"], 16 * (b // 2 + 1))
                for tt in range(NT):
                    i = n_ * NT + tt
                    at = b * NT + tt
                    dve.wait_ge(s["y_psum"], i + 2 * NT + 1)
                    dve.wait_ge(s["acc_done"], i + 1)
                    nc.vector.tensor_tensor(acc[:, at, :], y_bank[tt % 2][:], acc[:, at, :],
                                            ALU.add).then_inc(s["acc_done"], 1)
                    if last:
                        dve.wait_ge(s["acc_done"], i + 3)
                        nc.vector.tensor_tensor(acc[:, at, :], acc[:, at, :], out_gate[:, b % 2, :],
                                                ALU.mult).then_inc(s["out_gated"], 1)
                        dve.wait_ge(s[f"x1_loaded{b % 2}"], 16 * (b // 2 + 1))
                        dve.wait_ge(s["out_gated"], at + 1)
                        nc.vector.tensor_tensor(acc[:, at, :], acc[:, at, :], x1[b % 2][:, tt, :],
                                                ALU.add).then_inc(s["out_done"], 1)

            def step(pair, w, first, last):
                odd, j = divmod(w, B * EB)
                b, ib = divmod(j, EB)
                e = pair * 2 + odd
                n_ = pair * 2 * B + w // EB
                activations(pair * STEPS + w, e, n_, b % 2, ib)
                if ib == 0 and not first:
                    accumulate(n_ - 1, (b - 1) % B, last and w > B * EB)
                if not (last and odd) and not is_turned_down(j):
                    dve.wait_ge(s["prep_hi"], e * SPLITS + sum(not is_turned_down(i) for i in range(j + 1)))
                    hi, lo = weight_parts(slots[1 - odd], j)
                    nc.vector.tensor_tensor(lo, weight_source(j, prep_bank[j % 2]), hi.bitcast(F32),
                                            ALU.subtract).then_inc(s["prep_lo"], 1)

            on_loop(dve, step, lambda: accumulate(NE * B - 1, B - 1, True))

        @block.gpsimd
        def _(pool):
            nc.gpsimd.memset(acc[:], 0.0).then_inc(s["acc_zero"], 1)


_CONSTANTS = {
    "ident": np.eye(P, dtype=np.float32),
    "had": hadamard(P),
    "cos": rope_tables()[0],
    "sin": rope_tables()[1],
}


def kernel(**inputs):
    import concourse.bacc as _bacc
    from concourse.bass_utils import run_bass_kernel_spmd as _run

    nc = _bacc.Bacc("TRN2", target_bir_lowering=False, num_devices=1)
    arrays, aps = {}, {}
    for name, value in [*inputs.items(), *_CONSTANTS.items()]:
        value = np.ascontiguousarray(value)
        arrays[f"in_{name}"] = value
        aps[name] = nc.dram_tensor(f"in_{name}", value.shape, mybir.dt.from_np(value.dtype), kind="ExternalInput").ap()
    aps["out"] = nc.dram_tensor("out_0", (B, T, H), F32, kind="ExternalOutput").ap()
    build_program(nc, aps)
    return _run(nc, [arrays], core_ids=[0]).results[0]["out_0"]
```
